# Optimizing a Trainium2 kernel written in Bass

```python
import numpy as np
import jax
import jax.numpy as jnp

def _softmax(x, axis=-1):
    return jax.nn.softmax(x, axis=axis)

def _gelu(x):
    return jax.nn.gelu(x, approximate=True)

def _silu(x):
    return jax.nn.silu(x)

def _sigmoid(x):
    return jax.nn.sigmoid(x)

def _layernorm(x, axis=-1, eps=1e-05):
    m = jnp.mean(x, axis=axis, keepdims=True)
    v = jnp.var(x, axis=axis, keepdims=True)
    return (x - m) / jnp.sqrt(v + eps)

def _scatter_add(tgt, idx, src, axis=0):
    return tgt.at[idx].add(src)

def _segment_sum(src, seg, n):
    return jax.ops.segment_sum(src, seg, n)
kernel_name = 'mk_flamingo_gated_d2_seqx_r4_141849'

def setup_inputs(seed: int=0):
    np.random.seed(seed)
    _w = jnp.asarray

    def _rec_inputs():
        import jax
        import jax.numpy as jnp
        _rk = jax.random.key(seed)
        x = -0.0002928 + 1 * jax.random.normal(jax.random.fold_in(_rk, 1), (8, 112, 256), jnp.float32)
        _lenS = 112 - jax.random.randint(jax.random.fold_in(_rk, 7), (8,), 0, max(1, 112 // 4) + 1, jnp.int32)
        _lenS2 = 375 - jax.random.randint(jax.random.fold_in(_rk, 8), (8,), 0, max(1, 375 // 4) + 1, jnp.int32)
        _ctx_2048P = jax.random.normal(jax.random.fold_in(_rk, 11), (8, 16, 512), jnp.float32)
        _ctx_2048c = jax.random.dirichlet(jax.random.fold_in(_rk, 511), 0.3 * jnp.ones((16,), jnp.float32), (8, 375))
        _ctx_2048t = jnp.einsum('bsk,bkd->bsd', _ctx_2048c, _ctx_2048P)
        _ctx_2048t = _ctx_2048t * jax.lax.rsqrt(jnp.mean(jnp.square(_ctx_2048t)) + 1e-12) * 0.953939
        ctx_2048 = -0.000514642 + 1.00011 * (_ctx_2048t + 0.3 * jax.random.normal(jax.random.fold_in(_rk, 611), (8, 375, 512), jnp.float32))
        _validS = jnp.arange(112)[None, :] < _lenS[:, None]
        _validS2 = jnp.arange(375)[None, :] < _lenS2[:, None]
        _causal = jnp.tril(jnp.ones((112, 112), dtype=bool))
        mask_BxS2_if0 = jnp.where(jnp.ones((8, 375), dtype=bool), 4, 0).astype(jnp.int32)
        _g = jax.random.normal(jax.random.fold_in(_rk, 9001), (2, 2), jnp.float32)
        _g = jnp.sign(_g) * jnp.maximum(jnp.abs(_g), 1.0) + (_g == 0) * 1.0
        g_xattn = _g[0]
        g_ffn = _g[1]
        return (x, ctx_2048, mask_BxS2_if0, g_xattn, g_ffn)
    x, ctx_2048, mask_BxS2_if0, g_xattn, g_ffn = _rec_inputs()

    def _L0_xattn_setup():
        import jax, jax.numpy as jnp
        import numpy as np
        NUM_HEADS = 16
        key = jax.random.key(seed)
        ks = jax.random.split(key, 5)
        dim = 256
        B, N, N_c = (4, 256, 64)
        x = jax.random.normal(ks[0], (B, N, dim), dtype=jnp.float32)
        context = jax.random.normal(ks[1], (B, N_c, 2 * dim), dtype=jnp.float32)
        w_qkv = jax.random.normal(ks[2], (3 * dim, dim), dtype=jnp.float32) * 0.02
        w_proj = jax.random.normal(ks[3], (dim, dim), dtype=jnp.float32) * 0.02
        b_proj = jax.random.normal(ks[4], (dim,), dtype=jnp.float32) * 0.02
        return {'x': x, 'context': context, 'w_qkv': w_qkv, 'w_proj': w_proj, 'b_proj': b_proj}
    _L0_xattn_all = _L0_xattn_setup()
    _L0_xattn_in = {k: v for k, v in _L0_xattn_all.items() if k in ('w_qkv', 'w_proj', 'b_proj')}
    del _L0_xattn_all

    def _L0_ffn_setup():
        import jax, jax.numpy as jnp
        import numpy as np
        B, S, D, H, E, K = (2, 256, 256, 128, 16, 4)
        HS = 2 * H

        def silu(z):
            return z * jax.nn.sigmoid(z)
        key = jax.random.key(seed)
        ks = jax.random.split(key, 8)
        sc = lambda fan_in: 1.0 / np.sqrt(fan_in)
        x = jax.random.normal(ks[0], (B, S, D), jnp.float32)
        gate_w = jax.random.normal(ks[1], (E, D), jnp.float32) * sc(D)
        ws_in = jax.random.normal(ks[2], (D, HS), jnp.float32) * sc(D)
        vs_in = jax.random.normal(ks[3], (D, HS), jnp.float32) * sc(D)
        ws_out = jax.random.normal(ks[4], (HS, D), jnp.float32) * sc(HS)
        e_win = jax.random.normal(ks[5], (E, D, H), jnp.float32) * sc(D)
        e_vin = jax.random.normal(ks[6], (E, D, H), jnp.float32) * sc(D)
        e_wout = jax.random.normal(ks[7], (E, H, D), jnp.float32) * sc(H)
        return {'x': x, 'gate_w': gate_w, 'ws_in': ws_in, 'vs_in': vs_in, 'ws_out': ws_out, 'e_win': e_win, 'e_vin': e_vin, 'e_wout': e_wout}
    _L0_ffn_all = _L0_ffn_setup()
    _L0_ffn_in = {k: v for k, v in _L0_ffn_all.items() if k in ('gate_w', 'ws_in', 'vs_in', 'ws_out', 'e_win', 'e_vin', 'e_wout')}
    del _L0_ffn_all

    def _L1_xattn_setup():
        import jax, jax.numpy as jnp
        import numpy as np
        B, L, P = (4, 1024, 256)
        D_MODEL = 256
        D_GLOBAL = 512
        HEADDIM = 32
        EPSILON = 0.001
        RMS_EPS = 1e-05

        def rmsnorm(x, g, eps=RMS_EPS):
            var = jnp.mean(jnp.square(x), axis=-1, keepdims=True)
            return x * jax.lax.rsqrt(var + eps) * g

        def _hnet_depool(h, h_patch_full, patch_lens):
            h_patch = h_patch_full[..., :D_MODEL]
            bsz, plen = (h_patch.shape[0], h_patch.shape[1])
            seqlen = h.shape[1]
            logp = jnp.full((bsz, plen), -EPSILON, dtype=jnp.float32)
            bidx = jnp.cumsum(patch_lens, axis=1) - 1
            boundary_mask = jnp.zeros((bsz, seqlen), dtype=jnp.int32)
            boundary_mask = boundary_mask.at[jnp.arange(bsz)[:, None], bidx].set(1)
            dt = (-jnp.log(-jnp.expm1(logp))).astype(h_patch.dtype)
            x = h_patch / dt[..., None]
            n_heads = D_MODEL // HEADDIM
            A = -jnp.ones((n_heads,), dtype=jnp.float32)
            bcoef = jnp.exp(logp).astype(h_patch.dtype)
            x4 = x.reshape(bsz, plen, n_heads, HEADDIM)
            a = jnp.exp(dt[:, :, None] * A[None, None, :])
            u = (dt * bcoef)[:, :, None, None] * x4
            a_b = jnp.broadcast_to(a[..., None], u.shape)

            def comb(lft, rgt):
                aL, uL = lft
                aR, uR = rgt
                return (aL * aR, uL * aR + uR)
            _, s = jax.lax.associative_scan(comb, (a_b, u), axis=1)
            depool = s.reshape(bsz, plen, D_MODEL)
            plug = jnp.clip(jnp.cumsum(boundary_mask, axis=1) - 1, 0, plen - 1)
            depool_out = depool[jnp.arange(bsz)[:, None], plug]
            return depool_out + h
        key = jax.random.key(seed)
        k1, k2, k3, k4 = jax.random.split(key, 4)
        embeds = jax.random.normal(k1, (B, L, D_MODEL), dtype=jnp.float32)
        patch_embeds = jax.random.normal(k2, (B, P, D_GLOBAL), dtype=jnp.float32)
        patch_lens = jnp.full((B, P), L // P, dtype=jnp.int64)
        W_in = jax.random.normal(k3, (D_MODEL, D_MODEL), dtype=jnp.float32) * 0.02
        b_in = jnp.zeros((D_MODEL,), dtype=jnp.float32)
        g_res = jnp.ones((D_MODEL,), dtype=jnp.float32)
        g_init = jnp.ones((D_GLOBAL,), dtype=jnp.float32)
        return {'embeds': embeds, 'patch_embeds': patch_embeds, 'patch_lens': patch_lens, 'W_in': W_in, 'b_in': b_in, 'g_res': g_res, 'g_init': g_init}
    _L1_xattn_all = _L1_xattn_setup()
    _L1_xattn_in = {k: v for k, v in _L1_xattn_all.items() if k in ('W_in', 'b_in', 'g_res', 'g_init')}
    del _L1_xattn_all

    def _L1_ffn_setup():
        import jax, jax.numpy as jnp
        import numpy as np
        QB = 127.0
        EPS = 1e-05

        def _ste(x, q):
            return x + jax.lax.stop_gradient(q - x)

        def bitlinear(x, W, b):
            w_scale = jnp.clip(jnp.mean(jnp.abs(W)), EPS, None)
            Wq = _ste(W, jnp.clip(jnp.round(W / w_scale), -1.0, 1.0) * w_scale)
            x_scale = jnp.clip(jnp.max(jnp.abs(x), axis=-1, keepdims=True), EPS, None)
            xq = _ste(x, jnp.clip(jnp.round(x * (QB / x_scale)), -QB - 1.0, QB) * (x_scale / QB))
            return jnp.einsum('bnd,hd->bnh', xq, Wq) + b
        key = jax.random.key(seed)
        k0, k1, k2 = jax.random.split(key, 3)
        B, N, D = (8, 1024, 256)
        H = int(D * 4.0)
        x = jax.random.normal(k0, (B, N, D), dtype=jnp.float32)
        W1 = jax.random.normal(k1, (H, D), dtype=jnp.float32) * 0.02
        b1 = jnp.zeros((H,), dtype=jnp.float32)
        W2 = jax.random.normal(k2, (D, H), dtype=jnp.float32) * 0.02
        b2 = jnp.zeros((D,), dtype=jnp.float32)
        return {'x': x, 'W1': W1, 'b1': b1, 'W2': W2, 'b2': b2}
    _L1_ffn_all = _L1_ffn_setup()
    _L1_ffn_in = {k: v for k, v in _L1_ffn_all.items() if k in ('W1', 'b1', 'W2', 'b2')}
    del _L1_ffn_all
    return {'x': x, 'ctx_2048': ctx_2048, 'mask_BxS2_if0': mask_BxS2_if0, 'g_xattn': g_xattn, 'g_ffn': g_ffn, 'L0_xattn_w_qkv': _L0_xattn_in['w_qkv'], 'L0_xattn_w_proj': _L0_xattn_in['w_proj'], 'L0_xattn_b_proj': _L0_xattn_in['b_proj'], 'L0_ffn_gate_w': _L0_ffn_in['gate_w'], 'L0_ffn_ws_in': _L0_ffn_in['ws_in'], 'L0_ffn_vs_in': _L0_ffn_in['vs_in'], 'L0_ffn_ws_out': _L0_ffn_in['ws_out'], 'L0_ffn_e_win': _L0_ffn_in['e_win'], 'L0_ffn_e_vin': _L0_ffn_in['e_vin'], 'L0_ffn_e_wout': _L0_ffn_in['e_wout'], 'L1_xattn_W_in': _L1_xattn_in['W_in'], 'L1_xattn_b_in': _L1_xattn_in['b_in'], 'L1_xattn_g_res': _L1_xattn_in['g_res'], 'L1_xattn_g_init': _L1_xattn_in['g_init'], 'L1_ffn_W1': _L1_ffn_in['W1'], 'L1_ffn_b1': _L1_ffn_in['b1'], 'L1_ffn_W2': _L1_ffn_in['W2'], 'L1_ffn_b2': _L1_ffn_in['b2']}

def reference(x, ctx_2048, mask_BxS2_if0, g_xattn, g_ffn, L0_xattn_w_qkv, L0_xattn_w_proj, L0_xattn_b_proj, L0_ffn_gate_w, L0_ffn_ws_in, L0_ffn_vs_in, L0_ffn_ws_out, L0_ffn_e_win, L0_ffn_e_vin, L0_ffn_e_wout, L1_xattn_W_in, L1_xattn_b_in, L1_xattn_g_res, L1_xattn_g_init, L1_ffn_W1, L1_ffn_b1, L1_ffn_W2, L1_ffn_b2):
    import jax
    import jax.numpy as jnp

    def _L0_xattn_ref(x, context, w_qkv, w_proj, b_proj):
        import jax, jax.numpy as jnp
        import numpy as np
        NUM_HEADS = 16
        B, N, C = x.shape
        H = NUM_HEADS
        D = C // H
        scale = D ** (-0.5)
        qkv = (x @ w_qkv.T).reshape(B, N, 3, H, D).transpose(2, 0, 3, 1, 4)
        q, k, v = (qkv[0], qkv[1], qkv[2])
        N_c = context.shape[1]
        kv = context.reshape(B, N_c, 2, H, D).transpose(2, 0, 3, 1, 4)
        extra_k, extra_v = (kv[0], kv[1])
        k = jnp.concatenate([extra_k, k], axis=2)
        v = jnp.concatenate([extra_v, v], axis=2)
        dtype = q.dtype
        attn = jnp.einsum('bhnd,bhmd->bhnm', q * scale, k).astype(jnp.float32)
        attn = jax.nn.softmax(attn, axis=-1).astype(dtype)
        out = jnp.einsum('bhnm,bhmd->bhnd', attn, v)
        out = out.transpose(0, 2, 1, 3).reshape(B, N, C)
        return out @ w_proj.T + b_proj

    def _L0_ffn_ref(x, gate_w, ws_in, vs_in, ws_out, e_win, e_vin, e_wout):
        import jax, jax.numpy as jnp
        import numpy as np
        B, S, D, H, E, K = (2, 256, 256, 128, 16, 4)
        HS = 2 * H

        def silu(z):
            return z * jax.nn.sigmoid(z)
        b, s, d = x.shape
        T = b * s
        xf = x.reshape(T, d)
        g = jax.nn.sigmoid(xf @ gate_w.T)
        topv, topi = jax.lax.top_k(g, K)
        wn = topv / jnp.sum(topv, axis=-1, keepdims=True)
        combine = jnp.zeros_like(g).at[jnp.arange(T)[:, None], topi].add(wn)
        hin = jnp.einsum('td,edh->eth', xf, e_win)
        vin = jnp.einsum('td,edh->eth', xf, e_vin)
        h = silu(hin) * vin * combine.T[:, :, None]
        routed = jnp.einsum('eth,ehd->td', h, e_wout)
        shared = silu(xf @ ws_in) * (xf @ vs_in) @ ws_out
        return (shared + routed).reshape(b, s, d)

    def _L1_xattn_ref(embeds, patch_embeds, patch_lens, W_in, b_in, g_res, g_init):
        import jax, jax.numpy as jnp
        import numpy as np
        B, L, P = (4, 1024, 256)
        D_MODEL = 256
        D_GLOBAL = 512
        HEADDIM = 32
        EPSILON = 0.001
        RMS_EPS = 1e-05

        def rmsnorm(x, g, eps=RMS_EPS):
            var = jnp.mean(jnp.square(x), axis=-1, keepdims=True)
            return x * jax.lax.rsqrt(var + eps) * g

        def _hnet_depool(h, h_patch_full, patch_lens):
            h_patch = h_patch_full[..., :D_MODEL]
            bsz, plen = (h_patch.shape[0], h_patch.shape[1])
            seqlen = h.shape[1]
            logp = jnp.full((bsz, plen), -EPSILON, dtype=jnp.float32)
            bidx = jnp.cumsum(patch_lens, axis=1) - 1
            boundary_mask = jnp.zeros((bsz, seqlen), dtype=jnp.int32)
            boundary_mask = boundary_mask.at[jnp.arange(bsz)[:, None], bidx].set(1)
            dt = (-jnp.log(-jnp.expm1(logp))).astype(h_patch.dtype)
            x = h_patch / dt[..., None]
            n_heads = D_MODEL // HEADDIM
            A = -jnp.ones((n_heads,), dtype=jnp.float32)
            bcoef = jnp.exp(logp).astype(h_patch.dtype)
            x4 = x.reshape(bsz, plen, n_heads, HEADDIM)
            a = jnp.exp(dt[:, :, None] * A[None, None, :])
            u = (dt * bcoef)[:, :, None, None] * x4
            a_b = jnp.broadcast_to(a[..., None], u.shape)

            def comb(lft, rgt):
                aL, uL = lft
                aR, uR = rgt
                return (aL * aR, uL * aR + uR)
            _, s = jax.lax.associative_scan(comb, (a_b, u), axis=1)
            depool = s.reshape(bsz, plen, D_MODEL)
            plug = jnp.clip(jnp.cumsum(boundary_mask, axis=1) - 1, 0, plen - 1)
            depool_out = depool[jnp.arange(bsz)[:, None], plug]
            return depool_out + h
        h = rmsnorm(embeds, g_res)
        h = jnp.einsum('bld,ed->ble', h, W_in) + b_in
        h_patch = rmsnorm(patch_embeds, g_init)
        return _hnet_depool(h, h_patch, patch_lens)

    def _L1_ffn_ref(x, W1, b1, W2, b2):
        import jax, jax.numpy as jnp
        import numpy as np
        QB = 127.0
        EPS = 1e-05

        def _ste(x, q):
            return x + jax.lax.stop_gradient(q - x)

        def bitlinear(x, W, b):
            w_scale = jnp.clip(jnp.mean(jnp.abs(W)), EPS, None)
            Wq = _ste(W, jnp.clip(jnp.round(W / w_scale), -1.0, 1.0) * w_scale)
            x_scale = jnp.clip(jnp.max(jnp.abs(x), axis=-1, keepdims=True), EPS, None)
            xq = _ste(x, jnp.clip(jnp.round(x * (QB / x_scale)), -QB - 1.0, QB) * (x_scale / QB))
            return jnp.einsum('bnd,hd->bnh', xq, Wq) + b
        h = bitlinear(x, W1, b1)
        h = jax.nn.gelu(h, approximate=False)
        return bitlinear(h, W2, b2)
    x = x + jnp.tanh(g_xattn[0]) * _L0_xattn_ref(_layernorm(x, axis=-1), ctx_2048, L0_xattn_w_qkv, L0_xattn_w_proj, L0_xattn_b_proj)
    x = x + jnp.tanh(g_ffn[0]) * _L0_ffn_ref(_layernorm(x, axis=-1), L0_ffn_gate_w, L0_ffn_ws_in, L0_ffn_vs_in, L0_ffn_ws_out, L0_ffn_e_win, L0_ffn_e_vin, L0_ffn_e_wout)
    x = x + jnp.tanh(g_xattn[1]) * _L1_xattn_ref(_layernorm(x, axis=-1), ctx_2048, mask_BxS2_if0, L1_xattn_W_in, L1_xattn_b_in, L1_xattn_g_res, L1_xattn_g_init)
    x = x + jnp.tanh(g_ffn[1]) * _L1_ffn_ref(_layernorm(x, axis=-1), L1_ffn_W1, L1_ffn_b1, L1_ffn_W2, L1_ffn_b2)
    return x

_drawn_inputs = setup_inputs


def setup_inputs(seed=0):
    import zlib

    import numpy as np

    out = dict(_drawn_inputs(seed))
    spreads = {'g_ffn': (-1.0, 0.6),
     'L1_xattn_b_in': (0.0, 0.1),
     'L1_xattn_g_res': (1.0, 0.2),
     'L1_xattn_g_init': (1.0, 0.2),
     'L1_ffn_b1': (0.0, 0.698),
     'L1_ffn_b2': (0.0, 0.1)}
    factors = {'L0_xattn_w_qkv': 3.543, 'L0_xattn_b_proj': 2.836}
    for name, (base, spread) in spreads.items():
        noise = np.random.default_rng([zlib.crc32(name.encode()), seed]).standard_normal(out[name].shape)
        drawn = base * np.exp(spread * noise) if base else spread * noise
        out[name] = jnp.asarray(drawn.astype(out[name].dtype))
    for name, factor in factors.items():
        out[name] = (out[name] * factor).astype(out[name].dtype)
    return out
```

```python
import math
from contextlib import ExitStack

import concourse.bass as bass
import concourse.mybir as mybir

F32 = mybir.dt.float32
BF16 = mybir.dt.bfloat16
I32 = mybir.dt.int32
ALU = mybir.AluOpType
ACT = mybir.ActivationFunctionType
AX = mybir.AxisListType

B, T, D = 8, 112, 256
S, DC = 375, 512
NH, DH = 16, 16
KEYS = S + T
CH, NCH = 125, 3
KPAD = CH * (NCH + 1)
HALF, HT = 2, 4
W = HT * T
NE, TOPK, HID = 16, 4, 128
NU = NE + 2
H4 = 4 * D
RB = 6 * DH
Q_PART = (0, 0, 1, 0, 2, 1)
K_PART = (0, 1, 0, 2, 0, 1)
LN_EPS = 1e-5
LOGP = -0.001
DT = -math.log(-math.expm1(LOGP))
BCOEF = math.exp(LOGP)
QB, Q_EPS = 127.0, 1e-5
MAGIC = 1.5 * 2.0 ** 23


def flamingo(nc, x, ctx_in, patch_lens, g_xattn, g_ffn, w_qkv, w_proj, b_proj, gate_w, ws_in, vs_in,
             ws_out, e_win, e_vin, e_wout, w_in, b_in, g_res, g_init, w1, b1, w2, b2, out):
    kscr = nc.dram_tensor("k_parts", (3, D, B, KEYS), BF16, kind="Internal").ap()
    qscr = nc.dram_tensor("q_parts", (3, D, B * T), BF16, kind="Internal").ap()
    cscr = nc.dram_tensor("combine_rows", (NE, B * T), F32, kind="Internal").ap()

    with ExitStack() as stack:
        def sb(name, shape, dt=F32):
            return stack.enter_context(nc.sbuf_tensor(name, shape, dt))

        def sem(name):
            return stack.enter_context(nc.semaphore(name))

        PS = stack.enter_context(nc.psum_tensor("banks", [128, 8, 512], F32))

        def bank(i):
            return PS[:, i, :]


        ident = sb("ident", [128, 128])
        identb = sb("identb", [128, 128], BF16)
        ones = sb("ones", [128, 128])
        onesb = sb("onesb", [128, 128], BF16)
        tri = sb("tri", [128, 128])
        before = sb("before", [128, NE, NE])
        mhalf = sb("mhalf", [128, HT])
        pidx = sb("pidx", [128, 1])
        iota_t = sb("iota_t", [128, T])
        xs = sb("xs", [128, B, D])
        xn = sb("xn", [128, HT, D])
        xnT = sb("xnT", [128, 2, B * T])
        wT = sb("wT", [128, 2, 4 * D])
        winT = sb("winT", [128, 2, D])
        gateT = sb("gateT", [128, 2, NE])
        gates = sb("gates", [128, 4])
        tg = sb("tg", [128, 4])
        gres = sb("gres", [128, 2])
        gbp = sb("gbp", [128, D])
        gbin = sb("gbin", [128, D])
        gb2 = sb("gb2", [128, D])
        gib = sb("gib", [128, D])
        b1_b = sb("b1_b", [128, H4])
        stats = sb("stats", [128, 2, HT, 6])
        mv = sb("mv", [128, 2, HT, 2])
        rs = sb("rs", [128, 2, 4, HT])
        ssq = sb("ssq", [128, B])
        rsc = sb("rsc", [128, 2, B])
        u = sb("u", [128, B, D])
        w2T = sb("w2T", [128, 8, D], BF16)
        ring = sb("ring", [128, 4, 6 * HID])
        kst = sb("kst", [128, 3, NH, KPAD], BF16)
        qst = sb("qst", [128, NH, B * T], BF16)
        ctxs = sb("ctxs", [128, 3, NCH, DC])
        vst = sb("vst", [128, 2, NCH + 1, NH, 32])
        ex = sb("ex", [128, 4, W])
        comp = sb("comp", [128, 2, 3, 2 * S], BF16)
        r1 = sb("r1", [128, 2, 2 * S])
        nm = sb("nm", [128, 2, NH])
        mrow = sb("mrow", [128, 2, 2, T], BF16)
        osb = sb("osb", [128, W])
        rinv = sb("rinv", [128, NH])
        asb = sb("asb", [128, NH, DH])
        attT = sb("attT", [128, 2 * T])
        gth = sb("gth", [128, HT, NE])
        gsg = sb("gsg", [128, HT, NE])
        gsum = sb("gsum", [128, 2, HT])
        cTs = sb("cTs", [NE, W])
        msk = sb("msk", [128, NCH * B], I32)
        sqj = sb("sqj", [128, DC], BF16)
        magic = sb("magic", [128, 1])
        mskf = sb("mskf", [128, NCH * B])
        idx = sb("idx", [128, 2, NCH * B])
        wabs = sb("wabs", [128, 2])
        wsc = sb("wsc", [128, 5, 2])
        lc = sb("lc", [128, HT, 24])

        later_q = qst[:, :, :].rearrange("p h t -> p (h t)").bitcast(F32)
        later_k = kst[:, :, :, :].rearrange("p s h t -> p (s h t)").bitcast(F32)
        later_v = vst[:, :, :, :, :].rearrange("p a c h d -> p (a c h d)")

        def cut(region, at, n):
            return region[:, at:at + n]

        silu_sb = [cut(later_q, i * W, W) for i in range(2)]
        t_sb = [cut(later_q, (2 + i) * W, W) for i in range(2)]
        h_sb = [cut(later_q, (4 + i) * W, W) for i in range(2)]
        cb = [cut(later_q, (6 + i) * W, W) for i in range(4)]
        w1s = cut(later_k, 0, 8 * D)
        w2s = cut(later_k, 2048, 2 * H4)
        junk = cut(later_k, 4096, 2048)
        tq1 = cut(later_k, 6144, 1024).bitcast(BF16)
        tq2 = cut(later_k, 7168, 1024).bitcast(BF16)
        eqm = cut(later_k, 8192, 1344).bitcast(BF16)
        bm = cut(later_k, 9536, B * T)
        keep = cut(later_k, 10432, B * T)
        h1 = [cut(later_k, i * H4, H4) for i in range(HT)]
        hq = [cut(later_k, 4096 + 512 * i, 512).bitcast(BF16) for i in range(HT)]
        hqT = [cut(later_k, 6144 + 448 * i, 448).bitcast(BF16) for i in range(HT)]
        wdep = cut(later_v, 0, B * T)
        w1T = cut(later_v, 3072, H4).bitcast(BF16).rearrange("p (k c) -> p k c", k=2)
        xh = [cut(later_v, 1024 + i * D, D) for i in range(HT)]
        xhT = [cut(later_v, 2048 + i * 2 * T, 2 * T) for i in range(HT)]
        qf = xh
        xq = [cut(later_q, 10 * W + 128 * i, 128).bitcast(BF16) for i in range(HT)]
        xqT = [cut(later_q, 10 * W + 512 + 112 * i, 112).bitcast(BF16) for i in range(HT)]
        ranks = cut(ctxs[:, :, :, :].rearrange("p a k d -> p (a k d)"), 0, 2 * HT * NE * NE)

        in_x, in_wq, in_wp, in_small, in_mask, in_w12 = (
            sem("in_x"), sem("in_wq"), sem("in_wp"), sem("in_small"), sem("in_mask"), sem("in_w12"))
        in_ctx = [sem(f"in_ctx{i}") for i in range(3)]
        in_kst = [sem(f"in_kst{i}") for i in range(3)]
        in_qst = [sem(f"in_qst{i}") for i in range(2)]
        in_ring = [sem(f"in_ring{i}") for i in range(4)]
        in_cb = [sem(f"in_cb{i}") for i in range(4)]
        parts_out = [sem(f"parts_out{i}") for i in range(2)]
        in_mrow, cscr_out, y_out = sem("in_mrow"), sem("cscr_out"), sem("y_out")
        names = ("const ones_pad tanh_g gbp_s gb_s wt_pe wt_act wt_dve ln_stats ln_rs ln_x xnt_pe xnt_act xnt_dve "
                 "qk_pe sp_hi sp_r1 sp_lo ct_pe v_pad v_pe v_own sq_act rs_pool u_dve xb_pool "
                 "a_pe max_dve mt_pe m_hi m_lo b_pe exp_act av_pe o_act nt_pe as_dve at_pe att_act pj_pe x1_dve "
                 "hin_pe vin_pe silu_act t_dve h_dve out_pe x2_dve gt_pe th_act cmb_dve cT_pe cT_act "
                 "abs_act ws_pe ws_dve tq_dve w1t_pe w12_act w12_dve m_dve cs_pe eq_dve cnt_pe keep_pool dd_dve e_act wdep_dve "
                 "l_st l_rs l_xh l_xg xht_pe xht_act win_pe x3_dve m_st m_rs xq_dve xqt_pe xqt_act w1_pe h1_dve gelu_act "
                 "s2_dve magic_dve hr_act hq_dve hqt_pe hqt_act w2_pe l_xg2 y_dve step_dve step_pool step_act").split()
        s = {n: sem(n) for n in names}

        SPLITS = ([("qk", i) for i in range(4)] + [("ctx", 0), ("ctx", 1), ("ctx", 2)]
                  + [("qk", 4 + i) for i in range(4)] + [("ctx", c) for c in range(3, B)])
        SP_AT = {k: n for n, k in enumerate(SPLITS)}

        def parts_written(n):
            return parts_out[n % 2], 48 * (n // 2 + 1)

        def l_bank(stage, t):
            if t < HT:
                return {"xh": 6, "win": 7, "xq": 6, "w1": 6, "hq": 7, "w2": 7}[stage]
            j = t - HT
            return {"xh": j, "win": 4 + j, "xq": j, "w1": (4, 6, 0, 2)[j], "hq": 4 + j, "w2": j}[stage]

        def l_slot(e, stage):
            at = {"xh": 0, "win": 1, "xq": 2, "w1": 3, "gelu": 4, "hq": 5, "w2": 6, "pre": -1}[stage]
            t, r = divmod(e - 2 - at, 3)
            return t if r == 0 and 0 <= t < HT else None

        block = stack.enter_context(nc.Block())

        @block.sync
        def _(sp):
            sp.dma_start(xs[0:T, :, :], x.rearrange("b t c -> t b c")).then_inc(in_x, 16)
            wq_st = ring[:, 0:2, :].rearrange("p a c -> p (a c)").rearrange("p (i c) -> p i c", c=D)
            sp.dma_start(wq_st, w_qkv.rearrange("(i p) c -> p i c", p=128)).then_inc(in_wq, 16)

            def load_ctx(c):
                if c >= 3:
                    sp.wait_ge(s["ct_pe"], c - 2)
                    sp.wait_ge(s["v_pad"], c - 2)
                    sp.wait_ge(s["u_dve"], c - 2)
                sp.dma_start(ctxs[0:CH, c % 3, :, :],
                             ctx_in[c].rearrange("(k p) d -> p k d", p=CH)).then_inc(in_ctx[c % 3], 16)

            def write_parts(n):
                kind, i = SPLITS[n]
                sp.wait_ge(s["sp_lo"], n + 1)
                sem_, _ = parts_written(n)
                if kind == "ctx":
                    for a in range(3):
                        src = comp[:, n % 2, a, :].rearrange("p (g t) -> p g t", g=2)
                        dst = kscr[a, :, i, 0:S].rearrange("(g r) t -> r g t", r=128)
                        sp.dma_start(dst, src).then_inc(sem_, 16)
                    return
                h, m = divmod(i, 4)
                for a in range(3):
                    src = comp[:, n % 2, a, 0:W]
                    if m < 2:
                        dst = qscr[a, m * 128:(m + 1) * 128, h * W:(h + 1) * W]
                        sp.dma_start(dst, src).then_inc(sem_, 16)
                    else:
                        dst = kscr[a, (m - 2) * 128:(m - 1) * 128, h * HT:(h + 1) * HT, S:KEYS]
                        sp.dma_start(dst, src.rearrange("p (b t) -> p b t", b=HT)).then_inc(sem_, 16)

            def read_k(c):
                for n in [SP_AT[("ctx", c)]] + [SP_AT[("qk", 4 * (c // HT) + i)] for i in (2, 3)]:
                    sp.wait_ge(*parts_written(n))
                if c >= 3:
                    sp.wait_ge(s["exp_act"], NH * (c - 2))
                for j, part in enumerate(K_PART):
                    sp.dma_start(kst[j * DH:(j + 1) * DH, c % 3, :, 0:KEYS],
                                 kscr[part, :, c, :].rearrange("(h r) t -> r h t", r=DH)).then_inc(in_kst[c % 3], 16)

            def read_q(h):
                for i in (0, 1):
                    sp.wait_ge(*parts_written(SP_AT[("qk", 4 * h + i)]))
                for j, part in enumerate(Q_PART):
                    sp.dma_start(qst[j * DH:(j + 1) * DH, :, h * W:(h + 1) * W],
                                 qscr[part, :, h * W:(h + 1) * W].rearrange("(h r) t -> r h t", r=DH))\
                        .then_inc(in_qst[h], 16)

            def write_max(b):
                sp.wait_ge(s["m_lo"], b + 1)
                for j in range(2):
                    sp.dma_start(qst[RB + j:RB + j + 1, :, b * T:(b + 1) * T],
                                 mrow[0:NH, b % 2, j, :]).then_inc(in_mrow, 16)

            for c in range(3):
                load_ctx(c)
            for n in range(4):
                write_parts(n)
            read_q(0)
            write_parts(4)
            read_k(0)
            for c in (1, 2):
                write_parts(4 + c)
                read_k(c)
            for n in range(7, 11):
                write_parts(n)
            load_ctx(3)
            read_q(1)
            write_max(0)
            for b in range(B):
                if b + 1 < B:
                    write_max(b + 1)
                if b + 3 < B:
                    write_parts(SP_AT[("ctx", b + 3)])
                if b + 4 < B:
                    load_ctx(b + 4)
                if b + 3 < B:
                    read_k(b + 3)

            def load_ring(i):
                e = i % NU
                r = ring[:, i % 4, :]
                if i >= 4:
                    sp.wait_ge(s["out_pe"], i - 3)
                else:
                    sp.wait_ge(s["wt_act"], 4)
                    sp.wait_ge(s["wt_dve"], 3)
                if e < 2:
                    cols = slice(e * HID, (e + 1) * HID)
                    wi, vi, wo = ws_in[:, cols], vs_in[:, cols], ws_out[e * HID:(e + 1) * HID, :]
                else:
                    wi, vi, wo = e_win[e - 2], e_vin[e - 2], e_wout[e - 2]
                for k, w_ in ((0, wi), (1, vi)):
                    sp.dma_start(r[:, k * 2 * HID:(k + 1) * 2 * HID].rearrange("p (k h) -> p k h", k=2),
                                 w_.rearrange("(k p) h -> p k h", p=128)).then_inc(in_ring[i % 4], 16)
                sp.dma_start(r[:, 4 * HID:6 * HID], wo).then_inc(in_ring[i % 4], 16)

            for i in range(4):
                load_ring(i)
            sp.wait_ge(s["exp_act"], NH * B)
            for h in range(HALF):
                sp.wait_ge(s["cT_act"], h + 1)
                sp.dma_start(cscr[:, h * W:(h + 1) * W], cTs[:, :]).then_inc(cscr_out, 16)
                sp.wait_ge(cscr_out, 16 * (h + 1))
                for e in range(NU):
                    i = h * NU + e
                    if e >= 2:
                        j = h * NE + e - 2
                        if j >= 4:
                            sp.wait_ge(s["h_dve"], j - 3)
                        sp.dma_start(cb[j % 4], cscr[e - 2:e - 1, h * W:(h + 1) * W].broadcast_to([128, W]))\
                            .then_inc(in_cb[j % 4], 16)
                    if i >= 4 - 2 and i + 2 < HALF * NU and i + 2 >= 4:
                        load_ring(i + 2)
                    if i == 1:
                        sp.dma_start(w1s.rearrange("p (i c) -> p i c", i=8),
                                     w1.rearrange("(i p) c -> p i c", p=128)).then_inc(in_w12, 16)
                        sp.dma_start(w2s.rearrange("p (i c) -> p i c", i=2),
                                     w2.rearrange("(i p) c -> p i c", p=128)).then_inc(in_w12, 16)
            for t in range(B):
                sp.wait_ge(s["y_dve"], t + 1)
                sp.dma_start(out[t], xs[0:T, t, :]).then_inc(y_out, 16)
            sp.wait_ge(y_out, 16 * B)

        @block.gpsimd
        def _(pool):
            g = nc.gpsimd
            steps = [0]

            def link(ins):
                steps[0] += 1
                ins.then_inc(s["step_pool"], 1)
                pool.wait_ge(s["step_pool"], steps[0])

            for m, v in ((ident, 0.0), (identb, 0.0), (tri, 1.0), (before, 1.0)):
                last = g.memset(m[:], v)
            link(last)
            for m in (ident, identb):
                g.affine_select(out=m[:, :], in_=m[:, :], compare_op=ALU.not_equal, fill=1.0, base=0,
                                pattern=[[-1, 128]], channel_multiplier=1)
            g.affine_select(out=tri[:, :], in_=tri[:, :], compare_op=ALU.is_ge, fill=0.0, base=0,
                            pattern=[[1, 128]], channel_multiplier=-1)
            g.affine_select(out=before[:, :, :], in_=before[:, :, :], compare_op=ALU.is_gt, fill=0.0, base=0,
                            pattern=[[1, NE], [-1, NE]], channel_multiplier=0)
            g.memset(ones[:, :], 1.0)
            g.memset(onesb[:, :], 1.0)
            g.memset(mhalf[:, :], -0.5)
            g.iota(pidx[:, :], pattern=[[0, 1]], base=0, channel_multiplier=1,
                   allow_small_or_imprecise_dtypes=True)
            g.iota(iota_t[:, :], pattern=[[1, T]], base=0, channel_multiplier=0,
                   allow_small_or_imprecise_dtypes=True).then_inc(s["const"], 1)
            pool.wait_ge(s["const"], 1)

            def ln_rs(k):
                pool.wait_ge(s["ln_stats"], k + 1)
                r = rs[0:T, k % 2]
                link(g.tensor_scalar(r[:, 0, :], mv[0:T, k % 2, :, 1], 1.0, LN_EPS, ALU.mult, ALU.add))
                g.tensor_tensor(r[:, 1, :], r[:, 0, :], mhalf[0:T, :], ALU.pow).then_inc(s["ln_rs"], 1)

            def split(n):
                width = 2 * S if SPLITS[n][0] == "ctx" else W
                pool.wait_ge(s["sp_r1"], n + 1)
                c_ = comp[:, n % 2]
                link(g.tensor_scalar(c_[:, 1, 0:width], r1[:, n % 2, 0:width], 1.0, 0.0, ALU.mult, ALU.add))
                g.tensor_tensor(c_[:, 2, 0:width], r1[:, n % 2, 0:width], c_[:, 1, 0:width],
                                ALU.subtract).then_inc(s["sp_lo"], 1)

            def v_pad(c):
                pool.wait_ge(in_ctx[c % 3], 16 * (c // 3 + 1))
                if c >= 2:
                    pool.wait_ge(s["av_pe"], NH * (c - 1))
                for k in range(NCH):
                    last = g.tensor_scalar(vst[0:CH, c % 2, k, :, 0:DH],
                                           ctxs[0:CH, c % 3, k, D:DC].rearrange("p (h d) -> p h d", d=DH),
                                           1.0, 0.0, ALU.mult, ALU.add)
                last.then_inc(s["v_pad"], 1)

            def patch_rs(c):
                pool.wait_ge(s["sq_act"], c + 1)
                link(g.tensor_scalar(rsc[0:T, 0, c:c + 1], ssq[0:T, c:c + 1], 1.0 / DC, LN_EPS, ALU.mult, ALU.add))
                g.tensor_tensor(rsc[0:T, 1, c:c + 1], rsc[0:T, 0, c:c + 1], mhalf[0:T, 0:1], ALU.pow)\
                    .then_inc(s["rs_pool"], 1)

            ln_rs(0)
            ln_rs(1)
            link(g.memset(kst[:, :, :, KEYS:KPAD], 0.0))
            link(g.memset(kst[RB:RB + 2, :, :, 0:KEYS], 1.0))
            g.memset(vst[:, :, :, :, DH:32], 1.0).then_inc(s["ones_pad"], 1)
            for n in range(4):
                split(n)
            v_pad(0)
            for c in range(3):
                split(4 + c)
                patch_rs(c)
            for n in range(7, 11):
                split(n)
            pool.wait_ge(s["gbp_s"], 1)
            pool.wait_ge(s["ln_x"], B)
            for b in range(B):
                last = g.tensor_tensor(xs[0:T, b, :], xs[0:T, b, :], gbp[0:T, :], ALU.add)
            last.then_inc(s["xb_pool"], 1)
            for b in range(B):
                if b + 1 < B:
                    v_pad(b + 1)
                if b + 3 < B:
                    split(SP_AT[("ctx", b + 3)])
                    patch_rs(b + 3)
                if b == 5:
                    ln_rs(2)
            pool.wait_ge(s["exp_act"], NH * B)
            link(g.memset(keep[0:T, :], 1.0))
            g.memset(keep[0:T, :].rearrange("p (b t) -> p b t", t=T)[:, :, 0:1], 0.0).then_inc(s["keep_pool"], 1)
            ln_rs(3)

            def roots(h):
                pool.wait_ge(s["l_st"], h + 1)
                r, v = rs[0:T, h % 2], mv[0:T, h % 2, :, 1]
                link(g.tensor_scalar(r[:, 0, :], v, 1.0, LN_EPS, ALU.mult, ALU.add))
                link(g.tensor_tensor(r[:, 1, :], r[:, 0, :], mhalf[0:T, :], ALU.pow))
                link(g.tensor_tensor(r[:, 2, :], v, r[:, 1, :], ALU.mult))
                link(g.tensor_tensor(r[:, 0, :], r[:, 2, :], r[:, 1, :], ALU.mult))
                link(g.tensor_scalar(r[:, 2, :], r[:, 0, :], 1.0, LN_EPS, ALU.mult, ALU.add))
                link(g.tensor_tensor(r[:, 0, :], r[:, 2, :], mhalf[0:T, :], ALU.pow))
                g.tensor_tensor(r[:, 3, :], r[:, 0, :], r[:, 1, :], ALU.mult).then_inc(s["l_rs"], 1)

            def add_bin(t):
                pool.wait_ge(s["l_xh"], t + 1)
                g.tensor_tensor(xs[0:T, t, :], xs[0:T, t, :], gbin[0:T, :], ALU.add).then_inc(s["l_xg"], 1)

            def root(t):
                pool.wait_ge(s["m_st"], t + 1)
                c_ = lc[0:T, t % HT]
                link(g.tensor_scalar(c_[:, 2:3], c_[:, 1:2], 1.0, LN_EPS, ALU.mult, ALU.add))
                g.tensor_tensor(c_[:, 3:4], c_[:, 2:3], mhalf[0:T, 0:1], ALU.pow).then_inc(s["m_rs"], 1)

            def add_b2(t):
                pool.wait_ge(s["xq_dve"], t + 1)
                g.tensor_tensor(xs[0:T, t, :], xs[0:T, t, :], gb2[0:T, :], ALU.add).then_inc(s["l_xg2"], 1)

            roots(0)
            for e in range(NU):
                for stage, step in (("xh", add_bin), ("win", root), ("xq", add_b2)):
                    t = l_slot(e, stage)
                    if t is not None:
                        step(t)
            roots(1)
            for step in (add_bin, root, add_b2):
                for t in range(HT, B):
                    step(t)

        @block.scalar
        def _(act):
            a = nc.scalar
            act.dma_start(ring[:, 2, 0:2 * D].rearrange("p (i c) -> p i c", c=D),
                          w_proj.rearrange("(i p) c -> p i c", p=128)).then_inc(in_wp, 16)
            act.dma_start(ring[:, 3, 0:2 * D].rearrange("p (i c) -> p i c", c=D),
                          w_in.rearrange("(i p) c -> p i c", p=128)).then_inc(in_wp, 16)
            act.dma_start(ring[0:NE, 2, 2 * D:3 * D], gate_w).then_inc(in_wp, 16)

            def row(v):
                return v.rearrange("(a n) -> a n", a=1)

            smalls = [(gates[:, 0:2], row(g_xattn)), (gates[:, 2:4], row(g_ffn)), (gbp[:, :], row(b_proj)),
                      (gbin[:, :], row(b_in)), (gb2[:, :], row(b2)), (gib[:, :], row(g_init)[:, 0:D]),
                      (b1_b[:, :], row(b1))]
            for dst, src in smalls:
                act.dma_start(dst, src.broadcast_to([128, dst.shape[1]])).then_inc(in_small, 16)
            with nc.allow_non_contiguous_dma(reason="256 scales and 3000 lengths onto partitions"):
                act.dma_start(gres[:, :], g_res.rearrange("(k p) -> p k", p=128)).then_inc(in_small, 16)
                for k in range(NCH):
                    act.dma_start(msk[0:CH, k * B:(k + 1) * B],
                                  patch_lens[:, k * CH:(k + 1) * CH].rearrange("b p -> p b")).then_inc(in_mask, 16)
            for k in range(2):
                act.wait_ge(s["wt_pe"], k + 1)
                a.activation(wT[:, 0, 512 * k:512 * k + 512], bank(k), ACT.Copy).then_inc(s["wt_act"], 1)

            def xnt(k):
                h = k % 2
                act.wait_ge(s["xnt_pe"], 2 * k + 1)
                a.activation(xnT[:, 0, h * W:(h + 1) * W], bank(6)[:, 0:W], ACT.Copy).then_inc(s["xnt_act"], 1)

            def split_hi(n):
                kind, i = SPLITS[n]
                if n >= 2:
                    act.wait_ge(*parts_written(n - 2))
                if kind == "ctx":
                    act.wait_ge(s["ct_pe"], i + 1)
                    a.activation(comp[:, n % 2, 0, :].rearrange("p (g t) -> p g t", g=2), PS[:, 6:8, 0:S],
                                 ACT.Copy).then_inc(s["sp_hi"], 1)
                else:
                    act.wait_ge(s["qk_pe"], i + 1)
                    a.activation(comp[:, n % 2, 0, 0:W], bank(i % 4)[:, 0:W], ACT.Copy,
                                 scale=DH ** -0.5 if i % 4 < 2 else 1.0).then_inc(s["sp_hi"], 1)

            def v_own(c):
                act.wait_ge(s["v_pe"], c + 1)
                if c >= 2:
                    act.wait_ge(s["av_pe"], NH * (c - 1))
                a.activation(vst[0:T, c % 2, NCH, :, 0:DH], bank(7)[0:T, 0:D].rearrange("p (h d) -> p h d", d=DH),
                             ACT.Copy).then_inc(s["v_own"], 1)

            def square(c):
                act.wait_ge(in_ctx[c % 3], 16 * (c // 3 + 1))
                if c >= 1:
                    act.wait_ge(s["sq_act"], c)
                a.activation(sqj[0:T, :], ctxs[0:T, c % 3, 0, :], ACT.Square,
                             accum_out=ssq[0:T, c:c + 1]).then_inc(s["sq_act"], 1)

            def m_hi(b):
                act.wait_ge(s["mt_pe"], b + 1)
                if b >= 2:
                    act.wait_ge(in_mrow, 32 * (b - 1))
                a.activation(mrow[0:NH, b % 2, 0, :], bank(7)[0:NH, 0:T], ACT.Copy).then_inc(s["m_hi"], 1)

            def o_out(b):
                act.wait_ge(s["av_pe"], NH * (b + 1))
                if b >= 1:
                    act.wait_ge(s["nt_pe"], b)
                a.activation(osb[:, :], bank(5)[:, 0:W], ACT.Copy).then_inc(s["o_act"], 1)

            def att_out(b):
                act.wait_ge(s["at_pe"], b + 1)
                if b >= 1:
                    act.wait_ge(s["pj_pe"], b)
                a.activation(attT[:, :], bank(6)[:, 0:2 * T], ACT.Copy).then_inc(s["att_act"], 1)

            def gate_tanh(h):
                act.wait_ge(s["gt_pe"], h + 1)
                if h:
                    act.wait_ge(s["cmb_dve"], h)
                a.activation(gth[0:T, :, :].rearrange("p t e -> p (t e)"), bank(6)[0:T, 0:HT * NE], ACT.Tanh,
                             scale=0.5).then_inc(s["th_act"], 1)

            def rows_out(h):
                act.wait_ge(s["cT_pe"], h + 1)
                if h:
                    act.wait_ge(cscr_out, 16 * h)
                a.activation(cTs[:, :], bank(7)[0:NE, 0:W], ACT.Copy).then_inc(s["cT_act"], 1)

            xnt(0)
            for n in range(4):
                split_hi(n)
            act.wait_ge(in_small, 16 * 8)
            a.activation(tg[:, :], gates[:, :], ACT.Tanh).then_inc(s["tanh_g"], 1)
            act.wait_ge(s["wt_pe"], 5)
            for k in range(2):
                a.mul(winT[:, k, :], bank(4)[:, k * D:(k + 1) * D], gres[:, k:k + 1]).then_inc(s["wt_act"], 1)
            for c in range(3):
                split_hi(4 + c)
                square(c)
            xnt(1)
            for n in range(7, 11):
                split_hi(n)
            v_own(0)
            m_hi(0)
            for b in range(B):
                for h in range(NH):
                    if h == 1 and b >= 1:
                        o_out(b - 1)
                    n = NH * b + h
                    act.wait_ge(s["b_pe"], n + 1)
                    if n >= 4:
                        act.wait_ge(s["av_pe"], n - 3)
                    a.activation(ex[0:CH, n % 4, :], bank(2 + n % 3)[0:CH, 0:W], ACT.Exp).then_inc(s["exp_act"], 1)
                    if h == 5 and b + 1 < B:
                        v_own(b + 1)
                    if h == 7 and b >= 1:
                        att_out(b - 1)
                    if h == 10 and b + 1 < B:
                        m_hi(b + 1)
                    if h == 14 and b + 3 < B:
                        split_hi(SP_AT[("ctx", b + 3)])
                        square(b + 3)
                    if h == 14 and b == 5:
                        xnt(2)
                    if h == 14 and b == 6:
                        gate_tanh(0)
                    if h == 14 and b == 7:
                        rows_out(0)
            o_out(B - 1)
            att_out(B - 1)

            def ternary_out(k):
                act.wait_ge(s["w1t_pe"], 2 * k + 1)
                src = bank(6).bitcast(BF16)
                if k == 0:
                    a.activation(w1T[:, 0, :], src, ACT.Copy).then_inc(s["w12_act"], 1)
                else:
                    a.activation(w2T[:, :, 0:128], src.rearrange("p (k c) -> p k c", k=8), ACT.Copy)\
                        .then_inc(s["w12_act"], 1)

            def xht_out(t):
                act.wait_ge(s["xht_pe"], t + 1)
                a.activation(xhT[t % HT], bank(l_bank("xh", t))[:, 0:2 * T], ACT.Copy).then_inc(s["xht_act"], 1)

            def xqt_out(t):
                act.wait_ge(s["xqt_pe"], t + 1)
                a.activation(xqT[t % HT], bank(l_bank("xq", t)).bitcast(BF16)[:, 0:2 * T], ACT.Copy)\
                    .then_inc(s["xqt_act"], 1)

            def gelu(t):
                act.wait_ge(s["h1_dve"], t + 1)
                a.activation(h1[t % HT][0:T, :], h1[t % HT][0:T, :], ACT.Gelu).then_inc(s["gelu_act"], 1)

            def scale_up(t):
                act.wait_ge(s["s2_dve"], t + 1)
                a.activation(h1[t % HT][0:T, :], h1[t % HT][0:T, :], ACT.Identity, bias=magic[0:T, :],
                             scale=lc[0:T, t % HT, 14:15]).then_inc(s["hr_act"], 1)

            def hqt_out(t):
                act.wait_ge(s["hqt_pe"], t + 1)
                a.activation(hqT[t % HT], bank(l_bank("hq", t)).bitcast(BF16)[:, 0:8 * T], ACT.Copy)\
                    .then_inc(s["hqt_act"], 1)

            for h in range(HALF):
                for e in range(NU):
                    i = h * NU + e
                    act.wait_ge(s["hin_pe"], i + 1)
                    if i >= 2:
                        act.wait_ge(s["t_dve"], i - 1)
                    a.activation(silu_sb[i % 2], bank(2 * (i % 2))[:, 0:W], ACT.Silu).then_inc(s["silu_act"], 1)
                    if h == 0:
                        if e == 2:
                            xnt(3)
                        if e == 5:
                            gate_tanh(1)
                        if e == 8:
                            rows_out(1)
                        if e == 9:
                            act.wait_ge(in_w12, 32)
                            for k, w_ in enumerate((w1s, w2s)):
                                a.activation(junk, w_, ACT.Abs, accum_out=wabs[:, k:k + 1]).then_inc(s["abs_act"], 1)
                                act.wait_ge(s["abs_act"], k + 1)
                        if e in (12, 13):
                            ternary_out(e - 12)
                        if e == 16:
                            act.wait_ge(s["dd_dve"], 1)
                            a.activation(bm[0:T, :], keep[0:T, :], ACT.Exp, scale=-DT).then_inc(s["e_act"], 1)
                    else:
                        for stage, step in (("xh", xht_out), ("gelu", gelu), ("hq", scale_up), ("xq", xqt_out),
                                            ("hq", hqt_out)):
                            t = l_slot(e, stage)
                            if t is not None:
                                step(t)

            for stages in ((xht_out,), (xqt_out,), (gelu,), (scale_up,), (hqt_out,)):
                for t in range(HT, B):
                    for stage in stages:
                        stage(t)

        @block.tensor
        def _(pe):
            mm, tr = nc.tensor.matmul, nc.tensor.transpose
            pe.wait_ge(s["const"], 1)
            pe.wait_ge(in_wq, 16)
            pe.wait_ge(in_wp, 48)
            wq_st = ring[:, 0:2, :].rearrange("p a c -> p (a c)")
            for k in range(2):
                for half_ in range(2):
                    for i in range(4):
                        blk = 4 * half_ + i
                        src = (wq_st[:, blk * D + k * 128:blk * D + (k + 1) * 128] if blk < 6 else
                               ring[:, 2, (blk - 6) * D + k * 128:(blk - 6) * D + (k + 1) * 128])
                        last = tr(bank(2 * k + half_)[:, 128 * i:128 * (i + 1)], src, ident[:, :])
                    last.then_inc(s["wt_pe"], 1)
            for k in range(2):
                for i in range(2):
                    last = tr(bank(4)[:, k * D + 128 * i:k * D + 128 * (i + 1)],
                              ring[:, 3, i * D + k * 128:i * D + (k + 1) * 128], ident[:, :])
            last.then_inc(s["wt_pe"], 1)
            for k in range(2):
                last = tr(bank(5)[:, k * NE:(k + 1) * NE],
                          ring[0:NE, 2, 2 * D + k * 128:2 * D + (k + 1) * 128], ident[0:NE, 0:NE])
            last.then_inc(s["wt_pe"], 1)

            free = {n: None for n in range(8)}

            def take(n, *then):
                if free[n] is not None:
                    pe.wait_ge(*free[n])
                free[n] = then

            def ln_t(k):
                h = k % 2
                pe.wait_ge(s["ln_x"], HT * (k + 1))
                take(6, s["xnt_act"], k + 1)
                take(7, s["xnt_dve"], k + 1)
                for c in range(2):
                    for t in range(HT):
                        last = tr(bank(6 + c)[:, t * T:(t + 1) * T], xn[0:T, t, c * 128:(c + 1) * 128],
                                  ident[0:T, 0:T])
                    last.then_inc(s["xnt_pe"], 1)

            def xnt_ready(k):
                pe.wait_ge(s["xnt_act"], k + 1)
                pe.wait_ge(s["xnt_dve"], k + 1)

            def qk(h):
                xnt_ready(h)
                for i in range(4):
                    if h == 0:
                        pe.wait_ge(s["wt_act"], min(i + 1, 2))
                        pe.wait_ge(s["wt_dve"], max(i - 1, 2))
                    else:
                        pe.wait_ge(s["sp_r1"], i + 1)
                    for c in range(2):
                        last = mm(bank(i)[:, 0:W], wT[:, c, i * 128:(i + 1) * 128], xnT[:, c, h * W:(h + 1) * W],
                                  start=c == 0, stop=c == 1)
                    last.then_inc(s["qk_pe"], 1)

            def ctx_t(c):
                pe.wait_ge(in_ctx[c % 3], 16 * (c // 3 + 1))
                n = SP_AT[("ctx", c)]
                take(6, s["sp_r1"], n + 1)
                take(7, s["sp_r1"], n + 1)
                for g_ in range(2):
                    for k in range(NCH):
                        last = tr(bank(6 + g_)[:, k * CH:(k + 1) * CH],
                                  ctxs[0:CH, c % 3, k, g_ * 128:(g_ + 1) * 128], ident[0:CH, 0:CH])
                last.then_inc(s["ct_pe"], 1)

            def own_v(c):
                take(7, s["v_own"], c + 1)
                for k in range(2):
                    last = mm(bank(7)[0:T, 0:D], xnT[:, k, c * T:(c + 1) * T], wT[:, k, 2 * D:3 * D],
                              start=k == 0, stop=k == 1)
                last.then_inc(s["v_pe"], 1)

            def score_rows(b, h):
                n = NH * b + h
                if h == 0:
                    pe.wait_ge(in_kst[b % 3], 96 * (b // 3 + 1))
                    pe.wait_ge(in_qst[b // HT], 96)
                if n >= 2:
                    pe.wait_ge(s["max_dve"], n - 1)
                mm(bank(n % 2)[0:T, 0:KEYS], qst[0:RB, h, b * T:(b + 1) * T], kst[0:RB, b % 3, h, 0:KEYS],
                   start=True, stop=True).then_inc(s["a_pe"], 1)

            def max_t(b):
                take(7, s["m_lo"], b + 1)
                pe.wait_ge(s["max_dve"], NH * (b + 1))
                tr(bank(7)[0:NH, 0:T], nm[0:T, b % 2, :], ident[0:T, 0:T]).then_inc(s["mt_pe"], 1)

            def score_cols(b, h):
                n = NH * b + h
                if h == 0:
                    pe.wait_ge(in_mrow, 32 * (b + 1))
                if n >= 3:
                    pe.wait_ge(s["exp_act"], n - 2)
                for c in range(NCH + 1):
                    last = mm(bank(2 + n % 3)[0:CH, c * T:(c + 1) * T],
                              kst[0:RB + 2, b % 3, h, c * CH:(c + 1) * CH],
                              qst[0:RB + 2, h, b * T:(b + 1) * T], start=True, stop=True)
                last.then_inc(s["b_pe"], 1)

            def values(b, h):
                n = NH * b + h
                j, i = h % 4, h // 4
                if h == 0:
                    pe.wait_ge(s["v_pad"], b + 1)
                    pe.wait_ge(s["v_own"], b + 1)
                    if b >= 1:
                        pe.wait_ge(s["o_act"], b)
                pe.wait_ge(s["exp_act"], n + 1)
                for c in range(NCH + 1):
                    rows = CH if c < NCH else T
                    last = mm(bank(5)[32 * j:32 * j + 32, i * T:(i + 1) * T], vst[0:rows, b % 2, c, h, :],
                              ex[0:rows, n % 4, c * T:(c + 1) * T], start=c == 0, stop=c == NCH)
                last.then_inc(s["av_pe"], 1)

            def norm_t(b):
                pe.wait_ge(s["o_act"], b + 1)
                take(6, s["as_dve"], b + 1)
                for i in range(4):
                    last = tr(bank(6)[0:T, 128 * i:128 * (i + 1)], osb[:, i * T:(i + 1) * T], ident[:, :])
                last.then_inc(s["nt_pe"], 1)

            def att_t(b):
                take(6, s["att_act"], b + 1)
                att = asb[0:T, :, :].rearrange("p h d -> p (h d)")
                for k in range(2):
                    last = tr(bank(6)[:, k * T:(k + 1) * T], att[:, k * 128:(k + 1) * 128], ident[0:T, 0:T])
                last.then_inc(s["at_pe"], 1)

            def project(b):
                take(6, s["x1_dve"], b + 1)
                for k in range(2):
                    last = mm(bank(6)[0:T, 0:D], attT[:, k * T:(k + 1) * T], wT[:, k, 3 * D:4 * D],
                              start=k == 0, stop=k == 1)
                last.then_inc(s["pj_pe"], 1)

            def gate_logits(h):
                take(6, s["th_act"], h + 1)
                pe.wait_ge(s["wt_dve"], 3)
                xnt_ready(2 + h)
                for t in range(HT):
                    for k in range(2):
                        at = h * W + t * T
                        last = mm(bank(6)[0:T, t * NE:(t + 1) * NE], xnT[:, k, at:at + T], gateT[:, k, :],
                                  start=k == 0, stop=k == 1)
                last.then_inc(s["gt_pe"], 1)

            def combine_t(h):
                take(7, s["cT_act"], h + 1)
                pe.wait_ge(s["cmb_dve"], h + 1)
                for t in range(HT):
                    last = tr(bank(7)[0:NE, t * T:(t + 1) * T], gsg[0:T, t, :], ident[0:T, 0:T])
                last.then_inc(s["cT_pe"], 1)

            ln_t(0)
            qk(0)
            for c in range(3):
                ctx_t(c)
            ln_t(1)
            qk(1)
            own_v(0)
            pe.wait_ge(s["ones_pad"], 1)
            pe.wait_ge(s["sp_r1"], 11)
            pe.wait_ge(s["wt_act"], 4)
            pe.wait_ge(s["wt_dve"], 3)
            for h in range(NH):
                score_rows(0, h)
            max_t(0)
            for b in range(B):
                for h in range(NH):
                    if h < 8 and b + 1 < B:
                        score_rows(b + 1, 2 * h)
                        score_rows(b + 1, 2 * h + 1)
                    score_cols(b, h)
                    if h >= 2:
                        values(b, h - 2)
                    if h == 3 and b >= 1:
                        norm_t(b - 1)
                    if h == 4 and b + 1 < B:
                        own_v(b + 1)
                    if h == 6 and b >= 1:
                        att_t(b - 1)
                    if h == 9 and b >= 1:
                        project(b - 1)
                    if h == 9 and b + 1 < B:
                        max_t(b + 1)
                    if h == 13 and b + 3 < B:
                        ctx_t(b + 3)
                    if h == 13 and b == 5:
                        ln_t(2)
                    if h == 13 and b == 6:
                        gate_logits(0)
                    if h == 13 and b == 7:
                        combine_t(0)
                values(b, NH - 2)
                values(b, NH - 1)
            norm_t(B - 1)
            att_t(B - 1)
            project(B - 1)

            def up(i):
                h = i // NU
                r = ring[:, i % 4, :]
                xnt_ready(2 + h)
                pe.wait_ge(in_ring[i % 4], 48 * (i // 4 + 1))
                if i >= 2:
                    pe.wait_ge(s["t_dve"], i - 1)
                for v, name in ((0, "hin_pe"), (1, "vin_pe")):
                    for k in range(2):
                        last = mm(bank(2 * (i % 2) + v)[:, 0:W], r[:, (2 * v + k) * HID:(2 * v + k + 1) * HID],
                                  xnT[:, k, h * W:(h + 1) * W], start=k == 0, stop=k == 1)
                    last.then_inc(s[name], 1)

            def down(i):
                h, e = divmod(i, NU)
                if e == 0:
                    if h:
                        pe.wait_ge(s["x2_dve"], HT * h)
                if e < 2:
                    pe.wait_ge(s["t_dve"], i + 1)
                else:
                    pe.wait_ge(s["h_dve"], h * NE + e - 1)
                for t in range(HT):
                    last = mm(bank(4 + t // 2)[0:T, (t % 2) * D:(t % 2 + 1) * D], h_sb[i % 2][:, t * T:(t + 1) * T],
                              ring[:, i % 4, 4 * HID:6 * HID], start=e == 0 and t % 2 == 0, stop=e == NU - 1,
                              skip_group_check=True)
                last.then_inc(s["out_pe"], 1)

            def sums_of_abs():
                take(6, s["ws_dve"], 1)
                pe.wait_ge(s["abs_act"], 2)
                mm(bank(6)[:, 0:2], ones[:, :], wabs[:, :], start=True, stop=True).then_inc(s["ws_pe"], 1)

            def ternary_t(k):
                pe.wait_ge(s["tq_dve"], k + 1)
                take(6, s["w12_act"], k + 1)
                take(7, s["w12_dve"], k + 1)
                for c in range(2):
                    for i in range(8):
                        src = (tq1[:, i * D + c * 128:i * D + (c + 1) * 128] if k == 0 else
                               tq2[:, c * H4 + i * 128:c * H4 + (i + 1) * 128])
                        last = tr(bank(6 + c).bitcast(BF16)[:, i * 128:(i + 1) * 128], src, identb[:, :])
                    last.then_inc(s["w1t_pe"], 1)

            def patch_ends():
                take(6, s["eq_dve"], 1)
                pe.wait_ge(s["m_dve"], 1)
                for c in range(NCH):
                    for k in range(c + 1):
                        last = mm(bank(6)[0:CH, c * B:(c + 1) * B], (tri if k == c else ones)[0:CH, 0:CH],
                                  mskf[0:CH, k * B:(k + 1) * B], start=k == 0, stop=k == c)
                last.then_inc(s["cs_pe"], 1)

            def end_counts():
                pe.wait_ge(s["eq_dve"], 2)
                take(6, s["dd_dve"], 1)
                take(7, s["dd_dve"], 1)
                for h in range(HALF):
                    for c in range(NCH):
                        last = mm(bank(6 + h)[0:T, 0:W], onesb[0:CH, 0:T],
                                  eqm[0:CH, c * B * T + h * W:c * B * T + (h + 1) * W], start=c == 0, stop=c == NCH - 1)
                last.then_inc(s["cnt_pe"], 1)

            def xh_t(t):
                n = l_bank("xh", t)
                pe.wait_ge(s["l_xh"], t + 1)
                take(n, s["xht_act"], t + 1)
                for c in range(2):
                    last = tr(bank(n)[:, c * T:(c + 1) * T], xh[t % HT][0:T, c * 128:(c + 1) * 128], ident[0:T, 0:T])
                last.then_inc(s["xht_pe"], 1)

            def win_depool(t):
                n = l_bank("win", t)
                take(n, s["x3_dve"], t + 1)
                pe.wait_ge(s["u_dve"], B)
                pe.wait_ge(s["wdep_dve"], 1)
                mm(bank(n)[0:T, 0:D], wdep[0:T, t * T:(t + 1) * T], u[0:T, t, :], start=True, stop=False)
                pe.wait_ge(s["xht_act"], t + 1)
                for c in range(2):
                    last = mm(bank(n)[0:T, 0:D], xhT[t % HT][:, c * T:(c + 1) * T], winT[:, c, :],
                              start=False, stop=c == 1)
                last.then_inc(s["win_pe"], 1)

            def xq_t(t):
                n = l_bank("xq", t)
                pe.wait_ge(s["xq_dve"], t + 1)
                take(n, s["xqt_act"], t + 1)
                for c in range(2):
                    last = tr(bank(n).bitcast(BF16)[:, c * T:(c + 1) * T], xq[t % HT][0:T, c * 128:(c + 1) * 128],
                              identb[0:T, 0:T])
                last.then_inc(s["xqt_pe"], 1)

            def w1_up(t):
                n = l_bank("w1", t)
                pe.wait_ge(s["xqt_act"], t + 1)
                pe.wait_ge(s["w12_act"], 2)
                pe.wait_ge(s["w12_dve"], 2)
                for half_ in range(2):
                    take(n + half_, s["h1_dve"], t + 1)
                    for c in range(2):
                        last = mm(bank(n + half_)[0:T, :], xqT[t % HT][:, c * T:(c + 1) * T],
                                  w1T[:, c, half_ * 512:(half_ + 1) * 512], start=c == 0, stop=c == 1)
                last.then_inc(s["w1_pe"], 1)

            def hq_t(t):
                n = l_bank("hq", t)
                pe.wait_ge(s["hq_dve"], t + 1)
                take(n, s["hqt_act"], t + 1)
                for c in range(8):
                    last = tr(bank(n).bitcast(BF16)[:, c * T:(c + 1) * T], hq[t % HT][0:T, c * 128:(c + 1) * 128],
                              identb[0:T, 0:T])
                last.then_inc(s["hqt_pe"], 1)

            def w2_down(t):
                n = l_bank("w2", t)
                pe.wait_ge(s["hqt_act"], t + 1)
                take(n, s["y_dve"], t + 1)
                for c in range(8):
                    last = mm(bank(n)[0:T, 0:D], hqT[t % HT][:, c * T:(c + 1) * T], w2T[:, c, :],
                              start=c == 0, stop=c == 7)
                last.then_inc(s["w2_pe"], 1)

            def l_steps(e, *steps):
                for stage, step in steps:
                    t = l_slot(e, stage)
                    if t is not None:
                        step(t)

            for h in range(HALF):
                for e in range(NU):
                    i = h * NU + e
                    up(i)
                    if h == 1:
                        l_steps(e, ("xh", xh_t), ("w2", w2_down), ("win", win_depool), ("xq", xq_t))
                    if e >= 1:
                        down(i - 1)
                    if h == 1:
                        l_steps(e, ("w1", w1_up), ("hq", hq_t))
                    if h == 0:
                        if e == 2:
                            ln_t(3)
                        if e == 5:
                            gate_logits(1)
                        if e == 8:
                            combine_t(1)
                        if e == 10:
                            sums_of_abs()
                        if e in (12, 13):
                            ternary_t(e - 12)
                        if e == 14:
                            patch_ends()
                        if e == 15:
                            end_counts()
                down(h * NU + NU - 1)

            pe.wait_ge(s["x2_dve"], B)
            pe.wait_ge(s["t_dve"], HALF * NU)
            for step in (xh_t, win_depool, xq_t, w1_up, hq_t, w2_down):
                for t in range(HT, B):
                    step(t)

        @block.vector
        def _(dve):
            v = nc.vector
            steps = [0]

            def link(ins):
                steps[0] += 1
                ins.then_inc(s["step_dve"], 1)
                dve.wait_ge(s["step_dve"], steps[0])

            def ln_stats(k, name="ln_stats"):
                h = k % 2
                for t in range(HT):
                    last = v.bn_stats(stats[0:T, h, t, :], xs[0:T, h * HT + t, :])
                link(last)
                for t in range(HT):
                    last = v.bn_aggr(mv[0:T, h, t, :], stats[0:T, h, t, :])
                last.then_inc(s[name], 1)
                dve.wait_ge(s[name], k + 1 if name == "ln_stats" else h + 1)

            def ln_x(k):
                h = k % 2
                dve.wait_ge(s["ln_rs"], k + 1)
                if k >= 1:
                    dve.wait_ge(s["xnt_pe"], 2 * k)
                for t in range(HT):
                    v.tensor_scalar(xn[0:T, t, :], xs[0:T, h * HT + t, :], mv[0:T, h, t, 0:1], rs[0:T, h, 1, t:t + 1],
                                    ALU.subtract, ALU.mult).then_inc(s["ln_x"], 1)

            def xnt(k):
                h = k % 2
                dve.wait_ge(s["xnt_pe"], 2 * k + 2)
                v.tensor_copy(xnT[:, 1, h * W:(h + 1) * W], bank(7)[:, 0:W]).then_inc(s["xnt_dve"], 1)

            def split_r1(n):
                kind, i = SPLITS[n]
                dve.wait_ge(s["sp_hi"], n + 1)
                if n >= 2:
                    dve.wait_ge(s["sp_lo"], n - 1)
                hi = comp[:, n % 2, 0, :]
                if kind == "ctx":
                    v.tensor_tensor(r1[:, n % 2, :].rearrange("p (g t) -> p g t", g=2), PS[:, 6:8, 0:S],
                                    hi.rearrange("p (g t) -> p g t", g=2), ALU.subtract).then_inc(s["sp_r1"], 1)
                else:
                    v.scalar_tensor_tensor(out=r1[:, n % 2, 0:W], in0=bank(i % 4)[:, 0:W],
                                           scalar=DH ** -0.5 if i % 4 < 2 else 1.0, in1=hi[:, 0:W],
                                           op0=ALU.mult, op1=ALU.subtract).then_inc(s["sp_r1"], 1)

            def patches(c):
                dve.wait_ge(s["rs_pool"], c + 1)
                v.scalar_tensor_tensor(out=u[0:T, c, :], in0=ctxs[0:T, c % 3, 0, 0:D], scalar=rsc[0:T, 1, c:c + 1],
                                       in1=gib[0:T, :], op0=ALU.mult, op1=ALU.mult).then_inc(s["u_dve"], 1)

            def row_max(b, h):
                n = NH * b + h
                dve.wait_ge(s["a_pe"], n + 1)
                if h == 0 and b >= 2:
                    dve.wait_ge(s["mt_pe"], b - 1)
                v.tensor_reduce(nm[0:T, b % 2, h:h + 1], bank(n % 2)[0:T, 0:KEYS], AX.X, ALU.max,
                                negate=True).then_inc(s["max_dve"], 1)

            def m_lo(b):
                dve.wait_ge(s["m_hi"], b + 1)
                v.tensor_tensor(mrow[0:NH, b % 2, 1, :], bank(7)[0:NH, 0:T], mrow[0:NH, b % 2, 0, :],
                                ALU.subtract).then_inc(s["m_lo"], 1)

            def normalise(b):
                dve.wait_ge(s["nt_pe"], b + 1)
                o = bank(6)[0:T, :].rearrange("p (h d) -> p h d", d=32)
                if b >= 1:
                    dve.wait_ge(s["as_dve"], b)
                link(v.reciprocal(rinv[0:T, :], o[:, :, DH]))
                if b >= 1:
                    dve.wait_ge(s["at_pe"], b)
                v.tensor_tensor(asb[0:T, :, :], o[:, :, 0:DH],
                                rinv[0:T, :].unsqueeze(2).broadcast_to([T, NH, DH]), ALU.mult)\
                    .then_inc(s["as_dve"], 1)

            def residual1(b):
                dve.wait_ge(s["pj_pe"], b + 1)
                dve.wait_ge(s["xb_pool"], 1)
                v.scalar_tensor_tensor(out=xs[0:T, b, :], in0=bank(6)[0:T, 0:D], scalar=tg[0:T, 0:1],
                                       in1=xs[0:T, b, :], op0=ALU.mult, op1=ALU.add).then_inc(s["x1_dve"], 1)

            def gate_weights(h):
                dve.wait_ge(s["th_act"], h + 1)
                dve.wait_ge(s["v_pad"], B)
                dve.wait_ge(s["ct_pe"], B)
                if h:
                    dve.wait_ge(s["cT_pe"], h)
                g_ = gth[0:T, :, :]
                link(v.tensor_scalar(g_, g_, 0.5, 0.5, ALU.mult, ALU.add))
                n = HT * NE * NE
                cmp, eq = ranks[0:T, 0:n], ranks[0:T, n:2 * n]
                for t in range(HT):
                    gj = g_[:, t, :].unsqueeze(1).broadcast_to([T, NE, NE])
                    ge = g_[:, t, :].unsqueeze(2).broadcast_to([T, NE, NE])
                    sl = slice(t * NE * NE, (t + 1) * NE * NE)
                    v.tensor_tensor(cmp[:, sl].rearrange("p (e j) -> p e j", e=NE), gj, ge, ALU.is_gt)
                    last = v.tensor_tensor(eq[:, sl].rearrange("p (e j) -> p e j", e=NE), gj, ge, ALU.is_equal)
                link(last)
                link(v.tensor_tensor(eq.rearrange("p (t n) -> p t n", t=HT), eq.rearrange("p (t n) -> p t n", t=HT),
                                     before[0:T, :, :].rearrange("p e j -> p (e j)").unsqueeze(1)
                                     .broadcast_to([T, HT, NE * NE]), ALU.mult))
                link(v.tensor_tensor(cmp, cmp, eq, ALU.add))
                rk = ranks[0:T, n:n + HT * NE]
                link(v.tensor_reduce(rk, cmp.rearrange("p (a j) -> p a j", j=NE), AX.X, ALU.add))
                flat = gsg[0:T, :, :].rearrange("p t e -> p (t e)")
                link(v.scalar_tensor_tensor(out=flat, in0=rk, scalar=float(TOPK), in1=g_.rearrange("p t e -> p (t e)"),
                                            op0=ALU.is_lt, op1=ALU.mult))
                link(v.tensor_reduce(gsum[0:T, 0, :], gsg[0:T, :, :], AX.X, ALU.add))
                link(v.reciprocal(gsum[0:T, 1, :], gsum[0:T, 0, :]))
                v.tensor_tensor(gsg[0:T, :, :], gsg[0:T, :, :],
                                gsum[0:T, 1, :].unsqueeze(2).broadcast_to([T, HT, NE]), ALU.mult)\
                    .then_inc(s["cmb_dve"], 1)
                dve.wait_ge(s["cmb_dve"], h + 1)

            v.memset(magic[:, :], MAGIC)
            dve.wait_ge(in_x, 16)
            ln_stats(0)
            ln_stats(1)
            for k in range(2):
                dve.wait_ge(s["wt_pe"], 3 + k)
                v.tensor_copy(wT[:, 1, 512 * k:512 * (k + 1)], bank(2 + k)).then_inc(s["wt_dve"], 1)
            ln_x(0)
            dve.wait_ge(s["wt_pe"], 6)
            v.tensor_copy(gateT[:, :, :], bank(5)[:, 0:2 * NE].rearrange("p (k e) -> p k e", k=2))\
                .then_inc(s["wt_dve"], 1)
            xnt(0)
            for n in range(4):
                split_r1(n)
            dve.wait_ge(s["tanh_g"], 1)
            link(v.tensor_scalar(gbp[:, :], gbp[:, :], tg[:, 0:1], None, ALU.mult))
            v.tensor_scalar(gib[:, :], gib[:, :], BCOEF, None, ALU.mult)
            v.tensor_scalar(gbin[:, :], gbin[:, :], tg[:, 1:2], None, ALU.mult)
            v.tensor_scalar(gb2[:, :], gb2[:, :], tg[:, 3:4], None, ALU.mult).then_inc(s["gbp_s"], 1)
            dve.wait_ge(s["gbp_s"], 1)
            ln_x(1)
            for c in range(3):
                split_r1(4 + c)
                patches(c)
            xnt(1)
            for n in range(7, 11):
                split_r1(n)
            for h in range(NH):
                row_max(0, h)
            m_lo(0)
            for b in range(B):
                for h in range(NH):
                    if b + 1 < B:
                        row_max(b + 1, h)
                    if h == 7 and b >= 1:
                        normalise(b - 1)
                if b + 1 < B:
                    m_lo(b + 1)
                if b >= 1:
                    residual1(b - 1)
                if b + 3 < B:
                    split_r1(SP_AT[("ctx", b + 3)])
                    patches(b + 3)
                if b == 5:
                    dve.wait_ge(s["x1_dve"], 4)
                    ln_stats(2)
                    ln_x(2)
                    xnt(2)
                if b == 6:
                    gate_weights(0)
            normalise(B - 1)
            residual1(B - 1)
            dve.wait_ge(s["x1_dve"], B)
            ln_stats(3)
            ln_x(3)
            dve.wait_ge(in_mask, 16 * NCH)
            v.tensor_copy(mskf[0:CH, :], msk[0:CH, :]).then_inc(s["m_dve"], 1)

            def ternary():
                dve.wait_ge(s["ws_pe"], 1)
                v.tensor_scalar(wsc[:, 0, :], bank(6)[:, 0:2], 1.0 / (H4 * D), Q_EPS, ALU.mult, ALU.max)\
                    .then_inc(s["ws_dve"], 1)
                dve.wait_ge(s["ws_dve"], 1)
                v.tensor_scalar(wsc[:, 1, :], wsc[:, 0, :], 0.5, None, ALU.mult)
                v.tensor_scalar(wsc[:, 2, :], wsc[:, 0, :], -0.5, None, ALU.mult)
                link(v.tensor_scalar(wsc[:, 3, :], wsc[:, 0, :], -1.0 / QB, None, ALU.mult))
                v.tensor_scalar(wsc[:, 4, 0:1], wsc[:, 3, 0:1], 1.0, None, ALU.mult)
                link(v.tensor_scalar(wsc[:, 4, 1:2], wsc[:, 3, 1:2], tg[:, 3:4], None, ALU.mult))
                for k, (w_, q_) in enumerate(((w1s, tq1), (w2s, tq2))):
                    big = junk[:, k * 1024:(k + 1) * 1024].bitcast(BF16)
                    link(v.tensor_scalar(big, w_, wsc[:, 1, k:k + 1], None, ALU.is_gt))
                    v.scalar_tensor_tensor(out=q_, in0=w_, scalar=wsc[:, 2, k:k + 1], in1=big,
                                           op0=ALU.is_lt, op1=ALU.subtract).then_inc(s["tq_dve"], 1)

            def ternary_out(k):
                dve.wait_ge(s["w1t_pe"], 2 * k + 2)
                src = bank(7).bitcast(BF16)
                if k == 0:
                    v.tensor_copy(w1T[:, 1, :], src).then_inc(s["w12_dve"], 1)
                else:
                    v.tensor_copy(w2T[:, :, 128:256], src.rearrange("p (k c) -> p k c", k=8)).then_inc(s["w12_dve"], 1)

            def ends_at():
                dve.wait_ge(s["cs_pe"], 1)
                i0, i1 = idx[0:CH, 0, :], idx[0:CH, 1, :]
                v.tensor_scalar(i0, bank(6)[0:CH, 0:NCH * B], 1.0, None, ALU.subtract).then_inc(s["eq_dve"], 1)
                dve.wait_ge(s["eq_dve"], 1)
                link(v.tensor_scalar(i1, i0, 0.0, float(T), ALU.is_lt, ALU.mult))
                link(v.tensor_tensor(i0, i0, i1, ALU.add))
                n = NCH * B
                v.tensor_tensor(eqm[0:CH, :].rearrange("p (n t) -> p n t", n=n),
                                iota_t[0:CH, :].unsqueeze(1).broadcast_to([CH, n, T]),
                                i0.unsqueeze(2).broadcast_to([CH, n, T]), ALU.is_equal).then_inc(s["eq_dve"], 1)

            def distance():
                dve.wait_ge(s["cnt_pe"], 1)
                dve.wait_ge(s["keep_pool"], 1)
                bm_, kp, wd = bm[0:T, :], keep[0:T, :], wdep[0:T, :]
                link(v.tensor_scalar(bm_.rearrange("p (a t) -> p a t", a=2), PS[0:T, 6:8, 0:W], 1.0, None, ALU.min))
                link(v.tensor_tensor_scan(wd, kp, bm_, 0.0, ALU.mult, ALU.add))
                link(v.tensor_scalar(wd, wd, -1.0, 0.0, ALU.add, ALU.max))
                link(v.tensor_scalar(wd, wd, pidx[0:T, :], None, ALU.subtract))
                v.tensor_scalar(kp, wd, 0.0, None, ALU.max).then_inc(s["dd_dve"], 1)

            def depool_weights():
                dve.wait_ge(s["e_act"], 1)
                v.scalar_tensor_tensor(out=wdep[0:T, :], in0=wdep[0:T, :], scalar=0.0, in1=bm[0:T, :],
                                       op0=ALU.is_ge, op1=ALU.mult).then_inc(s["wdep_dve"], 1)

            def hidden(i):
                h, e = divmod(i, NU)
                dve.wait_ge(s["vin_pe"], i + 1)
                dve.wait_ge(s["silu_act"], i + 1)
                shared = e < 2
                if shared and i >= 2:
                    dve.wait_ge(s["out_pe"], i - 1)
                dst = h_sb[i % 2] if shared else t_sb[i % 2]
                v.tensor_tensor(dst, bank(2 * (i % 2) + 1)[:, 0:W], silu_sb[i % 2], ALU.mult)\
                    .then_inc(s["t_dve"], 1)
                if shared:
                    return
                j = h * NE + e - 2
                dve.wait_ge(s["t_dve"], i + 1)
                dve.wait_ge(in_cb[j % 4], 16 * (j // 4 + 1))
                if i >= 2:
                    dve.wait_ge(s["out_pe"], i - 1)
                v.tensor_tensor(h_sb[i % 2], t_sb[i % 2], cb[j % 4], ALU.mult).then_inc(s["h_dve"], 1)

            def residual2(t):
                h, k = divmod(t, HT)
                dve.wait_ge(s["out_pe"], NU * (h + 1))
                v.scalar_tensor_tensor(out=xs[0:T, t, :], in0=bank(4 + k // 2)[0:T, (k % 2) * D:(k % 2 + 1) * D],
                                       scalar=tg[0:T, 2:3], in1=xs[0:T, t, :], op0=ALU.mult, op1=ALU.add)\
                    .then_inc(s["x2_dve"], 1)

            def stage_a(t):
                h = t // HT
                dve.wait_ge(s["l_rs"], h + 1)
                v.tensor_scalar(xh[t % HT][0:T, :], xs[0:T, t, :], mv[0:T, h, t % HT, 0:1],
                                rs[0:T, h, 3, t % HT:t % HT + 1], ALU.subtract, ALU.mult).then_inc(s["l_xh"], 1)

            def stage_b(t):
                dve.wait_ge(s["win_pe"], t + 1)
                dve.wait_ge(s["l_xg"], t + 1)
                c_ = lc[0:T, t % HT]
                v.scalar_tensor_tensor(out=xs[0:T, t, :], in0=bank(l_bank("win", t))[0:T, 0:D], scalar=tg[0:T, 1:2],
                                       in1=xs[0:T, t, :], op0=ALU.mult, op1=ALU.add).then_inc(s["x3_dve"], 1)
                dve.wait_ge(s["x3_dve"], t + 1)
                link(v.bn_stats(c_[:, 16:22], xs[0:T, t, :]))
                v.bn_aggr(c_[:, 0:2], c_[:, 16:22]).then_inc(s["m_st"], 1)

            def stage_c(t):
                dve.wait_ge(s["m_st"], t + 1)
                dve.wait_ge(s["m_rs"], t + 1)
                c_, f = lc[0:T, t % HT], qf[t % HT][0:T, :]
                link(v.tensor_scalar(f, xs[0:T, t, :], c_[:, 0:1], c_[:, 3:4], ALU.subtract, ALU.mult))
                link(v.tensor_reduce(c_[:, 4:5], f, AX.X, ALU.max, apply_absolute_value=True))
                link(v.tensor_scalar(c_[:, 5:6], c_[:, 4:5], Q_EPS, None, ALU.max))
                link(v.reciprocal(c_[:, 6:7], c_[:, 5:6]))
                v.tensor_tensor(c_[:, 8:9], c_[:, 5:6], wsc[0:T, 4, 0:1], ALU.mult)
                link(v.tensor_scalar(c_[:, 7:8], c_[:, 6:7], QB, None, ALU.mult))
                link(v.tensor_scalar(f, f, c_[:, 7:8], MAGIC, ALU.mult, ALU.add))
                v.tensor_scalar(xq[t % HT][0:T, :], f, MAGIC, QB, ALU.subtract, ALU.min).then_inc(s["xq_dve"], 1)

            def stage_d(t):
                n = l_bank("w1", t)
                dve.wait_ge(s["w1_pe"], t + 1)
                dve.wait_ge(s["xq_dve"], t + 1)
                v.scalar_tensor_tensor(out=h1[t % HT][0:T, :].rearrange("p (a n) -> p a n", a=2),
                                       in0=PS[0:T, n:n + 2, :], scalar=lc[0:T, t % HT, 8:9],
                                       in1=b1_b[0:T, :].rearrange("p (a n) -> p a n", a=2),
                                       op0=ALU.mult, op1=ALU.add).then_inc(s["h1_dve"], 1)

            def stage_e(t):
                c_ = lc[0:T, t % HT]
                dve.wait_ge(s["gelu_act"], t + 1)
                link(v.tensor_reduce(c_[:, 10:11], h1[t % HT][0:T, :], AX.X, ALU.max, apply_absolute_value=True))
                link(v.tensor_scalar(c_[:, 11:12], c_[:, 10:11], Q_EPS, None, ALU.max))
                link(v.reciprocal(c_[:, 12:13], c_[:, 11:12]))
                v.tensor_tensor(c_[:, 13:14], c_[:, 11:12], wsc[0:T, 4, 1:2], ALU.mult)
                v.tensor_scalar(c_[:, 14:15], c_[:, 12:13], QB, None, ALU.mult).then_inc(s["s2_dve"], 1)

            def stage_f(t):
                dve.wait_ge(s["s2_dve"], t + 1)
                dve.wait_ge(s["hr_act"], t + 1)
                v.tensor_scalar(hq[t % HT][0:T, :], h1[t % HT][0:T, :], MAGIC, QB, ALU.subtract, ALU.min)\
                    .then_inc(s["hq_dve"], 1)

            def stage_g(t):
                dve.wait_ge(s["w2_pe"], t + 1)
                dve.wait_ge(s["l_xg2"], t + 1)
                v.scalar_tensor_tensor(out=xs[0:T, t, :], in0=bank(l_bank("w2", t))[0:T, 0:D],
                                       scalar=lc[0:T, t % HT, 13:14], in1=xs[0:T, t, :],
                                       op0=ALU.mult, op1=ALU.add).then_inc(s["y_dve"], 1)

            def l_steps(e, *steps):
                for stage, step in steps:
                    t = l_slot(e, stage)
                    if t is not None:
                        step(t)

            for h in range(HALF):
                for e in range(NU):
                    hidden(h * NU + e)
                    if h == 0:
                        if e == 2:
                            xnt(3)
                        if e == 6:
                            gate_weights(1)
                        if e == 10:
                            ternary()
                        if e in (12, 13):
                            ternary_out(e - 12)
                        if e == 14:
                            ends_at()
                        if e == 15:
                            distance()
                        if e == 17:
                            depool_weights()
                    else:
                        l_steps(e, ("w2", stage_g), ("win", stage_b), ("gelu", stage_e), ("win", stage_c),
                                ("hq", stage_f), ("pre", stage_a), ("w1", stage_d))
                for t in range(h * HT, (h + 1) * HT):
                    residual2(t)
                dve.wait_ge(s["x2_dve"], HT * (h + 1))
                ln_stats(h, "l_st")
            for step in (stage_a, stage_b, stage_c, stage_d, stage_e, stage_f, stage_g):
                for t in range(HT, B):
                    step(t)


_INS = ['x', 'ctx_2048', 'mask_BxS2_if0', 'g_xattn', 'g_ffn', 'L0_xattn_w_qkv', 'L0_xattn_w_proj', 'L0_xattn_b_proj',
        'L0_ffn_gate_w', 'L0_ffn_ws_in', 'L0_ffn_vs_in', 'L0_ffn_ws_out', 'L0_ffn_e_win', 'L0_ffn_e_vin',
        'L0_ffn_e_wout', 'L1_xattn_W_in', 'L1_xattn_b_in', 'L1_xattn_g_res', 'L1_xattn_g_init', 'L1_ffn_W1',
        'L1_ffn_b1', 'L1_ffn_W2', 'L1_ffn_b2']


def kernel(**inputs):
    import numpy as _np
    import concourse.bacc as _bacc
    from concourse import mybir as _mybir
    from concourse.bass_utils import run_bass_kernel_spmd as _run

    nc = _bacc.Bacc("TRN2", target_bir_lowering=False, num_devices=1)
    arrays, args = {}, []
    for name in _INS:
        a = _np.ascontiguousarray(inputs[name])
        arrays[f"in_{name}_dram"] = a
        args.append(nc.dram_tensor(f"in_{name}_dram", a.shape, _mybir.dt.from_np(a.dtype), kind="ExternalInput").ap())
    args.append(nc.dram_tensor("out_0_dram", (B, T, D), F32, kind="ExternalOutput").ap())
    flamingo(nc, *args)
    r = _run(nc, [arrays], core_ids=[0])
    return r.results[0]["out_0_dram"]
```

```python
import math
import struct
from contextlib import ExitStack

import concourse.bass as bass
import concourse.mybir as mybir

F32 = mybir.dt.float32
BF16 = mybir.dt.bfloat16
I32 = mybir.dt.int32
ALU = mybir.AluOpType
ACT = mybir.ActivationFunctionType
AX = mybir.AxisListType

B, T, D = 8, 112, 256
S, DC = 375, 512
NH, DH = 16, 16
KEYS = S + T
CH, NCH = 125, 3
KPAD = CH * (NCH + 1)
HALF, HT = 2, 4
W = HT * T
NE, TOPK, HID = 16, 4, 128
NU = NE + 2
H4 = 4 * D
RB = 6 * DH
Q_PART = (0, 0, 0, 1, 1, 2)
K_PART = (0, 1, 2, 0, 1, 0)
LN_EPS = 1e-5
LOGP = -0.001
DT = -math.log(-math.expm1(LOGP))
BCOEF = math.exp(LOGP)
SCORE_ROWS = (0, 1, 4)
NCOMP = 4
EARLY = 7
QB, Q_EPS = 127.0, 1e-5
ONE_PAIR = struct.unpack("f", struct.pack("I", 0x3F803F80))[0]
MAGIC = 1.5 * 2.0 ** 23


def flamingo(nc, x, ctx_in, patch_lens, g_xattn, g_ffn, w_qkv, w_proj, b_proj, gate_w, ws_in, vs_in,
             ws_out, e_win, e_vin, e_wout, w_in, b_in, g_res, g_init, w1, b1, w2, b2, out):
    kscr = nc.dram_tensor("k_parts", (3, D, B, KEYS), BF16, kind="Internal").ap()
    qscr = nc.dram_tensor("q_parts", (3, D, B * T), BF16, kind="Internal").ap()
    cscr = nc.dram_tensor("combine_rows", (NE, B * T), F32, kind="Internal").ap()

    with ExitStack() as stack:
        def sb(name, shape, dt=F32):
            return stack.enter_context(nc.sbuf_tensor(name, shape, dt))

        def sem(name):
            return stack.enter_context(nc.semaphore(name))

        PS = stack.enter_context(nc.psum_tensor("banks", [128, 8, 512], F32))

        def bank(i):
            return PS[:, i, :]


        ident = sb("ident", [128, 128])
        identb = sb("identb", [128, 128], BF16)
        ones = sb("ones", [128, 128])
        onesb = sb("onesb", [128, 128], BF16)
        tri = sb("tri", [128, 128])
        before = sb("before", [128, NE, NE])
        mhalf = sb("mhalf", [128, HT])
        pidx = sb("pidx", [128, 1])
        iota_t = sb("iota_t", [128, T])
        xs = sb("xs", [128, B, D])
        xn = sb("xn", [128, HT, D])
        xnT = sb("xnT", [128, 2, B * T])
        wT = sb("wT", [128, 2, 4 * D])
        winT = sb("winT", [128, 2, D])
        gateT = sb("gateT", [128, 2, NE])
        gates = sb("gates", [128, 4])
        tg = sb("tg", [128, 4])
        gres = sb("gres", [128, 2])
        gbp = sb("gbp", [128, D])
        gbin = sb("gbin", [128, D])
        gb2 = sb("gb2", [128, D])
        gib = sb("gib", [128, D])
        b1_b = sb("b1_b", [128, H4])
        stats = sb("stats", [128, 2, HT, 6])
        mv = sb("mv", [128, 2, HT, 2])
        rs = sb("rs", [128, 2, 4, HT])
        ssq = sb("ssq", [128, B])
        rsc = sb("rsc", [128, 2, B])
        u = sb("u", [128, B, D])
        w2T = sb("w2T", [128, 8, D], BF16)
        ring = sb("ring", [128, 4, 6 * HID])
        kst = sb("kst", [128, 3, NH, KPAD], BF16)
        qst = sb("qst", [128, NH, B * T], BF16)
        ctxs = sb("ctxs", [128, 3, NCH, DC])
        vst = sb("vst", [128, 2, NCH + 1, NH, 32])
        ex = sb("ex", [128, 4, W])
        comp_ = sb("comp", [128, NCOMP - 1, 3, 2 * S], BF16)
        r1 = sb("r1", [128, 2, 2 * S])
        nm = sb("nm", [128, 2, NH])
        mrow = sb("mrow", [128, 2, 2, T], BF16)
        osb = sb("osb", [128, W])
        rinv = sb("rinv", [128, NH])
        asb = sb("asb", [128, NH, DH])
        attT = sb("attT", [128, 2 * T])
        comp = [comp_[:, n, :, :] for n in range(NCOMP - 1)] + [
            ring[:, 0:2, :].rearrange("p a c -> p (a c)").bitcast(BF16)[:, 0:6 * S]
            .rearrange("p (a t) -> p a t", a=3)]
        gth = sb("gth", [128, HT, NE])
        gsg = sb("gsg", [128, HT, NE])
        gsum = sb("gsum", [128, 2, HT])
        msk = sb("msk", [128, NCH * B], I32)
        sqj = sb("sqj", [128, DC], BF16)
        magic = sb("magic", [128, 1])
        mskf = sb("mskf", [128, NCH * B])
        idx = sb("idx", [128, 2, NCH * B])
        wabs = sb("wabs", [128, 2])
        wsc = sb("wsc", [128, 5, 2])
        lc = sb("lc", [128, HT, 24])

        later_q = qst[:, :, :].rearrange("p h t -> p (h t)").bitcast(F32)
        later_k = kst[:, :, :, :].rearrange("p s h t -> p (s h t)").bitcast(F32)
        later_v = vst[:, :, :, :, :].rearrange("p a c h d -> p (a c h d)")

        def cut(region, at, n):
            return region[:, at:at + n]

        silu_sb = [cut(later_q, i * W, W) for i in range(2)]
        t_sb = [cut(later_q, (2 + i) * W, W) for i in range(2)]
        h_sb = [cut(later_q, (4 + i) * W, W) for i in range(2)]
        cb = [cut(later_q, (6 + i) * W, W) for i in range(4)]
        w1s = cut(later_k, 0, 8 * D)
        w2s = cut(later_k, 2048, 2 * H4)
        junk = cut(later_k, 4096, 2048)
        tq1 = cut(later_k, 6144, 1024).bitcast(BF16)
        tq2 = cut(later_k, 7168, 1024).bitcast(BF16)
        eqm = cut(later_k, 8192, 1344).bitcast(BF16)
        bm = cut(later_k, 9536, B * T)
        keep = cut(later_k, 10432, B * T)
        h1 = [cut(later_k, i * H4, H4) for i in range(HT)]
        hq = [cut(later_k, 4096 + 512 * i, 512).bitcast(BF16) for i in range(HT)]
        hqT = [cut(later_k, 6144 + 448 * i, 448).bitcast(BF16) for i in range(HT)]
        wdep = cut(later_v, 0, B * T)
        w1T = cut(later_v, 3072, H4).bitcast(BF16).rearrange("p (k c) -> p k c", k=2)
        xh = [cut(later_v, 1024 + i * D, D) for i in range(HT)]
        xhT = [cut(later_v, 2048 + i * 2 * T, 2 * T) for i in range(HT)]
        qf = xh
        xq = [cut(later_q, 10 * W + 128 * i, 128).bitcast(BF16) for i in range(HT)]
        xqT = [cut(later_q, 10 * W + 512 + 112 * i, 112).bitcast(BF16) for i in range(HT)]
        cTs = comp[0][0:NE, :, :].rearrange("p a t -> p (a t)").bitcast(F32)[:, 0:W]
        ranks = cut(ctxs[:, :, :, :].rearrange("p a k d -> p (a k d)"), 0, 2 * HT * NE * NE)

        in_x = [sem(f"in_x{h}") for h in range(HALF)]
        in_wq, in_wp, in_wg, in_small, in_mask, in_w12 = (
            sem("in_wq"), sem("in_wp"), sem("in_wg"), sem("in_small"), sem("in_mask"), sem("in_w12"))
        in_ctx = [sem(f"in_ctx{i}") for i in range(3)]
        in_kst = [sem(f"in_kst{i}") for i in range(3)]
        in_qst = [sem(f"in_qst{i}") for i in range(2)]
        in_ring = [sem(f"in_ring{i}") for i in range(4)]
        in_cb = [sem(f"in_cb{i}") for i in range(4)]
        parts_out = [sem(f"parts_out{i}") for i in range(NCOMP)]
        in_mrow, cscr_out, y_out = sem("in_mrow"), sem("cscr_out"), sem("y_out")
        names = ("const ones_pad tanh_g gbp_s gb_s wt_pe wt_act wt_dve ln_stats ln_rs ln_x xnt_pe xnt_act xnt_dve "
                 "qk_pe sp_hi sp_r1 sp_mid sp_lo ct_pe v_pad v_pe v_own sq_act rs_pool u_dve xb_pool "
                 "a_pe max_dve mt_pe m_hi m_lo b_pe exp_act av_pe o_act nt_pe as_dve at_pe att_act pj_pe x1_dve "
                 "hin_pe vin_pe silu_act t_dve h_dve out_pe x2_dve gt_pe th_act cmb_dve cT_pe cT_act "
                 "abs_act ws_pe ws_dve tq_dve w1t_pe w12_act w12_dve m_dve cs_pe eq_dve cnt_pe keep_pool dd_dve e_act wdep_dve "
                 "l_st l_rs l_xh l_xg xht_pe xht_act win_pe x3_dve m_st m_rs xq_dve xqt_pe xqt_act w1_pe h1_dve gelu_act "
                 "s2_dve magic_dve hr_act hq_dve hqt_pe hqt_act w2_pe l_xg2 y_dve step_dve step_pool step_act").split()
        s = {n: sem(n) for n in names}

        SPLITS = ([("qk", i) for i in range(4)] + [("ctx", 0), ("ctx", 1), ("ctx", 2)]
                  + [("qk", 4 + i) for i in range(4)] + [("ctx", c) for c in range(3, B)])
        SP_AT = {k: n for n, k in enumerate(SPLITS)}
        WRITES = [2 if kind == "ctx" else 1 if i % 4 < 2 else 3 for kind, i in SPLITS]

        def parts_written(n):
            return parts_out[n % NCOMP], 16 * sum(WRITES[k] for k in range(n % NCOMP, n + 1, NCOMP))

        def l_bank(stage, t):
            if t < HT:
                return {"xh": 6, "win": 7, "xq": 6, "w1": 6, "hq": 7, "w2": 7}[stage]
            j = t - HT
            return {"xh": j, "win": 4 + j, "xq": j, "w1": (4, 6, 0, 2)[j], "hq": 4 + j, "w2": j}[stage]

        def l_slot(e, stage):
            at = {"xh": 0, "win": 1, "xq": 2, "w1": 3, "gelu": 4, "hq": 5, "w2": 6, "pre": -1}[stage]
            t, r = divmod(e - 2 - at, 3)
            return t if r == 0 and 0 <= t < HT else None

        def qk_bank(i):
            return (4, 5, 0, 2)[i] if i < 4 else 6 + i % 2

        block = stack.enter_context(nc.Block())

        @block.sync
        def _(sp):
            def load_x(h):
                sp.dma_start(xs[0:T, h * HT:(h + 1) * HT, :],
                             x[h * HT:(h + 1) * HT].rearrange("b t c -> t b c")).then_inc(in_x[h], 16)

            load_x(0)
            wq_st = ring[:, 0:2, :].rearrange("p a c -> p (a c)").rearrange("p (i c) -> p i c", c=D)
            sp.dma_start(wq_st, w_qkv.rearrange("(i p) c -> p i c", p=128)).then_inc(in_wq, 16)

            def load_ctx(c):
                if c >= 3:
                    sp.wait_ge(s["ct_pe"], c - 2)
                    sp.wait_ge(s["v_pad"], c - 2)
                    sp.wait_ge(s["u_dve"], c - 2)
                sp.dma_start(ctxs[0:CH, c % 3, :, :],
                             ctx_in[c].rearrange("(k p) d -> p k d", p=CH)).then_inc(in_ctx[c % 3], 16)

            def write_parts(n):
                kind, i = SPLITS[n]
                sp.wait_ge(s["sp_lo"], n + 1)
                sem_, _ = parts_written(n)
                parts = comp[n % NCOMP]
                if kind == "ctx":
                    for g_ in range(2):
                        sp.dma_start(kscr[:, g_ * 128:(g_ + 1) * 128, i, 0:S].rearrange("a r t -> r a t"),
                                     parts[:, :, g_ * S:(g_ + 1) * S]).then_inc(sem_, 16)
                    return
                h, m = divmod(i, 4)
                src = parts[:, :, 0:W]
                if m < 2:
                    sp.dma_start(qscr[:, m * 128:(m + 1) * 128, h * W:(h + 1) * W].rearrange("a r t -> r a t"), src)\
                        .then_inc(sem_, 16)
                else:
                    for a_ in range(3):
                        sp.dma_start(kscr[a_, (m - 2) * 128:(m - 1) * 128, h * HT:(h + 1) * HT, S:KEYS],
                                     parts[:, a_, 0:W].rearrange("p (b t) -> p b t", b=HT)).then_inc(sem_, 16)

            def read_k(c):
                for n in [SP_AT[("ctx", c)]] + [SP_AT[("qk", 4 * (c // HT) + i)] for i in (2, 3)]:
                    sp.wait_ge(*parts_written(n))
                if c >= 3:
                    sp.wait_ge(s["exp_act"], NH * (c - 2))
                for j, part in enumerate(K_PART):
                    sp.dma_start(kst[j * DH:(j + 1) * DH, c % 3, :, 0:KEYS],
                                 kscr[part, :, c, :].rearrange("(h r) t -> r h t", r=DH)).then_inc(in_kst[c % 3], 16)

            def read_q(h):
                for i in (0, 1):
                    sp.wait_ge(*parts_written(SP_AT[("qk", 4 * h + i)]))
                for j, part in enumerate(Q_PART):
                    sp.dma_start(qst[j * DH:(j + 1) * DH, :, h * W:(h + 1) * W],
                                 qscr[part, :, h * W:(h + 1) * W].rearrange("(h r) t -> r h t", r=DH))\
                        .then_inc(in_qst[h], 16)

            def write_max(b):
                sp.wait_ge(s["m_lo"], b + 1)
                for j in range(2):
                    sp.dma_start(qst[RB + j:RB + j + 1, :, b * T:(b + 1) * T],
                                 mrow[0:NH, b % 2, j, :]).then_inc(in_mrow, 16)

            load_ctx(0)
            load_ctx(1)
            load_x(1)
            load_ctx(2)
            write_parts(0)
            write_parts(1)
            read_q(0)
            write_parts(2)
            write_parts(3)
            write_parts(4)
            read_k(0)
            write_parts(5)
            write_parts(6)
            read_k(1)
            write_max(0)
            read_k(2)
            load_ctx(3)
            for b in range(B):
                if b == 0:
                    write_parts(7)
                    write_parts(8)
                if b + 1 < B:
                    write_max(b + 1)
                if b == 1:
                    read_q(1)
                if b == 0:
                    write_parts(9)
                    write_parts(10)
                if b + 3 < B:
                    write_parts(SP_AT[("ctx", b + 3)])
                if b + 4 < B:
                    load_ctx(b + 4)
                if b + 3 < B:
                    read_k(b + 3)

            def load_ring(i):
                e = i % NU
                r = ring[:, i % 4, :]
                if i >= 4:
                    sp.wait_ge(s["out_pe"], i - 3)
                else:
                    sp.wait_ge(s["wt_act"], 4)
                    sp.wait_ge(s["wt_dve"], 3)
                if e < 2:
                    cols = slice(e * HID, (e + 1) * HID)
                    wi, vi, wo = ws_in[:, cols], vs_in[:, cols], ws_out[e * HID:(e + 1) * HID, :]
                else:
                    wi, vi, wo = e_win[e - 2], e_vin[e - 2], e_wout[e - 2]
                for k, w_ in ((0, wi), (1, vi)):
                    sp.dma_start(r[:, k * 2 * HID:(k + 1) * 2 * HID].rearrange("p (k h) -> p k h", k=2),
                                 w_.rearrange("(k p) h -> p k h", p=128)).then_inc(in_ring[i % 4], 16)
                sp.dma_start(r[:, 4 * HID:6 * HID], wo).then_inc(in_ring[i % 4], 16)

            for i in range(4):
                load_ring(i)
            sp.wait_ge(s["exp_act"], NH * B)
            for h in range(HALF):
                sp.wait_ge(s["cT_act"], h + 1)
                sp.dma_start(cscr[:, h * W:(h + 1) * W], cTs[:, :]).then_inc(cscr_out, 16)
                sp.wait_ge(cscr_out, 16 * (h + 1))
                for e in range(NU):
                    i = h * NU + e
                    if e >= 2:
                        j = h * NE + e - 2
                        if j >= 4:
                            sp.wait_ge(s["h_dve"], j - 3)
                        sp.dma_start(cb[j % 4], cscr[e - 2:e - 1, h * W:(h + 1) * W].broadcast_to([128, W]))\
                            .then_inc(in_cb[j % 4], 16)
                    if i >= 4 - 2 and i + 2 < HALF * NU and i + 2 >= 4:
                        load_ring(i + 2)
                    if i == 1:
                        sp.dma_start(w1s.rearrange("p (i c) -> p i c", i=8),
                                     w1.rearrange("(i p) c -> p i c", p=128)).then_inc(in_w12, 16)
                        sp.dma_start(w2s.rearrange("p (i c) -> p i c", i=2),
                                     w2.rearrange("(i p) c -> p i c", p=128)).then_inc(in_w12, 16)
            for t in range(B):
                sp.wait_ge(s["y_dve"], t + 1)
                sp.dma_start(out[t], xs[0:T, t, :]).then_inc(y_out, 16)
            sp.wait_ge(y_out, 16 * B)

        @block.gpsimd
        def _(pool):
            g = nc.gpsimd
            steps = [0]

            def link(ins):
                steps[0] += 1
                ins.then_inc(s["step_pool"], 1)
                pool.wait_ge(s["step_pool"], steps[0])

            for m, v in ((ident, 0.0), (identb, 0.0), (tri, 1.0), (before, 1.0)):
                last = g.memset(m[:], v)
            link(last)
            for m in (ident, identb):
                g.affine_select(out=m[:, :], in_=m[:, :], compare_op=ALU.not_equal, fill=1.0, base=0,
                                pattern=[[-1, 128]], channel_multiplier=1)
            g.affine_select(out=tri[:, :], in_=tri[:, :], compare_op=ALU.is_ge, fill=0.0, base=0,
                            pattern=[[1, 128]], channel_multiplier=-1)
            g.affine_select(out=before[:, :, :], in_=before[:, :, :], compare_op=ALU.is_gt, fill=0.0, base=0,
                            pattern=[[1, NE], [-1, NE]], channel_multiplier=0)
            g.memset(mhalf[:, :], -0.5).then_inc(s["const"], 1)
            g.memset(ones[:, :], 1.0)
            g.memset(onesb[:, :], 1.0)
            g.iota(pidx[:, :], pattern=[[0, 1]], base=0, channel_multiplier=1,
                   allow_small_or_imprecise_dtypes=True)
            g.iota(iota_t[:, :], pattern=[[1, T]], base=0, channel_multiplier=0,
                   allow_small_or_imprecise_dtypes=True).then_inc(s["const"], 1)
            pool.wait_ge(s["const"], 2)

            def ln_rs(k):
                pool.wait_ge(s["ln_stats"], k + 1)
                r = rs[0:T, k % 2]
                link(g.tensor_scalar(r[:, 0, :], mv[0:T, k % 2, :, 1], 1.0, LN_EPS, ALU.mult, ALU.add))
                g.tensor_tensor(r[:, 1, :], r[:, 0, :], mhalf[0:T, :], ALU.pow).then_inc(s["ln_rs"], 1)

            def split(n):
                width = 2 * S if SPLITS[n][0] == "ctx" else W
                pool.wait_ge(s["sp_r1"], n + 1)
                c_ = comp[n % NCOMP]
                if n < EARLY:
                    pool.wait_ge(s["sp_mid"], n + 1)
                else:
                    link(g.tensor_scalar(c_[:, 1, 0:width], r1[:, n % 2, 0:width], 1.0, 0.0, ALU.mult, ALU.add))
                g.tensor_tensor(c_[:, 2, 0:width], r1[:, n % 2, 0:width], c_[:, 1, 0:width],
                                ALU.subtract).then_inc(s["sp_lo"], 1)

            def v_pad(c):
                pool.wait_ge(in_ctx[c % 3], 16 * (c // 3 + 1))
                if c >= 2:
                    pool.wait_ge(s["av_pe"], NH * (c - 1))
                for k in range(NCH):
                    last = g.tensor_scalar(vst[0:CH, c % 2, k, :, 0:DH],
                                           ctxs[0:CH, c % 3, k, D:DC].rearrange("p (h d) -> p h d", d=DH),
                                           1.0, 0.0, ALU.mult, ALU.add)
                last.then_inc(s["v_pad"], 1)

            def patch_rs(c):
                pool.wait_ge(s["sq_act"], c + 1)
                link(g.tensor_scalar(rsc[0:T, 0, c:c + 1], ssq[0:T, c:c + 1], 1.0 / DC, LN_EPS, ALU.mult, ALU.add))
                g.tensor_tensor(rsc[0:T, 1, c:c + 1], rsc[0:T, 0, c:c + 1], mhalf[0:T, 0:1], ALU.pow)\
                    .then_inc(s["rs_pool"], 1)

            def ones_rows(c):
                g.memset(kst[RB:RB + 2, c, :, :].rearrange("p h t -> p (h t)").bitcast(F32), ONE_PAIR)\
                    .then_inc(s["ones_pad"], 1)
                pool.wait_ge(s["ones_pad"], c + 2)

            link(g.memset(kst[0:RB, :, :, KEYS:KPAD], 0.0))
            g.memset(vst[:, :, :, :, DH:32], 1.0).then_inc(s["ones_pad"], 1)
            pool.wait_ge(s["ones_pad"], 1)
            ln_rs(0)
            pool.wait_ge(s["ln_rs"], 1)
            ones_rows(0)
            for n in range(4):
                split(n)
            split(4)
            v_pad(0)
            patch_rs(0)
            for c in (1, 2):
                split(4 + c)
                patch_rs(c)
            ln_rs(1)
            pool.wait_ge(s["ln_rs"], 2)
            ones_rows(1)
            ones_rows(2)
            for b in range(B):
                if b == 0:
                    for n in range(7, 11):
                        split(n)
                if b == 1:
                    pool.wait_ge(s["gbp_s"], 1)
                    pool.wait_ge(s["ln_x"], B)
                    for t in range(B):
                        last = g.tensor_tensor(xs[0:T, t, :], xs[0:T, t, :], gbp[0:T, :], ALU.add)
                    last.then_inc(s["xb_pool"], 1)
                if b + 1 < B:
                    v_pad(b + 1)
                if b + 3 < B:
                    patch_rs(b + 3)
                    split(SP_AT[("ctx", b + 3)])
                if b == 5:
                    ln_rs(2)
            pool.wait_ge(s["exp_act"], NH * B)
            link(g.memset(keep[0:T, :], 1.0))
            g.memset(keep[0:T, :].rearrange("p (b t) -> p b t", t=T)[:, :, 0:1], 0.0).then_inc(s["keep_pool"], 1)
            ln_rs(3)

            def roots(h):
                pool.wait_ge(s["l_st"], h + 1)
                r, v = rs[0:T, h % 2], mv[0:T, h % 2, :, 1]
                link(g.tensor_scalar(r[:, 0, :], v, 1.0, LN_EPS, ALU.mult, ALU.add))
                link(g.tensor_tensor(r[:, 1, :], r[:, 0, :], mhalf[0:T, :], ALU.pow))
                link(g.tensor_tensor(r[:, 2, :], v, r[:, 1, :], ALU.mult))
                link(g.tensor_tensor(r[:, 0, :], r[:, 2, :], r[:, 1, :], ALU.mult))
                link(g.tensor_scalar(r[:, 2, :], r[:, 0, :], 1.0, LN_EPS, ALU.mult, ALU.add))
                link(g.tensor_tensor(r[:, 0, :], r[:, 2, :], mhalf[0:T, :], ALU.pow))
                g.tensor_tensor(r[:, 3, :], r[:, 0, :], r[:, 1, :], ALU.mult).then_inc(s["l_rs"], 1)

            def add_bin(t):
                pool.wait_ge(s["l_xh"], t + 1)
                g.tensor_tensor(xs[0:T, t, :], xs[0:T, t, :], gbin[0:T, :], ALU.add).then_inc(s["l_xg"], 1)

            def root(t):
                pool.wait_ge(s["m_st"], t + 1)
                c_ = lc[0:T, t % HT]
                link(g.tensor_scalar(c_[:, 2:3], c_[:, 1:2], 1.0, LN_EPS, ALU.mult, ALU.add))
                g.tensor_tensor(c_[:, 3:4], c_[:, 2:3], mhalf[0:T, 0:1], ALU.pow).then_inc(s["m_rs"], 1)

            def add_b2(t):
                pool.wait_ge(s["xq_dve"], t + 1)
                g.tensor_tensor(xs[0:T, t, :], xs[0:T, t, :], gb2[0:T, :], ALU.add).then_inc(s["l_xg2"], 1)

            roots(0)
            for e in range(NU):
                for stage, step in (("xh", add_bin), ("win", root), ("xq", add_b2)):
                    t = l_slot(e, stage)
                    if t is not None:
                        step(t)
            roots(1)
            for step in (add_bin, root, add_b2):
                for t in range(HT, B):
                    step(t)

        @block.scalar
        def _(act):
            a = nc.scalar
            act.dma_start(ring[:, 2, 0:2 * D].rearrange("p (i c) -> p i c", c=D),
                          w_proj.rearrange("(i p) c -> p i c", p=128)).then_inc(in_wp, 16)

            def row(v):
                return v.rearrange("(a n) -> a n", a=1)

            smalls = [(gates[:, 0:2], row(g_xattn)), (gates[:, 2:4], row(g_ffn)), (gbp[:, :], row(b_proj)),
                      (gbin[:, :], row(b_in)), (gb2[:, :], row(b2)), (gib[:, :], row(g_init)[:, 0:D]),
                      (b1_b[:, :], row(b1))]

            def load_small():
                act.dma_start(ring[:, 3, 0:2 * D].rearrange("p (i c) -> p i c", c=D),
                              w_in.rearrange("(i p) c -> p i c", p=128)).then_inc(in_wg, 16)
                act.dma_start(ring[0:NE, 2, 2 * D:3 * D], gate_w).then_inc(in_wg, 16)
                for dst, src in smalls:
                    act.dma_start(dst, src.broadcast_to([128, dst.shape[1]])).then_inc(in_small, 16)
                with nc.allow_non_contiguous_dma(reason="256 scales and 3000 lengths onto partitions"):
                    act.dma_start(gres[:, :], g_res.rearrange("(k p) -> p k", p=128)).then_inc(in_small, 16)
                    for k in range(NCH):
                        act.dma_start(msk[0:CH, k * B:(k + 1) * B],
                                      patch_lens[:, k * CH:(k + 1) * CH].rearrange("b p -> p b")).then_inc(in_mask, 16)

            def w_out(half_):
                act.wait_ge(s["wt_pe"], 2 * half_ + 1)
                a.activation(wT[:, 0, 512 * half_:512 * half_ + 512], bank(half_), ACT.Copy).then_inc(s["wt_act"], 1)

            def xnt(k):
                h = k % 2
                act.wait_ge(s["xnt_pe"], 2 * k + 1)
                a.activation(xnT[:, 0, h * W:(h + 1) * W], bank(6)[:, 0:W], ACT.Copy).then_inc(s["xnt_act"], 1)

            def split_hi(n):
                kind, i = SPLITS[n]
                if n >= NCOMP:
                    act.wait_ge(*parts_written(n - NCOMP))
                if kind == "ctx":
                    act.wait_ge(s["ct_pe"], i + 1)
                    a.activation(comp[n % NCOMP][:, 0, :].rearrange("p (g t) -> p g t", g=2), PS[:, 6:8, 0:S],
                                 ACT.Copy).then_inc(s["sp_hi"], 1)
                else:
                    act.wait_ge(s["qk_pe"], i + 1)
                    a.activation(comp[n % NCOMP][:, 0, 0:W], bank(qk_bank(i))[:, 0:W], ACT.Copy,
                                 scale=DH ** -0.5 if i % 4 < 2 else 1.0).then_inc(s["sp_hi"], 1)

            def split_mid(n):
                width = 2 * S if SPLITS[n][0] == "ctx" else W
                act.wait_ge(s["sp_r1"], n + 1)
                a.activation(comp[n % NCOMP][:, 1, 0:width], r1[:, n % 2, 0:width], ACT.Copy).then_inc(s["sp_mid"], 1)

            def v_own(c):
                act.wait_ge(s["v_pe"], c + 1)
                if c >= 2:
                    act.wait_ge(s["av_pe"], NH * (c - 1))
                a.activation(vst[0:T, c % 2, NCH, :, 0:DH], bank(7)[0:T, 0:D].rearrange("p (h d) -> p h d", d=DH),
                             ACT.Copy).then_inc(s["v_own"], 1)

            def square(c):
                act.wait_ge(in_ctx[c % 3], 16 * (c // 3 + 1))
                if c >= 1:
                    act.wait_ge(s["sq_act"], c)
                a.activation(sqj[0:T, :], ctxs[0:T, c % 3, 0, :], ACT.Square,
                             accum_out=ssq[0:T, c:c + 1]).then_inc(s["sq_act"], 1)

            def m_hi(b):
                act.wait_ge(s["mt_pe"], b + 1)
                if b >= 2:
                    act.wait_ge(in_mrow, 32 * (b - 1))
                a.activation(mrow[0:NH, b % 2, 0, :], bank(7)[0:NH, 0:T], ACT.Copy).then_inc(s["m_hi"], 1)

            def o_out(b):
                act.wait_ge(s["av_pe"], NH * (b + 1))
                if b >= 1:
                    act.wait_ge(s["nt_pe"], b)
                a.activation(osb[:, :], bank(5)[:, 0:W], ACT.Copy).then_inc(s["o_act"], 1)

            def att_out(b):
                act.wait_ge(s["at_pe"], b + 1)
                if b >= 1:
                    act.wait_ge(s["pj_pe"], b)
                a.activation(attT[:, :], bank(6)[:, 0:2 * T], ACT.Copy).then_inc(s["att_act"], 1)

            def gate_tanh(h):
                act.wait_ge(s["gt_pe"], h + 1)
                if h:
                    act.wait_ge(s["cmb_dve"], h)
                a.activation(gth[0:T, :, :].rearrange("p t e -> p (t e)"), bank(6)[0:T, 0:HT * NE], ACT.Tanh,
                             scale=0.5).then_inc(s["th_act"], 1)

            def rows_out(h):
                act.wait_ge(s["cT_pe"], h + 1)
                if h:
                    act.wait_ge(cscr_out, 16 * h)
                a.activation(cTs[:, :], bank(7)[0:NE, 0:W], ACT.Copy).then_inc(s["cT_act"], 1)

            w_out(0)
            xnt(0)
            w_out(1)
            load_small()
            for n in range(5):
                split_hi(n)
                if n >= 1:
                    split_mid(n - 1)
            split_mid(4)
            v_own(0)
            square(0)
            for c in (1, 2):
                split_hi(4 + c)
                square(c)
                split_mid(4 + c)
            act.wait_ge(in_small, 16 * 8)
            a.activation(tg[:, :], gates[:, :], ACT.Tanh).then_inc(s["tanh_g"], 1)
            act.wait_ge(s["wt_pe"], 5)
            for k in range(2):
                a.mul(winT[:, k, :], bank(6)[:, k * D:(k + 1) * D], gres[:, k:k + 1]).then_inc(s["wt_act"], 1)
            m_hi(0)
            for b in range(B):
                for h in range(NH):
                    if h == 1 and b >= 1:
                        o_out(b - 1)
                    n = NH * b + h
                    act.wait_ge(s["b_pe"], n + 1)
                    if n >= 4:
                        act.wait_ge(s["av_pe"], n - 3)
                    a.activation(ex[0:CH, n % 4, :], bank(2 + n % 2)[0:CH, 0:W], ACT.Exp).then_inc(s["exp_act"], 1)
                    if h == 4 and b == 0:
                        xnt(1)
                    if h == (6 if b else 5) and b + 1 < B:
                        v_own(b + 1)
                    if h in (7, 11) and b == 0:
                        for n in ((7, 8) if h == 7 else (9, 10)):
                            split_hi(n)
                    if h == 8 and b >= 1:
                        att_out(b - 1)
                    if h == 11 and b + 1 < B:
                        m_hi(b + 1)
                    if h == 13 and b + 3 < B:
                        square(b + 3)
                    if h == 0 and 1 <= b <= B - 3:
                        split_hi(SP_AT[("ctx", b + 2)])
                    if h == 14 and b == 5:
                        xnt(2)
                    if h == 14 and b == 6:
                        gate_tanh(0)
                    if h == 14 and b == 7:
                        rows_out(0)
            o_out(B - 1)
            att_out(B - 1)

            def ternary_out(k):
                act.wait_ge(s["w1t_pe"], 2 * k + 1)
                src = bank(6).bitcast(BF16)
                if k == 0:
                    a.activation(w1T[:, 0, :], src, ACT.Copy).then_inc(s["w12_act"], 1)
                else:
                    a.activation(w2T[:, :, 0:128], src.rearrange("p (k c) -> p k c", k=8), ACT.Copy)\
                        .then_inc(s["w12_act"], 1)

            def xht_out(t):
                act.wait_ge(s["xht_pe"], t + 1)
                a.activation(xhT[t % HT], bank(l_bank("xh", t))[:, 0:2 * T], ACT.Copy).then_inc(s["xht_act"], 1)

            def xqt_out(t):
                act.wait_ge(s["xqt_pe"], t + 1)
                a.activation(xqT[t % HT], bank(l_bank("xq", t)).bitcast(BF16)[:, 0:2 * T], ACT.Copy)\
                    .then_inc(s["xqt_act"], 1)

            def gelu(t):
                act.wait_ge(s["h1_dve"], t + 1)
                a.activation(h1[t % HT][0:T, :], h1[t % HT][0:T, :], ACT.Gelu).then_inc(s["gelu_act"], 1)

            def scale_up(t):
                act.wait_ge(s["s2_dve"], t + 1)
                a.activation(h1[t % HT][0:T, :], h1[t % HT][0:T, :], ACT.Identity, bias=magic[0:T, :],
                             scale=lc[0:T, t % HT, 14:15]).then_inc(s["hr_act"], 1)

            def hqt_out(t):
                act.wait_ge(s["hqt_pe"], t + 1)
                a.activation(hqT[t % HT], bank(l_bank("hq", t)).bitcast(BF16)[:, 0:8 * T], ACT.Copy)\
                    .then_inc(s["hqt_act"], 1)

            for h in range(HALF):
                for e in range(NU):
                    i = h * NU + e
                    act.wait_ge(s["hin_pe"], i + 1)
                    if i >= 2:
                        act.wait_ge(s["t_dve"], i - 1)
                    a.activation(silu_sb[i % 2], bank(2 * (i % 2))[:, 0:W], ACT.Silu).then_inc(s["silu_act"], 1)
                    if h == 0:
                        if e == 2:
                            xnt(3)
                        if e == 5:
                            gate_tanh(1)
                        if e == 8:
                            rows_out(1)
                        if e == 9:
                            act.wait_ge(in_w12, 32)
                            for k, w_ in enumerate((w1s, w2s)):
                                a.activation(junk, w_, ACT.Abs, accum_out=wabs[:, k:k + 1]).then_inc(s["abs_act"], 1)
                                act.wait_ge(s["abs_act"], k + 1)
                        if e in (12, 13):
                            ternary_out(e - 12)
                        if e == 16:
                            act.wait_ge(s["dd_dve"], 1)
                            a.activation(bm[0:T, :], keep[0:T, :], ACT.Exp, scale=-DT).then_inc(s["e_act"], 1)
                    else:
                        for stage, step in (("xh", xht_out), ("gelu", gelu), ("hq", scale_up), ("xq", xqt_out),
                                            ("hq", hqt_out)):
                            t = l_slot(e, stage)
                            if t is not None:
                                step(t)

            for stages in ((xht_out,), (xqt_out,), (gelu,), (scale_up,), (hqt_out,)):
                for t in range(HT, B):
                    for stage in stages:
                        stage(t)

        @block.tensor
        def _(pe):
            mm, tr = nc.tensor.matmul, nc.tensor.transpose
            pe.wait_ge(s["const"], 1)

            def w_t(half_):
                pe.wait_ge(in_wq, 16)
                if half_:
                    pe.wait_ge(in_wp, 16)
                for k in range(2):
                    for i in range(4):
                        blk = 4 * half_ + i
                        src = (wq_st[:, blk * D + k * 128:blk * D + (k + 1) * 128] if blk < 6 else
                               ring[:, 2, (blk - 6) * D + k * 128:(blk - 6) * D + (k + 1) * 128])
                        last = tr(bank(2 * k + half_)[:, 128 * i:128 * (i + 1)], src, ident[:, :])
                    last.then_inc(s["wt_pe"], 1)

            wq_st = ring[:, 0:2, :].rearrange("p a c -> p (a c)")

            def w_in_t():
                pe.wait_ge(in_wg, 32)
                take(6, s["wt_act"], 4)
                for k in range(2):
                    for i in range(2):
                        last = tr(bank(6)[:, k * D + 128 * i:k * D + 128 * (i + 1)],
                                  ring[:, 3, i * D + k * 128:i * D + (k + 1) * 128], ident[:, :])
                last.then_inc(s["wt_pe"], 1)
                take(7, s["wt_dve"], 3)
                for k in range(2):
                    last = tr(bank(7)[:, k * NE:(k + 1) * NE],
                              ring[0:NE, 2, 2 * D + k * 128:2 * D + (k + 1) * 128], ident[0:NE, 0:NE])
                last.then_inc(s["wt_pe"], 1)

            free = {n: None for n in range(8)}

            def take(n, *then):
                if free[n] is not None:
                    pe.wait_ge(*free[n])
                free[n] = then

            def ln_t(k):
                h = k % 2
                pe.wait_ge(s["ln_x"], HT * (k + 1))
                take(6, s["xnt_act"], k + 1)
                take(7, s["xnt_dve"], k + 1)
                for c in range(2):
                    for t in range(HT):
                        last = tr(bank(6 + c)[:, t * T:(t + 1) * T], xn[0:T, t, c * 128:(c + 1) * 128],
                                  ident[0:T, 0:T])
                    last.then_inc(s["xnt_pe"], 1)

            def xnt_ready(k):
                pe.wait_ge(s["xnt_act"], k + 1)
                pe.wait_ge(s["xnt_dve"], k + 1)

            def qk(i):
                h, m = divmod(i, 4)
                xnt_ready(h)
                if h == 0:
                    pe.wait_ge(s["wt_act"], 1)
                    pe.wait_ge(s["wt_dve"], 1)
                else:
                    take(qk_bank(i), s["sp_r1"], SP_AT[("qk", i)] + 1)
                for c in range(2):
                    last = mm(bank(qk_bank(i))[:, 0:W],
                              wT[:, c, m * 128:(m + 1) * 128],
                              xnT[:, c, h * W:(h + 1) * W], start=c == 0, stop=c == 1)
                last.then_inc(s["qk_pe"], 1)

            def ctx_t(c):
                pe.wait_ge(in_ctx[c % 3], 16 * (c // 3 + 1))
                n = SP_AT[("ctx", c)]
                take(6, s["sp_r1"], n + 1)
                take(7, s["sp_r1"], n + 1)
                for g_ in range(2):
                    for k in range(NCH):
                        last = tr(bank(6 + g_)[:, k * CH:(k + 1) * CH],
                                  ctxs[0:CH, c % 3, k, g_ * 128:(g_ + 1) * 128], ident[0:CH, 0:CH])
                last.then_inc(s["ct_pe"], 1)

            def own_v(c):
                take(7, s["v_own"], c + 1)
                for k in range(2):
                    last = mm(bank(7)[0:T, 0:D], xnT[:, k, c * T:(c + 1) * T], wT[:, k, 2 * D:3 * D],
                              start=k == 0, stop=k == 1)
                last.then_inc(s["v_pe"], 1)

            def score_rows(b, h):
                n = NH * b + h
                if h == 0:
                    pe.wait_ge(in_kst[b % 3], 96 * (b // 3 + 1))
                    pe.wait_ge(in_qst[b // HT], 96)
                if n >= 3:
                    pe.wait_ge(s["max_dve"], n - 2)
                mm(bank(SCORE_ROWS[n % 3])[0:T, 0:KEYS], qst[0:RB, h, b * T:(b + 1) * T], kst[0:RB, b % 3, h, 0:KEYS],
                   start=True, stop=True).then_inc(s["a_pe"], 1)

            def max_t(b):
                take(7, s["m_lo"], b + 1)
                pe.wait_ge(s["max_dve"], NH * (b + 1))
                tr(bank(7)[0:NH, 0:T], nm[0:T, b % 2, :], ident[0:T, 0:T]).then_inc(s["mt_pe"], 1)

            def score_cols(b, h):
                n = NH * b + h
                if h == 0:
                    pe.wait_ge(in_mrow, 32 * (b + 1))
                    pe.wait_ge(s["ones_pad"], (2, 3, 4)[min(b, 2)])
                if n >= 2:
                    pe.wait_ge(s["exp_act"], n - 1)
                for c in range(NCH + 1):
                    last = mm(bank(2 + n % 2)[0:CH, c * T:(c + 1) * T],
                              kst[0:RB + 2, b % 3, h, c * CH:(c + 1) * CH],
                              qst[0:RB + 2, h, b * T:(b + 1) * T], start=True, stop=True)
                last.then_inc(s["b_pe"], 1)

            def values(b, h):
                n = NH * b + h
                j, i = h % 4, h // 4
                if h == 0:
                    pe.wait_ge(s["v_pad"], b + 1)
                    pe.wait_ge(s["v_own"], b + 1)
                    if b >= 1:
                        pe.wait_ge(s["o_act"], b)
                pe.wait_ge(s["exp_act"], n + 1)
                for c in range(NCH + 1):
                    rows = CH if c < NCH else T
                    last = mm(bank(5)[32 * j:32 * j + 32, i * T:(i + 1) * T], vst[0:rows, b % 2, c, h, :],
                              ex[0:rows, n % 4, c * T:(c + 1) * T], start=c == 0, stop=c == NCH)
                last.then_inc(s["av_pe"], 1)

            def norm_t(b):
                pe.wait_ge(s["o_act"], b + 1)
                take(6, s["as_dve"], b + 1)
                for i in range(4):
                    last = tr(bank(6)[0:T, 128 * i:128 * (i + 1)], osb[:, i * T:(i + 1) * T], ident[:, :])
                last.then_inc(s["nt_pe"], 1)

            def att_t(b):
                take(6, s["att_act"], b + 1)
                att = asb[0:T, :, :].rearrange("p h d -> p (h d)")
                for k in range(2):
                    last = tr(bank(6)[:, k * T:(k + 1) * T], att[:, k * 128:(k + 1) * 128], ident[0:T, 0:T])
                last.then_inc(s["at_pe"], 1)

            def project(b):
                take(6, s["x1_dve"], b + 1)
                for k in range(2):
                    last = mm(bank(6)[0:T, 0:D], attT[:, k * T:(k + 1) * T], wT[:, k, 3 * D:4 * D],
                              start=k == 0, stop=k == 1)
                last.then_inc(s["pj_pe"], 1)

            def gate_logits(h):
                take(6, s["th_act"], h + 1)
                pe.wait_ge(s["wt_dve"], 3)
                xnt_ready(2 + h)
                for t in range(HT):
                    for k in range(2):
                        at = h * W + t * T
                        last = mm(bank(6)[0:T, t * NE:(t + 1) * NE], xnT[:, k, at:at + T], gateT[:, k, :],
                                  start=k == 0, stop=k == 1)
                last.then_inc(s["gt_pe"], 1)

            def combine_t(h):
                take(7, s["cT_act"], h + 1)
                pe.wait_ge(s["cmb_dve"], h + 1)
                for t in range(HT):
                    last = tr(bank(7)[0:NE, t * T:(t + 1) * T], gsg[0:T, t, :], ident[0:T, 0:T])
                last.then_inc(s["cT_pe"], 1)

            w_t(0)
            ln_t(0)
            w_t(1)
            for i in range(4):
                qk(i)
            ctx_t(0)
            pe.wait_ge(s["wt_act"], 2)
            pe.wait_ge(s["wt_dve"], 2)
            own_v(0)
            ctx_t(1)
            ctx_t(2)
            w_in_t()
            pe.wait_ge(s["sp_r1"], 4)
            for h in range(NH):
                score_rows(0, h)
            max_t(0)
            for b in range(B):
                for h in range(NH):
                    if b + 1 < B:
                        for j in range(min(5 * h // 3, NH), min(5 * (h + 1) // 3, NH)):
                            score_rows(b + 1, j)
                    score_cols(b, h)
                    if h >= 2:
                        values(b, h - 2)
                    if h == 2 and b == 0:
                        ln_t(1)
                    if h == 4 and b >= 1:
                        norm_t(b - 1)
                    if h == (5 if b else 3) and b + 1 < B:
                        own_v(b + 1)
                    if h in (5, 10) and b == 0:
                        for i in ((4, 5) if h == 5 else (6, 7)):
                            qk(i)
                    if h == 7 and b >= 1:
                        att_t(b - 1)
                    if h == 10 and b >= 1:
                        project(b - 1)
                    if h == 11 and b + 1 < B:
                        max_t(b + 1)
                    if h == 13 and b == 5:
                        ln_t(2)
                    if h == 13 and b == 6:
                        gate_logits(0)
                    if h == 13 and b == 7:
                        combine_t(0)
                if b + 3 < B:
                    ctx_t(b + 3)
                values(b, NH - 2)
                values(b, NH - 1)
            norm_t(B - 1)
            att_t(B - 1)
            project(B - 1)

            def up(i):
                h = i // NU
                r = ring[:, i % 4, :]
                xnt_ready(2 + h)
                pe.wait_ge(in_ring[i % 4], 48 * (i // 4 + 1))
                if i >= 2:
                    pe.wait_ge(s["t_dve"], i - 1)
                for v, name in ((0, "hin_pe"), (1, "vin_pe")):
                    for k in range(2):
                        last = mm(bank(2 * (i % 2) + v)[:, 0:W], r[:, (2 * v + k) * HID:(2 * v + k + 1) * HID],
                                  xnT[:, k, h * W:(h + 1) * W], start=k == 0, stop=k == 1)
                    last.then_inc(s[name], 1)

            def down(i):
                h, e = divmod(i, NU)
                if e == 0:
                    if h:
                        pe.wait_ge(s["x2_dve"], HT * h)
                if e < 2:
                    pe.wait_ge(s["t_dve"], i + 1)
                else:
                    pe.wait_ge(s["h_dve"], h * NE + e - 1)
                for t in range(HT):
                    last = mm(bank(4 + t // 2)[0:T, (t % 2) * D:(t % 2 + 1) * D], h_sb[i % 2][:, t * T:(t + 1) * T],
                              ring[:, i % 4, 4 * HID:6 * HID], start=e == 0 and t % 2 == 0, stop=e == NU - 1,
                              skip_group_check=True)
                last.then_inc(s["out_pe"], 1)

            def sums_of_abs():
                take(6, s["ws_dve"], 1)
                pe.wait_ge(s["abs_act"], 2)
                mm(bank(6)[:, 0:2], ones[:, :], wabs[:, :], start=True, stop=True).then_inc(s["ws_pe"], 1)

            def ternary_t(k):
                pe.wait_ge(s["tq_dve"], k + 1)
                take(6, s["w12_act"], k + 1)
                take(7, s["w12_dve"], k + 1)
                for c in range(2):
                    for i in range(8):
                        src = (tq1[:, i * D + c * 128:i * D + (c + 1) * 128] if k == 0 else
                               tq2[:, c * H4 + i * 128:c * H4 + (i + 1) * 128])
                        last = tr(bank(6 + c).bitcast(BF16)[:, i * 128:(i + 1) * 128], src, identb[:, :])
                    last.then_inc(s["w1t_pe"], 1)

            def patch_ends():
                take(6, s["eq_dve"], 1)
                pe.wait_ge(s["m_dve"], 1)
                for c in range(NCH):
                    for k in range(c + 1):
                        last = mm(bank(6)[0:CH, c * B:(c + 1) * B], (tri if k == c else ones)[0:CH, 0:CH],
                                  mskf[0:CH, k * B:(k + 1) * B], start=k == 0, stop=k == c)
                last.then_inc(s["cs_pe"], 1)

            def end_counts():
                pe.wait_ge(s["eq_dve"], 2)
                take(6, s["dd_dve"], 1)
                take(7, s["dd_dve"], 1)
                for h in range(HALF):
                    for c in range(NCH):
                        last = mm(bank(6 + h)[0:T, 0:W], onesb[0:CH, 0:T],
                                  eqm[0:CH, c * B * T + h * W:c * B * T + (h + 1) * W], start=c == 0, stop=c == NCH - 1)
                last.then_inc(s["cnt_pe"], 1)

            def xh_t(t):
                n = l_bank("xh", t)
                pe.wait_ge(s["l_xh"], t + 1)
                take(n, s["xht_act"], t + 1)
                for c in range(2):
                    last = tr(bank(n)[:, c * T:(c + 1) * T], xh[t % HT][0:T, c * 128:(c + 1) * 128], ident[0:T, 0:T])
                last.then_inc(s["xht_pe"], 1)

            def win_depool(t):
                n = l_bank("win", t)
                take(n, s["x3_dve"], t + 1)
                pe.wait_ge(s["u_dve"], B)
                pe.wait_ge(s["wdep_dve"], 1)
                mm(bank(n)[0:T, 0:D], wdep[0:T, t * T:(t + 1) * T], u[0:T, t, :], start=True, stop=False)
                pe.wait_ge(s["xht_act"], t + 1)
                for c in range(2):
                    last = mm(bank(n)[0:T, 0:D], xhT[t % HT][:, c * T:(c + 1) * T], winT[:, c, :],
                              start=False, stop=c == 1)
                last.then_inc(s["win_pe"], 1)

            def xq_t(t):
                n = l_bank("xq", t)
                pe.wait_ge(s["xq_dve"], t + 1)
                take(n, s["xqt_act"], t + 1)
                for c in range(2):
                    last = tr(bank(n).bitcast(BF16)[:, c * T:(c + 1) * T], xq[t % HT][0:T, c * 128:(c + 1) * 128],
                              identb[0:T, 0:T])
                last.then_inc(s["xqt_pe"], 1)

            def w1_up(t):
                n = l_bank("w1", t)
                pe.wait_ge(s["xqt_act"], t + 1)
                pe.wait_ge(s["w12_act"], 2)
                pe.wait_ge(s["w12_dve"], 2)
                for half_ in range(2):
                    take(n + half_, s["h1_dve"], t + 1)
                    for c in range(2):
                        last = mm(bank(n + half_)[0:T, :], xqT[t % HT][:, c * T:(c + 1) * T],
                                  w1T[:, c, half_ * 512:(half_ + 1) * 512], start=c == 0, stop=c == 1)
                last.then_inc(s["w1_pe"], 1)

            def hq_t(t):
                n = l_bank("hq", t)
                pe.wait_ge(s["hq_dve"], t + 1)
                take(n, s["hqt_act"], t + 1)
                for c in range(8):
                    last = tr(bank(n).bitcast(BF16)[:, c * T:(c + 1) * T], hq[t % HT][0:T, c * 128:(c + 1) * 128],
                              identb[0:T, 0:T])
                last.then_inc(s["hqt_pe"], 1)

            def w2_down(t):
                n = l_bank("w2", t)
                pe.wait_ge(s["hqt_act"], t + 1)
                take(n, s["y_dve"], t + 1)
                for c in range(8):
                    last = mm(bank(n)[0:T, 0:D], hqT[t % HT][:, c * T:(c + 1) * T], w2T[:, c, :],
                              start=c == 0, stop=c == 7)
                last.then_inc(s["w2_pe"], 1)

            def l_steps(e, *steps):
                for stage, step in steps:
                    t = l_slot(e, stage)
                    if t is not None:
                        step(t)

            for h in range(HALF):
                for e in range(NU):
                    i = h * NU + e
                    up(i)
                    if h == 1:
                        l_steps(e, ("xh", xh_t), ("w2", w2_down), ("win", win_depool), ("xq", xq_t))
                    if e >= 1:
                        down(i - 1)
                    if h == 1:
                        l_steps(e, ("w1", w1_up), ("hq", hq_t))
                    if h == 0:
                        if e == 2:
                            ln_t(3)
                        if e == 5:
                            gate_logits(1)
                        if e == 8:
                            combine_t(1)
                        if e == 10:
                            sums_of_abs()
                        if e in (12, 13):
                            ternary_t(e - 12)
                        if e == 14:
                            patch_ends()
                        if e == 15:
                            end_counts()
                down(h * NU + NU - 1)

            pe.wait_ge(s["x2_dve"], B)
            pe.wait_ge(s["t_dve"], HALF * NU)
            for step in (xh_t, win_depool, xq_t, w1_up, hq_t, w2_down):
                for t in range(HT, B):
                    step(t)

        @block.vector
        def _(dve):
            v = nc.vector
            steps = [0]

            def link(ins):
                steps[0] += 1
                ins.then_inc(s["step_dve"], 1)
                dve.wait_ge(s["step_dve"], steps[0])

            def ln_stats(k, name="ln_stats"):
                h = k % 2
                for t in range(HT):
                    last = v.bn_stats(stats[0:T, h, t, :], xs[0:T, h * HT + t, :])
                link(last)
                for t in range(HT):
                    last = v.bn_aggr(mv[0:T, h, t, :], stats[0:T, h, t, :])
                last.then_inc(s[name], 1)
                dve.wait_ge(s[name], k + 1 if name == "ln_stats" else h + 1)

            def ln_x(k):
                h = k % 2
                dve.wait_ge(s["ln_rs"], k + 1)
                if k >= 1:
                    dve.wait_ge(s["xnt_pe"], 2 * k)
                for t in range(HT):
                    v.tensor_scalar(xn[0:T, t, :], xs[0:T, h * HT + t, :], mv[0:T, h, t, 0:1], rs[0:T, h, 1, t:t + 1],
                                    ALU.subtract, ALU.mult).then_inc(s["ln_x"], 1)

            def xnt(k):
                h = k % 2
                dve.wait_ge(s["xnt_pe"], 2 * k + 2)
                v.tensor_copy(xnT[:, 1, h * W:(h + 1) * W], bank(7)[:, 0:W]).then_inc(s["xnt_dve"], 1)

            def split_r1(n):
                kind, i = SPLITS[n]
                dve.wait_ge(s["sp_hi"], n + 1)
                if n >= 2:
                    dve.wait_ge(s["sp_lo"], n - 1)
                hi = comp[n % NCOMP][:, 0, :]
                if kind == "ctx":
                    v.tensor_tensor(r1[:, n % 2, :].rearrange("p (g t) -> p g t", g=2), PS[:, 6:8, 0:S],
                                    hi.rearrange("p (g t) -> p g t", g=2), ALU.subtract).then_inc(s["sp_r1"], 1)
                else:
                    v.scalar_tensor_tensor(out=r1[:, n % 2, 0:W], in0=bank(qk_bank(i))[:, 0:W],
                                           scalar=DH ** -0.5 if i % 4 < 2 else 1.0, in1=hi[:, 0:W],
                                           op0=ALU.mult, op1=ALU.subtract).then_inc(s["sp_r1"], 1)

            def patches(c):
                dve.wait_ge(s["rs_pool"], c + 1)
                v.scalar_tensor_tensor(out=u[0:T, c, :], in0=ctxs[0:T, c % 3, 0, 0:D], scalar=rsc[0:T, 1, c:c + 1],
                                       in1=gib[0:T, :], op0=ALU.mult, op1=ALU.mult).then_inc(s["u_dve"], 1)

            def row_max(b, h):
                n = NH * b + h
                dve.wait_ge(s["a_pe"], n + 1)
                if h == 0 and b >= 2:
                    dve.wait_ge(s["mt_pe"], b - 1)
                v.tensor_reduce(nm[0:T, b % 2, h:h + 1], bank(SCORE_ROWS[n % 3])[0:T, 0:KEYS], AX.X, ALU.max,
                                negate=True).then_inc(s["max_dve"], 1)

            def m_lo(b):
                dve.wait_ge(s["m_hi"], b + 1)
                v.tensor_tensor(mrow[0:NH, b % 2, 1, :], bank(7)[0:NH, 0:T], mrow[0:NH, b % 2, 0, :],
                                ALU.subtract).then_inc(s["m_lo"], 1)

            def normalise(b):
                dve.wait_ge(s["nt_pe"], b + 1)
                o = bank(6)[0:T, :].rearrange("p (h d) -> p h d", d=32)
                if b >= 1:
                    dve.wait_ge(s["as_dve"], b)
                link(v.reciprocal(rinv[0:T, :], o[:, :, DH]))
                if b >= 1:
                    dve.wait_ge(s["at_pe"], b)
                v.tensor_tensor(asb[0:T, :, :], o[:, :, 0:DH],
                                rinv[0:T, :].unsqueeze(2).broadcast_to([T, NH, DH]), ALU.mult)\
                    .then_inc(s["as_dve"], 1)

            def residual1(b):
                dve.wait_ge(s["pj_pe"], b + 1)
                dve.wait_ge(s["xb_pool"], 1)
                v.scalar_tensor_tensor(out=xs[0:T, b, :], in0=bank(6)[0:T, 0:D], scalar=tg[0:T, 0:1],
                                       in1=xs[0:T, b, :], op0=ALU.mult, op1=ALU.add).then_inc(s["x1_dve"], 1)

            def gate_weights(h):
                dve.wait_ge(s["th_act"], h + 1)
                dve.wait_ge(s["v_pad"], B)
                dve.wait_ge(s["ct_pe"], B)
                if h:
                    dve.wait_ge(s["cT_pe"], h)
                g_ = gth[0:T, :, :]
                link(v.tensor_scalar(g_, g_, 0.5, 0.5, ALU.mult, ALU.add))
                n = HT * NE * NE
                cmp, eq = ranks[0:T, 0:n], ranks[0:T, n:2 * n]
                for t in range(HT):
                    gj = g_[:, t, :].unsqueeze(1).broadcast_to([T, NE, NE])
                    ge = g_[:, t, :].unsqueeze(2).broadcast_to([T, NE, NE])
                    sl = slice(t * NE * NE, (t + 1) * NE * NE)
                    v.tensor_tensor(cmp[:, sl].rearrange("p (e j) -> p e j", e=NE), gj, ge, ALU.is_gt)
                    last = v.tensor_tensor(eq[:, sl].rearrange("p (e j) -> p e j", e=NE), gj, ge, ALU.is_equal)
                link(last)
                link(v.tensor_tensor(eq.rearrange("p (t n) -> p t n", t=HT), eq.rearrange("p (t n) -> p t n", t=HT),
                                     before[0:T, :, :].rearrange("p e j -> p (e j)").unsqueeze(1)
                                     .broadcast_to([T, HT, NE * NE]), ALU.mult))
                link(v.tensor_tensor(cmp, cmp, eq, ALU.add))
                rk = ranks[0:T, n:n + HT * NE]
                link(v.tensor_reduce(rk, cmp.rearrange("p (a j) -> p a j", j=NE), AX.X, ALU.add))
                flat = gsg[0:T, :, :].rearrange("p t e -> p (t e)")
                link(v.scalar_tensor_tensor(out=flat, in0=rk, scalar=float(TOPK), in1=g_.rearrange("p t e -> p (t e)"),
                                            op0=ALU.is_lt, op1=ALU.mult))
                link(v.tensor_reduce(gsum[0:T, 0, :], gsg[0:T, :, :], AX.X, ALU.add))
                link(v.reciprocal(gsum[0:T, 1, :], gsum[0:T, 0, :]))
                v.tensor_tensor(gsg[0:T, :, :], gsg[0:T, :, :],
                                gsum[0:T, 1, :].unsqueeze(2).broadcast_to([T, HT, NE]), ALU.mult)\
                    .then_inc(s["cmb_dve"], 1)
                dve.wait_ge(s["cmb_dve"], h + 1)

            def w_out(half_):
                dve.wait_ge(s["wt_pe"], 2 * half_ + 2)
                v.tensor_copy(wT[:, 1, 512 * half_:512 * (half_ + 1)], bank(2 + half_)).then_inc(s["wt_dve"], 1)

            v.memset(magic[:, :], MAGIC)
            dve.wait_ge(in_x[0], 16)
            ln_stats(0)
            ln_x(0)
            w_out(0)
            xnt(0)
            w_out(1)
            for n in range(5):
                split_r1(n)
            split_r1(5)
            split_r1(6)
            dve.wait_ge(in_x[1], 16)
            ln_stats(1)
            dve.wait_ge(s["tanh_g"], 1)
            link(v.tensor_scalar(gbp[:, :], gbp[:, :], tg[:, 0:1], None, ALU.mult))
            v.tensor_scalar(gib[:, :], gib[:, :], BCOEF, None, ALU.mult)
            v.tensor_scalar(gbin[:, :], gbin[:, :], tg[:, 1:2], None, ALU.mult)
            v.tensor_scalar(gb2[:, :], gb2[:, :], tg[:, 3:4], None, ALU.mult).then_inc(s["gbp_s"], 1)
            dve.wait_ge(s["gbp_s"], 1)
            for c in range(3):
                patches(c)
            dve.wait_ge(s["wt_pe"], 6)
            v.tensor_copy(gateT[:, :, :], bank(7)[:, 0:2 * NE].rearrange("p (k e) -> p k e", k=2))\
                .then_inc(s["wt_dve"], 1)
            ln_x(1)
            for h in range(NH):
                row_max(0, h)
            m_lo(0)
            for b in range(B):
                for h in range(NH):
                    if b + 1 < B:
                        row_max(b + 1, h)
                    if b == 0 and h == 5:
                        xnt(1)
                    if b == 0 and h == 11:
                        split_r1(7)
                        split_r1(8)
                    if h == 4 and 1 <= b <= B - 3:
                        split_r1(SP_AT[("ctx", b + 2)])
                    if h == 5 and b == 5:
                        dve.wait_ge(s["x1_dve"], HT)
                        ln_stats(2)
                    if h == 9 and b >= 1:
                        normalise(b - 1)
                    if h == 8 and b == 5:
                        ln_x(2)
                    if h == 12 and 1 <= b and b + 2 < B:
                        patches(b + 2)
                if b == 0:
                    split_r1(9)
                    split_r1(10)
                if b >= 1:
                    residual1(b - 1)
                if b + 1 < B:
                    m_lo(b + 1)
                if b == 5:
                    xnt(2)
                if b == 6:
                    gate_weights(0)
            normalise(B - 1)
            residual1(B - 1)
            dve.wait_ge(s["x1_dve"], B)
            ln_stats(3)
            ln_x(3)
            dve.wait_ge(in_mask, 16 * NCH)
            v.tensor_copy(mskf[0:CH, :], msk[0:CH, :]).then_inc(s["m_dve"], 1)

            def ternary():
                dve.wait_ge(s["ws_pe"], 1)
                v.tensor_scalar(wsc[:, 0, :], bank(6)[:, 0:2], 1.0 / (H4 * D), Q_EPS, ALU.mult, ALU.max)\
                    .then_inc(s["ws_dve"], 1)
                dve.wait_ge(s["ws_dve"], 1)
                v.tensor_scalar(wsc[:, 1, :], wsc[:, 0, :], 0.5, None, ALU.mult)
                v.tensor_scalar(wsc[:, 2, :], wsc[:, 0, :], -0.5, None, ALU.mult)
                link(v.tensor_scalar(wsc[:, 3, :], wsc[:, 0, :], -1.0 / QB, None, ALU.mult))
                v.tensor_scalar(wsc[:, 4, 0:1], wsc[:, 3, 0:1], 1.0, None, ALU.mult)
                link(v.tensor_scalar(wsc[:, 4, 1:2], wsc[:, 3, 1:2], tg[:, 3:4], None, ALU.mult))
                for k, (w_, q_) in enumerate(((w1s, tq1), (w2s, tq2))):
                    big = junk[:, k * 1024:(k + 1) * 1024].bitcast(BF16)
                    link(v.tensor_scalar(big, w_, wsc[:, 1, k:k + 1], None, ALU.is_gt))
                    v.scalar_tensor_tensor(out=q_, in0=w_, scalar=wsc[:, 2, k:k + 1], in1=big,
                                           op0=ALU.is_lt, op1=ALU.subtract).then_inc(s["tq_dve"], 1)

            def ternary_out(k):
                dve.wait_ge(s["w1t_pe"], 2 * k + 2)
                src = bank(7).bitcast(BF16)
                if k == 0:
                    v.tensor_copy(w1T[:, 1, :], src).then_inc(s["w12_dve"], 1)
                else:
                    v.tensor_copy(w2T[:, :, 128:256], src.rearrange("p (k c) -> p k c", k=8)).then_inc(s["w12_dve"], 1)

            def ends_at():
                dve.wait_ge(s["cs_pe"], 1)
                i0, i1 = idx[0:CH, 0, :], idx[0:CH, 1, :]
                v.tensor_scalar(i0, bank(6)[0:CH, 0:NCH * B], 1.0, None, ALU.subtract).then_inc(s["eq_dve"], 1)
                dve.wait_ge(s["eq_dve"], 1)
                link(v.tensor_scalar(i1, i0, 0.0, float(T), ALU.is_lt, ALU.mult))
                link(v.tensor_tensor(i0, i0, i1, ALU.add))
                n = NCH * B
                v.tensor_tensor(eqm[0:CH, :].rearrange("p (n t) -> p n t", n=n),
                                iota_t[0:CH, :].unsqueeze(1).broadcast_to([CH, n, T]),
                                i0.unsqueeze(2).broadcast_to([CH, n, T]), ALU.is_equal).then_inc(s["eq_dve"], 1)

            def distance():
                dve.wait_ge(s["cnt_pe"], 1)
                dve.wait_ge(s["keep_pool"], 1)
                bm_, kp, wd = bm[0:T, :], keep[0:T, :], wdep[0:T, :]
                link(v.tensor_scalar(bm_.rearrange("p (a t) -> p a t", a=2), PS[0:T, 6:8, 0:W], 1.0, None, ALU.min))
                link(v.tensor_tensor_scan(wd, kp, bm_, 0.0, ALU.mult, ALU.add))
                link(v.tensor_scalar(wd, wd, -1.0, 0.0, ALU.add, ALU.max))
                link(v.tensor_scalar(wd, wd, pidx[0:T, :], None, ALU.subtract))
                v.tensor_scalar(kp, wd, 0.0, None, ALU.max).then_inc(s["dd_dve"], 1)

            def depool_weights():
                dve.wait_ge(s["e_act"], 1)
                v.scalar_tensor_tensor(out=wdep[0:T, :], in0=wdep[0:T, :], scalar=0.0, in1=bm[0:T, :],
                                       op0=ALU.is_ge, op1=ALU.mult).then_inc(s["wdep_dve"], 1)

            def hidden(i):
                h, e = divmod(i, NU)
                dve.wait_ge(s["vin_pe"], i + 1)
                dve.wait_ge(s["silu_act"], i + 1)
                shared = e < 2
                if shared and i >= 2:
                    dve.wait_ge(s["out_pe"], i - 1)
                dst = h_sb[i % 2] if shared else t_sb[i % 2]
                v.tensor_tensor(dst, bank(2 * (i % 2) + 1)[:, 0:W], silu_sb[i % 2], ALU.mult)\
                    .then_inc(s["t_dve"], 1)
                if shared:
                    return
                j = h * NE + e - 2
                dve.wait_ge(s["t_dve"], i + 1)
                dve.wait_ge(in_cb[j % 4], 16 * (j // 4 + 1))
                if i >= 2:
                    dve.wait_ge(s["out_pe"], i - 1)
                v.tensor_tensor(h_sb[i % 2], t_sb[i % 2], cb[j % 4], ALU.mult).then_inc(s["h_dve"], 1)

            def residual2(t):
                h, k = divmod(t, HT)
                dve.wait_ge(s["out_pe"], NU * (h + 1))
                v.scalar_tensor_tensor(out=xs[0:T, t, :], in0=bank(4 + k // 2)[0:T, (k % 2) * D:(k % 2 + 1) * D],
                                       scalar=tg[0:T, 2:3], in1=xs[0:T, t, :], op0=ALU.mult, op1=ALU.add)\
                    .then_inc(s["x2_dve"], 1)

            def stage_a(t):
                h = t // HT
                dve.wait_ge(s["l_rs"], h + 1)
                v.tensor_scalar(xh[t % HT][0:T, :], xs[0:T, t, :], mv[0:T, h, t % HT, 0:1],
                                rs[0:T, h, 3, t % HT:t % HT + 1], ALU.subtract, ALU.mult).then_inc(s["l_xh"], 1)

            def stage_b(t):
                dve.wait_ge(s["win_pe"], t + 1)
                dve.wait_ge(s["l_xg"], t + 1)
                c_ = lc[0:T, t % HT]
                v.scalar_tensor_tensor(out=xs[0:T, t, :], in0=bank(l_bank("win", t))[0:T, 0:D], scalar=tg[0:T, 1:2],
                                       in1=xs[0:T, t, :], op0=ALU.mult, op1=ALU.add).then_inc(s["x3_dve"], 1)
                dve.wait_ge(s["x3_dve"], t + 1)
                link(v.bn_stats(c_[:, 16:22], xs[0:T, t, :]))
                v.bn_aggr(c_[:, 0:2], c_[:, 16:22]).then_inc(s["m_st"], 1)

            def stage_c(t):
                dve.wait_ge(s["m_st"], t + 1)
                dve.wait_ge(s["m_rs"], t + 1)
                c_, f = lc[0:T, t % HT], qf[t % HT][0:T, :]
                link(v.tensor_scalar(f, xs[0:T, t, :], c_[:, 0:1], c_[:, 3:4], ALU.subtract, ALU.mult))
                link(v.tensor_reduce(c_[:, 4:5], f, AX.X, ALU.max, apply_absolute_value=True))
                link(v.tensor_scalar(c_[:, 5:6], c_[:, 4:5], Q_EPS, None, ALU.max))
                link(v.reciprocal(c_[:, 6:7], c_[:, 5:6]))
                v.tensor_tensor(c_[:, 8:9], c_[:, 5:6], wsc[0:T, 4, 0:1], ALU.mult)
                link(v.tensor_scalar(c_[:, 7:8], c_[:, 6:7], QB, None, ALU.mult))
                link(v.tensor_scalar(f, f, c_[:, 7:8], MAGIC, ALU.mult, ALU.add))
                v.tensor_scalar(xq[t % HT][0:T, :], f, MAGIC, QB, ALU.subtract, ALU.min).then_inc(s["xq_dve"], 1)

            def stage_d(t):
                n = l_bank("w1", t)
                dve.wait_ge(s["w1_pe"], t + 1)
                dve.wait_ge(s["xq_dve"], t + 1)
                v.scalar_tensor_tensor(out=h1[t % HT][0:T, :].rearrange("p (a n) -> p a n", a=2),
                                       in0=PS[0:T, n:n + 2, :], scalar=lc[0:T, t % HT, 8:9],
                                       in1=b1_b[0:T, :].rearrange("p (a n) -> p a n", a=2),
                                       op0=ALU.mult, op1=ALU.add).then_inc(s["h1_dve"], 1)

            def stage_e(t):
                c_ = lc[0:T, t % HT]
                dve.wait_ge(s["gelu_act"], t + 1)
                link(v.tensor_reduce(c_[:, 10:11], h1[t % HT][0:T, :], AX.X, ALU.max, apply_absolute_value=True))
                link(v.tensor_scalar(c_[:, 11:12], c_[:, 10:11], Q_EPS, None, ALU.max))
                link(v.reciprocal(c_[:, 12:13], c_[:, 11:12]))
                v.tensor_tensor(c_[:, 13:14], c_[:, 11:12], wsc[0:T, 4, 1:2], ALU.mult)
                v.tensor_scalar(c_[:, 14:15], c_[:, 12:13], QB, None, ALU.mult).then_inc(s["s2_dve"], 1)

            def stage_f(t):
                dve.wait_ge(s["s2_dve"], t + 1)
                dve.wait_ge(s["hr_act"], t + 1)
                v.tensor_scalar(hq[t % HT][0:T, :], h1[t % HT][0:T, :], MAGIC, QB, ALU.subtract, ALU.min)\
                    .then_inc(s["hq_dve"], 1)

            def stage_g(t):
                dve.wait_ge(s["w2_pe"], t + 1)
                dve.wait_ge(s["l_xg2"], t + 1)
                v.scalar_tensor_tensor(out=xs[0:T, t, :], in0=bank(l_bank("w2", t))[0:T, 0:D],
                                       scalar=lc[0:T, t % HT, 13:14], in1=xs[0:T, t, :],
                                       op0=ALU.mult, op1=ALU.add).then_inc(s["y_dve"], 1)

            def l_steps(e, *steps):
                for stage, step in steps:
                    t = l_slot(e, stage)
                    if t is not None:
                        step(t)

            for h in range(HALF):
                for e in range(NU):
                    hidden(h * NU + e)
                    if h == 0:
                        if e == 2:
                            xnt(3)
                        if e == 6:
                            gate_weights(1)
                        if e == 10:
                            ternary()
                        if e in (12, 13):
                            ternary_out(e - 12)
                        if e == 14:
                            ends_at()
                        if e == 15:
                            distance()
                        if e == 17:
                            depool_weights()
                    else:
                        l_steps(e, ("w2", stage_g), ("win", stage_b), ("gelu", stage_e), ("win", stage_c),
                                ("hq", stage_f), ("pre", stage_a), ("w1", stage_d))
                for t in range(h * HT, (h + 1) * HT):
                    residual2(t)
                dve.wait_ge(s["x2_dve"], HT * (h + 1))
                ln_stats(h, "l_st")
            for step in (stage_a, stage_b, stage_c, stage_d, stage_e, stage_f, stage_g):
                for t in range(HT, B):
                    step(t)


_INS = ['x', 'ctx_2048', 'mask_BxS2_if0', 'g_xattn', 'g_ffn', 'L0_xattn_w_qkv', 'L0_xattn_w_proj', 'L0_xattn_b_proj',
        'L0_ffn_gate_w', 'L0_ffn_ws_in', 'L0_ffn_vs_in', 'L0_ffn_ws_out', 'L0_ffn_e_win', 'L0_ffn_e_vin',
        'L0_ffn_e_wout', 'L1_xattn_W_in', 'L1_xattn_b_in', 'L1_xattn_g_res', 'L1_xattn_g_init', 'L1_ffn_W1',
        'L1_ffn_b1', 'L1_ffn_W2', 'L1_ffn_b2']


def kernel(**inputs):
    import numpy as _np
    import concourse.bacc as _bacc
    from concourse import mybir as _mybir
    from concourse.bass_utils import run_bass_kernel_spmd as _run

    nc = _bacc.Bacc("TRN2", target_bir_lowering=False, num_devices=1)
    arrays, args = {}, []
    for name in _INS:
        a = _np.ascontiguousarray(inputs[name])
        arrays[f"in_{name}_dram"] = a
        args.append(nc.dram_tensor(f"in_{name}_dram", a.shape, _mybir.dt.from_np(a.dtype), kind="ExternalInput").ap())
    args.append(nc.dram_tensor("out_0_dram", (B, T, D), F32, kind="ExternalOutput").ap())
    flamingo(nc, *args)
    r = _run(nc, [arrays], core_ids=[0])
    return r.results[0]["out_0_dram"]
```

```python
import math
import struct
from contextlib import ExitStack

import concourse.bass as bass
import concourse.mybir as mybir

F32 = mybir.dt.float32
BF16 = mybir.dt.bfloat16
F32R = mybir.dt.float32r
I32 = mybir.dt.int32
ALU = mybir.AluOpType
ACT = mybir.ActivationFunctionType
AX = mybir.AxisListType

B, T, D = 8, 112, 256
S, DC = 375, 512
NH, DH = 16, 16
KEYS = S + T
CH, NCH = 125, 3
KPAD = CH * (NCH + 1)
HALF, HT = 2, 4
W = HT * T
NE, TOPK, HID = 16, 4, 128
NU = NE + 2
H4 = 4 * D
RB = 6 * DH
Q_PART = (0, 0, 0, 1, 1, 2)
K_PART = (0, 1, 2, 0, 1, 0)
LN_EPS = 1e-5
LOGP = -0.001
DT = -math.log(-math.expm1(LOGP))
BCOEF = math.exp(LOGP)
SCORE_ROWS = (0, 1, 4)
NCOMP = 4
EARLY = 7
QB, Q_EPS = 127.0, 1e-5
ONE_PAIR = struct.unpack("f", struct.pack("I", 0x3F803F80))[0]
MAGIC = 1.5 * 2.0 ** 23


def flamingo(nc, x, ctx_in, patch_lens, g_xattn, g_ffn, w_qkv, w_proj, b_proj, gate_w, ws_in, vs_in,
             ws_out, e_win, e_vin, e_wout, w_in, b_in, g_res, g_init, w1, b1, w2, b2, out):
    kscr = nc.dram_tensor("k_parts", (3, D, B, KEYS), BF16, kind="Internal").ap()
    qscr = nc.dram_tensor("q_parts", (3, D, B * T), BF16, kind="Internal").ap()
    cscr = nc.dram_tensor("combine_rows", (NE, B * T), F32, kind="Internal").ap()

    with ExitStack() as stack:
        def sb(name, shape, dt=F32):
            return stack.enter_context(nc.sbuf_tensor(name, shape, dt))

        def sem(name):
            return stack.enter_context(nc.semaphore(name))

        PS = stack.enter_context(nc.psum_tensor("banks", [128, 8, 512], F32))

        def bank(i):
            return PS[:, i, :]

        ident = sb("ident", [128, 128])
        identb = sb("identb", [128, 128], BF16)
        ones = sb("ones", [128, 128])
        onesb = sb("onesb", [128, 128], BF16)
        tri = sb("tri", [128, 128])
        before = sb("before", [128, NE, NE])
        mhalf = sb("mhalf", [128, HT])
        pidx = sb("pidx", [128, 1])
        iota_t = sb("iota_t", [128, T])
        xs = sb("xs", [128, B, D])
        xn = sb("xn", [128, HT, D])
        xnT = sb("xnT", [128, 2, B * T])
        wT = sb("wT", [128, 2, 4 * D])
        winT = sb("winT", [128, 2, D])
        gateT = sb("gateT", [128, 2, NE])
        gates = sb("gates", [128, 4])
        tg = sb("tg", [128, 4])
        gres = sb("gres", [128, 2])
        gbp = sb("gbp", [128, D])
        gbin = sb("gbin", [128, D])
        gb2 = sb("gb2", [128, D])
        gib = sb("gib", [128, D])
        b1_b = sb("b1_b", [128, H4])
        stats = sb("stats", [128, 2, HT, 6])
        mv = sb("mv", [128, 2, HT, 2])
        rs = sb("rs", [128, 2, 4, HT])
        ssq = sb("ssq", [128, B])
        rsc = sb("rsc", [128, 2, B])
        u = sb("u", [128, B, D])
        w2T = sb("w2T", [128, 8, D], BF16)
        ring = sb("ring", [128, 4, 6 * HID])
        nm = sb("nm", [128, 2, NH])
        mrow = sb("mrow", [128, 2, 2, T], BF16)
        osb = sb("osb", [128, W])
        rinv = sb("rinv", [128, NH])
        asb = sb("asb", [128, NH, DH])
        attT = sb("attT", [128, 2 * T])
        gth = sb("gth", [128, HT, NE])
        gsg = sb("gsg", [128, HT, NE])
        gsum = sb("gsum", [128, 2, HT])
        msk = sb("msk", [128, NCH * B], I32)
        sqj = sb("sqj", [128, DC], BF16)
        magic = sb("magic", [128, 1])
        gelu_pre = sb("gelu_pre", [128, 1])
        mskf = sb("mskf", [128, NCH * B])
        idx = sb("idx", [128, 2, NCH * B])
        wabs = sb("wabs", [128, 2])
        wsc = sb("wsc", [128, 5, 2])
        lc = sb("lc", [128, 12, HT])

        with ExitStack() as attention:
            def sb_a(name, shape, dt=F32):
                return attention.enter_context(nc.sbuf_tensor(name, shape, dt))

            comp_ = sb_a("comp", [128, NCOMP - 1, 3, 2 * S], BF16)
            r1 = sb_a("r1", [128, 2, 2 * S])
            ctxs = sb_a("ctxs", [128, 3, NCH, DC])
            ex = sb_a("ex", [128, 4, W])
            vst = sb_a("vst", [128, 2, NCH + 1, NH, 32])
            qst = sb_a("qst", [128, NH, B * T], BF16)
            kst = sb_a("kst", [128, 3, NH, KPAD], BF16)
        comp = [comp_[:, n, :, :] for n in range(NCOMP - 1)] + [
            ring[:, 0:2, :].rearrange("p a c -> p (a c)").bitcast(BF16)[:, 0:6 * S]
            .rearrange("p (a t) -> p a t", a=3)]

        comp_words, half_words = 6 * S * (NCOMP - 1) // 2, 4 * W
        ranks_words = (2 * NE + 1) * HT * NE
        xp0 = sb("x_parts0", [128, 2, 2, W], F32R)
        sb("gap_rows", [128, W])
        ranks = sb("ranks", [128, ranks_words])
        sb("gap_r1", [128, comp_words + 4 * S - half_words - W - ranks_words])
        wp = sb("w_parts", [128, 3, 2, 6 * HID], F32R)
        xp1 = sb("x_parts1", [128, 2, 2, W], F32R)
        hp = sb("h_parts", [128, 2, 2, W], F32R)

        def cut(region, at, n):
            return region[:, at:at + n]

        xp = [xp0, xp1]
        later_c = comp_[:, :, :, :].rearrange("p n a t -> p (n a t)").bitcast(F32)
        cTs = cut(later_c, half_words, W)[0:NE, :]
        later_v = vst[:, :, :, :, :].rearrange("p a c h d -> p (a c h d)")
        wdep = cut(later_v, half_words, B * T)
        xh = [cut(later_v, half_words + B * T + i * D, D) for i in range(HT)]
        qf = xh
        later_q = qst[:, :, :].rearrange("p h t -> p (h t)").bitcast(F32)
        silu_sb = [cut(later_q, i * W, W) for i in range(2)]
        t_sb = [cut(later_q, (2 + i) * W, W) for i in range(2)]
        h_sb = [cut(later_q, (4 + i) * W, W) for i in range(2)]
        cb = [cut(later_q, (6 + i) * W, W) for i in range(4)]
        xq = [cut(later_q, 10 * W + i * D // 2, D // 2).bitcast(BF16) for i in range(HT)]
        xqT = [cut(later_q, 10 * W + HT * D // 2 + i * T, T).bitcast(BF16) for i in range(HT)]
        w1T = cut(later_q, 10 * W + HT * D // 2 + HT * T, H4).bitcast(BF16).rearrange("p (k c) -> p k c", k=2)
        later_k = kst[:, :, :, :].rearrange("p s h t -> p (s h t)").bitcast(F32)
        w1s = cut(later_k, 0, 8 * D)
        w2s = cut(later_k, 2048, 2 * H4)
        junk = cut(later_k, 4096, 2048)
        tq1 = cut(later_k, 6144, 1024).bitcast(BF16)
        tq2 = cut(later_k, 7168, 1024).bitcast(BF16)
        eqm = cut(later_k, 8192, 1344).bitcast(BF16)
        bm = cut(later_k, 9536, B * T)
        keep = cut(later_k, 10432, B * T)
        h1 = [cut(later_k, i * H4, H4) for i in range(HT)]
        hq = [cut(later_k, 4096 + 512 * i, 512).bitcast(BF16) for i in range(HT)]
        hqT = [cut(later_k, 6144 + 448 * i, 448).bitcast(BF16) for i in range(HT)]
        xhT = [cut(later_k, 8192 + i * 2 * T, 2 * T) for i in range(HT)]

        in_x = [sem(f"in_x{h}") for h in range(HALF)]
        in_wq, in_wp, in_wg, in_small, in_mask, in_w12 = (
            sem("in_wq"), sem("in_wp"), sem("in_wg"), sem("in_small"), sem("in_mask"), sem("in_w12"))
        in_ctx = [sem(f"in_ctx{i}") for i in range(3)]
        in_kst = [sem(f"in_kst{i}") for i in range(3)]
        in_qst = [sem(f"in_qst{i}") for i in range(3)]
        in_ring = [sem(f"in_ring{i}") for i in range(4)]
        in_cb = [sem(f"in_cb{i}") for i in range(4)]
        parts_out = [sem(f"parts_out{i}") for i in range(NCOMP)]
        in_mrow, cscr_out, y_out = sem("in_mrow"), sem("cscr_out"), sem("y_out")
        names = ("const ones_pad tanh_g gbp_s wt_pe wt_act wt_dve ln_stats ln_rs ln_x xnt_pe xnt_act xnt_dve "
                 "qk_pe sp_hi sp_r1 sp_mid sp_lo ct_pe v_pad v_pe v_own sq_act rs_pool u_dve xb_pool "
                 "a_pe max_dve mt_pe m_hi m_lo b_pe exp_act av_pe o_act nt_pe as_dve at_pe att_act pj_pe x1_dve "
                 "hin_pe vin_pe silu_act t_dve h_dve ha_act hb_dve w_hi w_lo xp_hi xp_lo out_pe x2_dve "
                 "gt_pe th_act cmb_dve cT_pe cT_act abs_act ws_pe ws_dve tq_dve w1t_pe w12_act w12_dve "
                 "m_dve cs_pe eq_dve cnt_pe keep_pool dd_dve e_act wdep_dve "
                 "l_st l_rs l_xh l_xg xht_pe xht_act win_pe x3_dve m_st m_rs xq_dve xqt_pe xqt_act w1_pe h1_dve gelu_act "
                 "s2_dve hr_act hq_dve hqt_pe hqt_act w2_pe l_xg2 y_dve step_dve step_pool").split()
        s = {n: sem(n) for n in names}

        SPLITS = ([("qk", i) for i in range(4)] + [("ctx", 0), ("ctx", 1), ("ctx", 2)]
                  + [("qk", 4 + i) for i in range(4)] + [("ctx", c) for c in range(3, B)])
        SP_AT = {k: n for n, k in enumerate(SPLITS)}
        WRITES = [2 if kind == "ctx" else 1 if i % 4 < 2 else 3 for kind, i in SPLITS]

        def parts_written(n):
            return parts_out[n % NCOMP], 16 * sum(WRITES[k] for k in range(n % NCOMP, n + 1, NCOMP))

        def l_bank(stage, t):
            if t < HT:
                return {"xh": 6, "win": 7, "xq": 7, "w1": 6, "hq": 7, "w2": 6}[stage]
            j = t - HT
            late = (6, 7, 4, 5)[j]
            return {"xh": j, "win": late, "xq": j, "w1": (6, 4, 0, 2)[j], "hq": late, "w2": j}[stage]

        def l_slot(e, stage):
            at = {"xh": 0, "win": 1, "xq": 2, "w1": 3, "gelu": 4, "scale": 5, "hq": 6, "w2": 7, "y": 8,
                  "pre": -1}[stage]
            t, r = divmod(e - 1 - at, 3)
            return t if r == 0 and 0 <= t < HT else None

        def h_done(i):
            h, e = divmod(i, NU)
            return (s["t_dve"], i + 1) if e < 2 else (s["h_dve"], h * NE + e - 1)

        Q_SETS = ((0, 1), (1, HT - 1), (HT, HT))
        ROOTS = ((0, HT), (HT, 2), (HT + 2, 2))

        def qk_bank(i):
            return (4, 5, 0, 2)[i] if i < 4 else 6 + i % 2

        block = stack.enter_context(nc.Block())

        @block.sync
        def _(sp):
            def load_x(h):
                sp.dma_start(xs[0:T, h * HT:(h + 1) * HT, :],
                             x[h * HT:(h + 1) * HT].rearrange("b t c -> t b c")).then_inc(in_x[h], 16)

            load_x(0)
            wq_st = ring[:, 0:2, :].rearrange("p a c -> p (a c)").rearrange("p (i c) -> p i c", c=D)
            sp.dma_start(wq_st, w_qkv.rearrange("(i p) c -> p i c", p=128)).then_inc(in_wq, 16)

            def load_ctx(c):
                if c >= 3:
                    sp.wait_ge(s["ct_pe"], c - 2)
                    sp.wait_ge(s["v_pad"], c - 2)
                    sp.wait_ge(s["u_dve"], c - 2)
                sp.dma_start(ctxs[0:CH, c % 3, :, :],
                             ctx_in[c].rearrange("(k p) d -> p k d", p=CH)).then_inc(in_ctx[c % 3], 16)

            def write_parts(n):
                kind, i = SPLITS[n]
                sp.wait_ge(s["sp_lo"], n + 1)
                sem_, _ = parts_written(n)
                parts = comp[n % NCOMP]
                if kind == "ctx":
                    for g_ in range(2):
                        sp.dma_start(kscr[:, g_ * 128:(g_ + 1) * 128, i, 0:S].rearrange("a r t -> r a t"),
                                     parts[:, :, g_ * S:(g_ + 1) * S]).then_inc(sem_, 16)
                    return
                h, m = divmod(i, 4)
                src = parts[:, :, 0:W]
                if m < 2:
                    sp.dma_start(qscr[:, m * 128:(m + 1) * 128, h * W:(h + 1) * W].rearrange("a r t -> r a t"), src)\
                        .then_inc(sem_, 16)
                else:
                    for a_ in range(3):
                        sp.dma_start(kscr[a_, (m - 2) * 128:(m - 1) * 128, h * HT:(h + 1) * HT, S:KEYS],
                                     parts[:, a_, 0:W].rearrange("p (b t) -> p b t", b=HT)).then_inc(sem_, 16)

            def read_k(c):
                for n in [SP_AT[("ctx", c)]] + [SP_AT[("qk", 4 * (c // HT) + i)] for i in (2, 3)]:
                    sp.wait_ge(*parts_written(n))
                if c >= 3:
                    sp.wait_ge(s["exp_act"], NH * (c - 2))
                for j, part in enumerate(K_PART):
                    sp.dma_start(kst[j * DH:(j + 1) * DH, c % 3, :, 0:KEYS],
                                 kscr[part, :, c, :].rearrange("(h r) t -> r h t", r=DH)).then_inc(in_kst[c % 3], 16)

            def read_q(k):
                first, n = Q_SETS[k]
                for i in (0, 1):
                    sp.wait_ge(*parts_written(SP_AT[("qk", 4 * (first // HT) + i)]))
                at = slice(first * T, (first + n) * T)
                for j, part in enumerate(Q_PART):
                    sp.dma_start(qst[j * DH:(j + 1) * DH, :, at],
                                 qscr[part, :, at].rearrange("(h r) t -> r h t", r=DH)).then_inc(in_qst[k], 16)

            def write_max(b):
                sp.wait_ge(s["m_lo"], b + 1)
                for j in range(2):
                    sp.dma_start(qst[RB + j:RB + j + 1, :, b * T:(b + 1) * T],
                                 mrow[0:NH, b % 2, j, :]).then_inc(in_mrow, 16)

            def row(v):
                return v.rearrange("(a n) -> a n", a=1)

            smalls = [(gates[:, 0:2], row(g_xattn)), (gates[:, 2:4], row(g_ffn)), (gbp[:, :], row(b_proj)),
                      (gbin[:, :], row(b_in)), (gb2[:, :], row(b2)), (gib[:, :], row(g_init)[:, 0:D]),
                      (b1_b[:, :], row(b1))]

            def load_small():
                sp.dma_start(ring[:, 3, 0:2 * D].rearrange("p (i c) -> p i c", c=D),
                              w_in.rearrange("(i p) c -> p i c", p=128)).then_inc(in_wg, 16)
                sp.dma_start(ring[0:NE, 2, 2 * D:3 * D], gate_w).then_inc(in_wg, 16)
                for dst, src in smalls:
                    sp.dma_start(dst, src.broadcast_to([128, dst.shape[1]])).then_inc(in_small, 16)
                with nc.allow_non_contiguous_dma(reason="256 scales and 3000 lengths onto partitions"):
                    sp.dma_start(gres[:, :], g_res.rearrange("(k p) -> p k", p=128)).then_inc(in_small, 16)
                    for k in range(NCH):
                        sp.dma_start(msk[0:CH, k * B:(k + 1) * B],
                                      patch_lens[:, k * CH:(k + 1) * CH].rearrange("b p -> p b")).then_inc(in_mask, 16)

            load_ctx(0)
            load_ctx(1)
            load_x(1)
            load_ctx(2)
            load_small()
            write_parts(0)
            write_parts(1)
            read_q(0)
            write_parts(2)
            write_parts(3)
            write_parts(4)
            read_k(0)
            read_q(1)
            write_parts(5)
            write_parts(6)
            read_k(1)
            write_max(0)
            read_k(2)
            load_ctx(3)
            for b in range(B):
                if b == 0:
                    write_parts(7)
                    write_parts(8)
                if b + 1 < B:
                    write_max(b + 1)
                if b == 1:
                    read_q(2)
                if b == 0:
                    write_parts(9)
                    write_parts(10)
                if b + 3 < B:
                    write_parts(SP_AT[("ctx", b + 3)])
                if b + 4 < B:
                    load_ctx(b + 4)
                if b + 3 < B:
                    read_k(b + 3)

            def load_ring(i):
                e = i % NU
                r = ring[:, i % 4, :]
                if i >= 4:
                    sp.wait_ge(s["w_lo"], i - 3)
                else:
                    sp.wait_ge(s["wt_act"], 4)
                    sp.wait_ge(s["wt_dve"], 3)
                if e < 2:
                    cols = slice(e * HID, (e + 1) * HID)
                    wi, vi, wo = ws_in[:, cols], vs_in[:, cols], ws_out[e * HID:(e + 1) * HID, :]
                else:
                    wi, vi, wo = e_win[e - 2], e_vin[e - 2], e_wout[e - 2]
                for k, w_ in ((0, wi), (1, vi)):
                    sp.dma_start(r[:, k * 2 * HID:(k + 1) * 2 * HID].rearrange("p (k h) -> p k h", k=2),
                                 w_.rearrange("(k p) h -> p k h", p=128)).then_inc(in_ring[i % 4], 16)
                sp.dma_start(r[:, 4 * HID:6 * HID], wo).then_inc(in_ring[i % 4], 16)

            for i in range(4):
                load_ring(i)
            sp.wait_ge(s["exp_act"], NH * B)
            for h in range(HALF):
                sp.wait_ge(s["cT_act"], h + 1)
                sp.dma_start(cscr[:, h * W:(h + 1) * W], cTs[:, :]).then_inc(cscr_out, 16)
                sp.wait_ge(cscr_out, 16 * (h + 1))
                for e in range(NU):
                    i = h * NU + e
                    if e >= 2:
                        j = h * NE + e - 2
                        if j >= 4:
                            sp.wait_ge(s["h_dve"], j - 3)
                        sp.dma_start(cb[j % 4], cscr[e - 2:e - 1, h * W:(h + 1) * W].broadcast_to([128, W]))\
                            .then_inc(in_cb[j % 4], 16)
                    if i >= 4 - 2 and i + 2 < HALF * NU and i + 2 >= 4:
                        load_ring(i + 2)
                    if i == 1:
                        sp.dma_start(w1s.rearrange("p (i c) -> p i c", i=8),
                                     w1.rearrange("(i p) c -> p i c", p=128)).then_inc(in_w12, 16)
                        sp.dma_start(w2s.rearrange("p (i c) -> p i c", i=2),
                                     w2.rearrange("(i p) c -> p i c", p=128)).then_inc(in_w12, 16)
            for t in range(B):
                sp.wait_ge(s["y_dve"], t + 1)
                sp.dma_start(out[t], xs[0:T, t, :]).then_inc(y_out, 16)
            sp.wait_ge(y_out, 16 * B)

        @block.gpsimd
        def _(pool):
            g = nc.gpsimd
            steps = [0]

            def link(ins):
                steps[0] += 1
                ins.then_inc(s["step_pool"], 1)
                pool.wait_ge(s["step_pool"], steps[0])

            for m, v in ((ident, 0.0), (identb, 0.0), (tri, 1.0), (before, 1.0)):
                last = g.memset(m[:], v)
            link(last)
            for m in (ident, identb):
                g.affine_select(out=m[:, :], in_=m[:, :], compare_op=ALU.not_equal, fill=1.0, base=0,
                                pattern=[[-1, 128]], channel_multiplier=1)
            g.affine_select(out=tri[:, :], in_=tri[:, :], compare_op=ALU.is_ge, fill=0.0, base=0,
                            pattern=[[1, 128]], channel_multiplier=-1)
            g.affine_select(out=before[:, :, :], in_=before[:, :, :], compare_op=ALU.is_gt, fill=0.0, base=0,
                            pattern=[[1, NE], [-1, NE]], channel_multiplier=0)
            g.memset(mhalf[:, :], -0.5).then_inc(s["const"], 1)
            g.memset(ones[:, :], 1.0)
            g.memset(onesb[:, :], 1.0)
            g.iota(pidx[:, :], pattern=[[0, 1]], base=0, channel_multiplier=1,
                   allow_small_or_imprecise_dtypes=True)
            g.iota(iota_t[:, :], pattern=[[1, T]], base=0, channel_multiplier=0,
                   allow_small_or_imprecise_dtypes=True).then_inc(s["const"], 1)
            pool.wait_ge(s["const"], 2)

            def ln_rs(k):
                pool.wait_ge(s["ln_stats"], k + 1)
                r = rs[0:T, k % 2]
                link(g.tensor_scalar(r[:, 0, :], mv[0:T, k % 2, :, 1], 1.0, LN_EPS, ALU.mult, ALU.add))
                g.tensor_tensor(r[:, 1, :], r[:, 0, :], mhalf[0:T, :], ALU.pow).then_inc(s["ln_rs"], 1)

            def split(n):
                width = 2 * S if SPLITS[n][0] == "ctx" else W
                pool.wait_ge(s["sp_r1"], n + 1)
                c_ = comp[n % NCOMP]
                if n < EARLY:
                    pool.wait_ge(s["sp_mid"], n + 1)
                else:
                    link(g.tensor_scalar(c_[:, 1, 0:width], r1[:, n % 2, 0:width], 1.0, 0.0, ALU.mult, ALU.add))
                g.tensor_tensor(c_[:, 2, 0:width], r1[:, n % 2, 0:width], c_[:, 1, 0:width],
                                ALU.subtract).then_inc(s["sp_lo"], 1)

            def v_pad(c):
                pool.wait_ge(in_ctx[c % 3], 16 * (c // 3 + 1))
                if c >= 2:
                    pool.wait_ge(s["av_pe"], NH * (c - 1))
                for k in range(NCH):
                    last = g.tensor_scalar(vst[0:CH, c % 2, k, :, 0:DH],
                                           ctxs[0:CH, c % 3, k, D:DC].rearrange("p (h d) -> p h d", d=DH),
                                           1.0, 0.0, ALU.mult, ALU.add)
                last.then_inc(s["v_pad"], 1)

            def patch_rs(c):
                pool.wait_ge(s["sq_act"], c + 1)
                link(g.tensor_scalar(rsc[0:T, 0, c:c + 1], ssq[0:T, c:c + 1], 1.0 / DC, LN_EPS, ALU.mult, ALU.add))
                g.tensor_tensor(rsc[0:T, 1, c:c + 1], rsc[0:T, 0, c:c + 1], mhalf[0:T, 0:1], ALU.pow)\
                    .then_inc(s["rs_pool"], 1)

            def ones_rows(c):
                g.memset(kst[RB:RB + 2, c, :, :].rearrange("p h t -> p (h t)").bitcast(F32), ONE_PAIR)\
                    .then_inc(s["ones_pad"], 1)
                pool.wait_ge(s["ones_pad"], c + 2)

            link(g.memset(kst[0:RB, :, :, KEYS:KPAD], 0.0))
            g.memset(vst[:, :, :, :, DH:32], 1.0).then_inc(s["ones_pad"], 1)
            pool.wait_ge(s["ones_pad"], 1)
            ln_rs(0)
            pool.wait_ge(s["ln_rs"], 1)
            ones_rows(0)
            for n in range(4):
                split(n)
            split(4)
            v_pad(0)
            patch_rs(0)
            for c in (1, 2):
                split(4 + c)
                patch_rs(c)
            ln_rs(1)
            pool.wait_ge(s["ln_rs"], 2)
            ones_rows(1)
            ones_rows(2)
            for b in range(B):
                if b == 0:
                    for n in range(7, 11):
                        split(n)
                if b == 1:
                    pool.wait_ge(s["gbp_s"], 1)
                    pool.wait_ge(s["ln_x"], B)
                    for t in range(B):
                        last = g.tensor_tensor(xs[0:T, t, :], xs[0:T, t, :], gbp[0:T, :], ALU.add)
                    last.then_inc(s["xb_pool"], 1)
                if b + 1 < B:
                    v_pad(b + 1)
                if b + 3 < B:
                    patch_rs(b + 3)
                    split(SP_AT[("ctx", b + 3)])
                if b == 5:
                    ln_rs(2)
            def split_x(h, piece):
                pool.wait_ge(s["xnt_act"], 3 + h)
                pool.wait_ge(s["xnt_dve"], 3 + h)
                x_ = xnT[:, :, h * W:(h + 1) * W]
                if piece == 0:
                    if h == 1:
                        pool.wait_ge(s["av_pe"], NH * B)
                    g.tensor_scalar(xp[h][:, 0, :, :], x_, 1.0, 0.0, ALU.mult, ALU.add).then_inc(s["xp_hi"], 1)
                    pool.wait_ge(s["xp_hi"], h + 1)
                else:
                    k = piece - 1
                    g.tensor_tensor(xp[h][:, 1, k, :], x_[:, k, :], xp[h][:, 0, k, :].bitcast(F32), ALU.subtract)\
                        .then_inc(s["xp_lo"], 1)

            def split_w(i):
                pool.wait_ge(in_ring[i % 4], 48 * (i // 4 + 1))
                if i >= 3:
                    pool.wait_ge(s["out_pe"], i - 2)
                w_, p_ = ring[:, i % 4, :], wp[:, i % 3]
                g.tensor_scalar(p_[:, 0, :], w_, 1.0, 0.0, ALU.mult, ALU.add).then_inc(s["w_hi"], 1)
                pool.wait_ge(s["w_hi"], i + 1)
                g.tensor_tensor(p_[:, 1, :], w_, p_[:, 0, :].bitcast(F32), ALU.subtract).then_inc(s["w_lo"], 1)

            def roots(k):
                first, n = ROOTS[k]
                h, at = divmod(first, HT)
                pool.wait_ge(s["l_st"], k + 1)
                r = rs[0:T, h, :, at:at + n]
                link(g.tensor_scalar(r[:, 0, :], mv[0:T, h, at:at + n, 1], 1.0 + LN_EPS, LN_EPS ** 2,
                                     ALU.mult, ALU.add))
                g.tensor_tensor(r[:, 3, :], r[:, 0, :], mhalf[0:T, 0:n], ALU.pow).then_inc(s["l_rs"], 1)

            def add_bin(t):
                pool.wait_ge(s["l_xh"], t + 1)
                g.tensor_tensor(xs[0:T, t, :], xs[0:T, t, :], gbin[0:T, :], ALU.add).then_inc(s["l_xg"], 1)

            def root(t):
                pool.wait_ge(s["m_st"], t + 1)
                k = t % HT
                link(g.tensor_scalar(lc[0:T, 0, k:k + 1], mv[0:T, t // HT, k, 1:2], 1.0, LN_EPS, ALU.mult, ALU.add))
                g.tensor_tensor(lc[0:T, 1, k:k + 1], lc[0:T, 0, k:k + 1], mhalf[0:T, 0:1], ALU.pow)\
                    .then_inc(s["m_rs"], 1)

            def add_b2(t):
                pool.wait_ge(s["xq_dve"], t + 1)
                g.tensor_tensor(xs[0:T, t, :], xs[0:T, t, :], gb2[0:T, :], ALU.add).then_inc(s["l_xg2"], 1)

            for n in range(len(SPLITS) - NCOMP, len(SPLITS)):
                pool.wait_ge(*parts_written(n))
            for piece in range(3):
                split_x(0, piece)
            pool.wait_ge(s["ct_pe"], B)
            pool.wait_ge(s["u_dve"], B)
            pool.wait_ge(s["sq_act"], B)
            pool.wait_ge(s["v_pad"], B)
            for i in range(3):
                split_w(i)
            pool.wait_ge(s["exp_act"], NH * B)
            link(g.memset(keep[0:T, :], 1.0))
            g.memset(keep[0:T, :].rearrange("p (b t) -> p b t", t=T)[:, :, 0:1], 0.0).then_inc(s["keep_pool"], 1)
            ln_rs(3)
            for h in range(HALF):
                for e in range(NU):
                    i = h * NU + e
                    if h == 1 and e == 0:
                        roots(0)
                    if h == 1:
                        for stage, step in (("xh", add_bin), ("win", root), ("xq", add_b2)):
                            t = l_slot(e, stage)
                            if t is not None:
                                step(t)
                    if i >= 1 and i + 2 < HALF * NU:
                        split_w(i + 2)
                    if h == 0 and e in (5, 8, 11):
                        split_x(1, (e - 5) // 3)
            roots(1)
            add_bin(HT)
            add_bin(HT + 1)
            roots(2)
            add_bin(HT + 2)
            add_bin(HT + 3)
            for step in (root, add_b2):
                for t in range(HT, B):
                    step(t)

        @block.scalar
        def _(act):
            a = nc.scalar
            act.dma_start(ring[:, 2, 0:2 * D].rearrange("p (i c) -> p i c", c=D),
                          w_proj.rearrange("(i p) c -> p i c", p=128)).then_inc(in_wp, 16)

            def w_out(half_):
                act.wait_ge(s["wt_pe"], 2 * half_ + 1)
                a.activation(wT[:, 0, 512 * half_:512 * half_ + 512], bank(half_), ACT.Copy).then_inc(s["wt_act"], 1)

            def xnt(k):
                h = k % 2
                act.wait_ge(s["xnt_pe"], 2 * k + 1)
                a.activation(xnT[:, 0, h * W:(h + 1) * W], bank(6)[:, 0:W], ACT.Copy).then_inc(s["xnt_act"], 1)

            def split_hi(n):
                kind, i = SPLITS[n]
                if n >= NCOMP:
                    act.wait_ge(*parts_written(n - NCOMP))
                if kind == "ctx":
                    act.wait_ge(s["ct_pe"], i + 1)
                    a.activation(comp[n % NCOMP][:, 0, :].rearrange("p (g t) -> p g t", g=2), PS[:, 6:8, 0:S],
                                 ACT.Copy).then_inc(s["sp_hi"], 1)
                else:
                    act.wait_ge(s["qk_pe"], i + 1)
                    a.activation(comp[n % NCOMP][:, 0, 0:W], bank(qk_bank(i))[:, 0:W], ACT.Copy,
                                 scale=DH ** -0.5 if i % 4 < 2 else 1.0).then_inc(s["sp_hi"], 1)

            def split_mid(n):
                width = 2 * S if SPLITS[n][0] == "ctx" else W
                act.wait_ge(s["sp_r1"], n + 1)
                a.activation(comp[n % NCOMP][:, 1, 0:width], r1[:, n % 2, 0:width], ACT.Copy).then_inc(s["sp_mid"], 1)

            def v_own(c):
                act.wait_ge(s["v_pe"], c + 1)
                if c >= 2:
                    act.wait_ge(s["av_pe"], NH * (c - 1))
                a.activation(vst[0:T, c % 2, NCH, :, 0:DH], bank(7)[0:T, 0:D].rearrange("p (h d) -> p h d", d=DH),
                             ACT.Copy).then_inc(s["v_own"], 1)

            def square(c):
                act.wait_ge(in_ctx[c % 3], 16 * (c // 3 + 1))
                if c >= 1:
                    act.wait_ge(s["sq_act"], c)
                a.activation(sqj[0:T, :], ctxs[0:T, c % 3, 0, :], ACT.Square,
                             accum_out=ssq[0:T, c:c + 1]).then_inc(s["sq_act"], 1)

            def m_hi(b):
                act.wait_ge(s["mt_pe"], b + 1)
                if b >= 2:
                    act.wait_ge(in_mrow, 32 * (b - 1))
                a.activation(mrow[0:NH, b % 2, 0, :], bank(7)[0:NH, 0:T], ACT.Copy).then_inc(s["m_hi"], 1)

            def o_out(b):
                act.wait_ge(s["av_pe"], NH * (b + 1))
                if b >= 1:
                    act.wait_ge(s["nt_pe"], b)
                a.activation(osb[:, :], bank(5)[:, 0:W], ACT.Copy).then_inc(s["o_act"], 1)

            def att_out(b):
                act.wait_ge(s["at_pe"], b + 1)
                if b >= 1:
                    act.wait_ge(s["pj_pe"], b)
                a.activation(attT[:, :], bank(6)[:, 0:2 * T], ACT.Copy).then_inc(s["att_act"], 1)

            def gate_tanh(h):
                act.wait_ge(s["gt_pe"], h + 1)
                if h:
                    act.wait_ge(s["cmb_dve"], h)
                a.activation(gth[0:T, :, :].rearrange("p t e -> p (t e)"), bank(6)[0:T, 0:HT * NE], ACT.Tanh,
                             scale=0.5).then_inc(s["th_act"], 1)

            def rows_out(h):
                act.wait_ge(s["cT_pe"], h + 1)
                if h:
                    act.wait_ge(cscr_out, 16 * h)
                a.activation(cTs[:, :], bank(7)[0:NE, 0:W], ACT.Copy).then_inc(s["cT_act"], 1)

            w_out(0)
            xnt(0)
            w_out(1)
            for n in range(5):
                split_hi(n)
                if n >= 1:
                    split_mid(n - 1)
            split_mid(4)
            v_own(0)
            square(0)
            for c in (1, 2):
                split_hi(4 + c)
                square(c)
                split_mid(4 + c)
            act.wait_ge(in_small, 16 * 8)
            a.activation(tg[:, :], gates[:, :], ACT.Tanh).then_inc(s["tanh_g"], 1)
            act.wait_ge(s["wt_pe"], 5)
            for k in range(2):
                a.mul(winT[:, k, :], bank(6)[:, k * D:(k + 1) * D], gres[:, k:k + 1]).then_inc(s["wt_act"], 1)
            m_hi(0)
            xnt(1)
            split_hi(7)
            split_hi(8)
            for b in range(B):
                for h in range(NH):
                    if h == 1 and b >= 1:
                        o_out(b - 1)
                    n = NH * b + h
                    act.wait_ge(s["b_pe"], n + 1)
                    if n >= 4:
                        act.wait_ge(s["av_pe"], n - 3)
                    a.activation(ex[0:CH, n % 4, :], bank(2 + n % 2)[0:CH, 0:W], ACT.Exp).then_inc(s["exp_act"], 1)
                    if h == (6 if b else 5) and b + 1 < B:
                        v_own(b + 1)
                    if h == 7 and b == 0:
                        split_hi(9)
                        split_hi(10)
                    if h == 8 and b >= 1:
                        att_out(b - 1)
                    if h == 11 and b + 1 < B:
                        m_hi(b + 1)
                    if h == 13 and b + 3 < B:
                        square(b + 3)
                    if h == 0 and 1 <= b <= B - 3:
                        split_hi(SP_AT[("ctx", b + 2)])
                    if h == 15 and b == 5:
                        xnt(2)
                    if h == 14 and b == 6:
                        gate_tanh(0)
                    if h == 14 and b == 7:
                        rows_out(0)
            o_out(B - 1)
            att_out(B - 1)

            def ternary_out(k):
                act.wait_ge(s["w1t_pe"], 2 * k + 1)
                src = bank(6).bitcast(BF16)
                if k == 0:
                    a.activation(w1T[:, 0, :], src, ACT.Copy).then_inc(s["w12_act"], 1)
                else:
                    a.activation(w2T[:, :, 0:128], src.rearrange("p (k c) -> p k c", k=8), ACT.Copy)\
                        .then_inc(s["w12_act"], 1)

            def xht_out(t):
                act.wait_ge(s["xht_pe"], t + 1)
                a.activation(xhT[t % HT], bank(l_bank("xh", t))[:, 0:2 * T], ACT.Copy).then_inc(s["xht_act"], 1)

            def xqt_out(t):
                act.wait_ge(s["xqt_pe"], t + 1)
                a.activation(xqT[t % HT], bank(l_bank("xq", t)).bitcast(BF16)[:, 0:2 * T], ACT.Copy)\
                    .then_inc(s["xqt_act"], 1)

            def gelu(t):
                act.wait_ge(s["h1_dve"], t + 1)
                a.activation(h1[t % HT][0:T, :], h1[t % HT][0:T, :], ACT.Gelu).then_inc(s["gelu_act"], 1)

            def scale_up(t):
                act.wait_ge(s["s2_dve"], t + 1)
                a.activation(h1[t % HT][0:T, :], h1[t % HT][0:T, :], ACT.Identity, bias=magic[0:T, :],
                             scale=lc[0:T, 9, t % HT:t % HT + 1]).then_inc(s["hr_act"], 1)

            def hqt_out(t):
                act.wait_ge(s["hqt_pe"], t + 1)
                a.activation(hqT[t % HT], bank(l_bank("hq", t)).bitcast(BF16)[:, 0:8 * T], ACT.Copy)\
                    .then_inc(s["hqt_act"], 1)

            for h in range(HALF):
                for e in range(NU):
                    i = h * NU + e
                    act.wait_ge(s["hin_pe"], i + 1)
                    if i >= 2:
                        act.wait_ge(s["t_dve"], i - 1)
                    a.activation(silu_sb[i % 2], bank(2 * (i % 2))[:, 0:W], ACT.Silu).then_inc(s["silu_act"], 1)
                    act.wait_ge(*h_done(i))
                    if i == 0:
                        act.wait_ge(s["av_pe"], NH * B)
                    if i >= 2:
                        act.wait_ge(s["out_pe"], i - 1)
                    a.activation(hp[:, i % 2, 0, :], h_sb[i % 2], ACT.Copy).then_inc(s["ha_act"], 1)
                    if h == 0:
                        if e == 2:
                            xnt(3)
                        if e == 5:
                            gate_tanh(1)
                        if e == 11:
                            rows_out(1)
                        if e in (6, 7):
                            act.wait_ge(in_w12, 32)
                            a.activation(junk, (w1s, w2s)[e - 6], ACT.Abs, accum_out=wabs[:, e - 6:e - 5])\
                                .then_inc(s["abs_act"], 1)
                            act.wait_ge(s["abs_act"], e - 5)
                        if e in (13, 15):
                            ternary_out((e - 13) // 2)
                        if e == 5:
                            act.wait_ge(s["dd_dve"], 2)
                            a.activation(bm[0:T, :], keep[0:T, :], ACT.Exp, scale=-DT).then_inc(s["e_act"], 1)
                    if h == 1:
                        for stage, step in (("xh", xht_out), ("gelu", gelu), ("scale", scale_up), ("xq", xqt_out),
                                            ("hq", hqt_out)):
                            t = l_slot(e, stage)
                            if t is not None:
                                step(t)

            t0 = HT
            for t in range(t0, B):
                xht_out(t)
            a.activation(gelu_pre[:, :], magic[:, :], ACT.Gelu)
            for stage, t in ((xqt_out, 0), (xqt_out, 1), (gelu, 0), (gelu, 1), (xqt_out, 2), (xqt_out, 3),
                             (scale_up, 0), (scale_up, 1), (gelu, 2), (gelu, 3), (hqt_out, 0), (hqt_out, 1),
                             (scale_up, 2), (scale_up, 3), (hqt_out, 2), (hqt_out, 3)):
                stage(t0 + t)

        @block.tensor
        def _(pe):
            mm, tr = nc.tensor.matmul, nc.tensor.transpose
            pe.wait_ge(s["const"], 1)

            def w_t(half_):
                pe.wait_ge(in_wq, 16)
                if half_:
                    pe.wait_ge(in_wp, 16)
                for k in range(2):
                    for i in range(4):
                        blk = 4 * half_ + i
                        src = (wq_st[:, blk * D + k * 128:blk * D + (k + 1) * 128] if blk < 6 else
                               ring[:, 2, (blk - 6) * D + k * 128:(blk - 6) * D + (k + 1) * 128])
                        last = tr(bank(2 * k + half_)[:, 128 * i:128 * (i + 1)], src, ident[:, :])
                    last.then_inc(s["wt_pe"], 1)

            wq_st = ring[:, 0:2, :].rearrange("p a c -> p (a c)")

            def w_in_t():
                pe.wait_ge(in_wg, 32)
                take(6, s["wt_act"], 4)
                for k in range(2):
                    for i in range(2):
                        last = tr(bank(6)[:, k * D + 128 * i:k * D + 128 * (i + 1)],
                                  ring[:, 3, i * D + k * 128:i * D + (k + 1) * 128], ident[:, :])
                last.then_inc(s["wt_pe"], 1)
                take(7, s["wt_dve"], 3)
                for k in range(2):
                    last = tr(bank(7)[:, k * NE:(k + 1) * NE],
                              ring[0:NE, 2, 2 * D + k * 128:2 * D + (k + 1) * 128], ident[0:NE, 0:NE])
                last.then_inc(s["wt_pe"], 1)

            free = {n: None for n in range(8)}

            def take(n, *then):
                if free[n] is not None:
                    pe.wait_ge(*free[n])
                free[n] = then

            def ln_t(k):
                h = k % 2
                pe.wait_ge(s["ln_x"], HT * (k + 1))
                take(6, s["xnt_act"], k + 1)
                take(7, s["xnt_dve"], k + 1)
                for c in range(2):
                    for t in range(HT):
                        last = tr(bank(6 + c)[:, t * T:(t + 1) * T], xn[0:T, t, c * 128:(c + 1) * 128],
                                  ident[0:T, 0:T])
                    last.then_inc(s["xnt_pe"], 1)

            def xnt_ready(k):
                pe.wait_ge(s["xnt_act"], k + 1)
                pe.wait_ge(s["xnt_dve"], k + 1)

            def qk(i):
                h, m = divmod(i, 4)
                xnt_ready(h)
                if h == 0:
                    pe.wait_ge(s["wt_act"], 1)
                    pe.wait_ge(s["wt_dve"], 1)
                else:
                    take(qk_bank(i), s["sp_r1"], SP_AT[("qk", i)] + 1)
                for c in range(2):
                    last = mm(bank(qk_bank(i))[:, 0:W],
                              wT[:, c, m * 128:(m + 1) * 128],
                              xnT[:, c, h * W:(h + 1) * W], start=c == 0, stop=c == 1)
                last.then_inc(s["qk_pe"], 1)

            def ctx_t(c):
                pe.wait_ge(in_ctx[c % 3], 16 * (c // 3 + 1))
                n = SP_AT[("ctx", c)]
                take(6, s["sp_r1"], n + 1)
                take(7, s["sp_r1"], n + 1)
                for g_ in range(2):
                    for k in range(NCH):
                        last = tr(bank(6 + g_)[:, k * CH:(k + 1) * CH],
                                  ctxs[0:CH, c % 3, k, g_ * 128:(g_ + 1) * 128], ident[0:CH, 0:CH])
                last.then_inc(s["ct_pe"], 1)

            def own_v(c):
                take(7, s["v_own"], c + 1)
                for k in range(2):
                    last = mm(bank(7)[0:T, 0:D], xnT[:, k, c * T:(c + 1) * T], wT[:, k, 2 * D:3 * D],
                              start=k == 0, stop=k == 1)
                last.then_inc(s["v_pe"], 1)

            def score_rows(b, h):
                n = NH * b + h
                if h == 0:
                    pe.wait_ge(in_kst[b % 3], 96 * (b // 3 + 1))
                    pe.wait_ge(in_qst[sum(b >= first for first, _ in Q_SETS) - 1], 96)
                if n >= 3:
                    pe.wait_ge(s["max_dve"], n - 2)
                mm(bank(SCORE_ROWS[n % 3])[0:T, 0:KEYS], qst[0:RB, h, b * T:(b + 1) * T], kst[0:RB, b % 3, h, 0:KEYS],
                   start=True, stop=True).then_inc(s["a_pe"], 1)

            def max_t(b):
                take(7, s["m_lo"], b + 1)
                pe.wait_ge(s["max_dve"], NH * (b + 1))
                tr(bank(7)[0:NH, 0:T], nm[0:T, b % 2, :], ident[0:T, 0:T]).then_inc(s["mt_pe"], 1)

            def score_cols(b, h):
                n = NH * b + h
                if h == 0:
                    pe.wait_ge(in_mrow, 32 * (b + 1))
                    pe.wait_ge(s["ones_pad"], (2, 3, 4)[min(b, 2)])
                if n >= 2:
                    pe.wait_ge(s["exp_act"], n - 1)
                for c in range(NCH + 1):
                    last = mm(bank(2 + n % 2)[0:CH, c * T:(c + 1) * T],
                              kst[0:RB + 2, b % 3, h, c * CH:(c + 1) * CH],
                              qst[0:RB + 2, h, b * T:(b + 1) * T], start=True, stop=True)
                last.then_inc(s["b_pe"], 1)

            def values(b, h):
                n = NH * b + h
                if h == 0:
                    pe.wait_ge(s["v_pad"], b + 1)
                    pe.wait_ge(s["v_own"], b + 1)
                    if b >= 1:
                        pe.wait_ge(s["o_act"], b)
                pe.wait_ge(s["exp_act"], n + 2)
                for c in range(NCH + 1):
                    rows = CH if c < NCH else T
                    for k in range(2):
                        i, j = divmod(h + k, 4)
                        last = mm(bank(5)[32 * j:32 * j + 32, i * T:(i + 1) * T], vst[0:rows, b % 2, c, h + k, :],
                                  ex[0:rows, (n + k) % 4, c * T:(c + 1) * T], start=c == 0, stop=c == NCH)
                last.then_inc(s["av_pe"], 2)

            def norm_t(b):
                pe.wait_ge(s["o_act"], b + 1)
                take(6, s["as_dve"], b + 1)
                for i in range(4):
                    last = tr(bank(6)[0:T, 128 * i:128 * (i + 1)], osb[:, i * T:(i + 1) * T], ident[:, :])
                last.then_inc(s["nt_pe"], 1)

            def att_t(b):
                take(6, s["att_act"], b + 1)
                att = asb[0:T, :, :].rearrange("p h d -> p (h d)")
                for k in range(2):
                    last = tr(bank(6)[:, k * T:(k + 1) * T], att[:, k * 128:(k + 1) * 128], ident[0:T, 0:T])
                last.then_inc(s["at_pe"], 1)

            def project(b):
                take(6, s["x1_dve"], b + 1)
                for k in range(2):
                    last = mm(bank(6)[0:T, 0:D], attT[:, k * T:(k + 1) * T], wT[:, k, 3 * D:4 * D],
                              start=k == 0, stop=k == 1)
                last.then_inc(s["pj_pe"], 1)

            def gate_logits(h):
                take(6, s["th_act"], h + 1)
                pe.wait_ge(s["wt_dve"], 3)
                xnt_ready(2 + h)
                for t in range(HT):
                    for k in range(2):
                        at = h * W + t * T
                        last = mm(bank(6)[0:T, t * NE:(t + 1) * NE], xnT[:, k, at:at + T], gateT[:, k, :],
                                  start=k == 0, stop=k == 1)
                last.then_inc(s["gt_pe"], 1)

            def combine_t(h):
                take(7, s["cT_act"], h + 1)
                pe.wait_ge(s["cmb_dve"], h + 1)
                for t in range(HT):
                    last = tr(bank(7)[0:NE, t * T:(t + 1) * T], gsg[0:T, t, :], ident[0:T, 0:T])
                last.then_inc(s["cT_pe"], 1)

            w_t(0)
            ln_t(0)
            w_t(1)
            for i in range(4):
                qk(i)
            ctx_t(0)
            pe.wait_ge(s["wt_act"], 2)
            pe.wait_ge(s["wt_dve"], 2)
            own_v(0)
            ctx_t(1)
            ctx_t(2)
            w_in_t()
            pe.wait_ge(s["sp_r1"], 4)
            for h in range(NH):
                score_rows(0, h)
            max_t(0)
            ln_t(1)
            qk(4)
            qk(5)
            for b in range(B):
                for h in range(NH):
                    if b + 1 < B:
                        for j in range(min(5 * h // 3, NH), min(5 * (h + 1) // 3, NH)):
                            score_rows(b + 1, j)
                    score_cols(b, h)
                    if h >= 3 and h % 2 == 1:
                        values(b, h - 3)
                    if h == 4 and b >= 1:
                        norm_t(b - 1)
                    if h == (5 if b else 3) and b + 1 < B:
                        own_v(b + 1)
                    if h == 5 and b == 0:
                        qk(6)
                        qk(7)
                    if h == 7 and b >= 1:
                        att_t(b - 1)
                    if h == 10 and b >= 1:
                        project(b - 1)
                    if h == 11 and b + 1 < B:
                        max_t(b + 1)
                    if h == 15 and b == 5:
                        ln_t(2)
                    if h == 13 and b == 6:
                        gate_logits(0)
                    if h == 13 and b == 7:
                        combine_t(0)
                if b + 3 < B:
                    ctx_t(b + 3)
                values(b, NH - 2)
            norm_t(B - 1)
            att_t(B - 1)
            project(B - 1)

            pe.wait_ge(s["const"], 2)
            PAIRS = ((0, 0), (0, 1), (1, 0))

            def up(i):
                h = i // NU
                w_ = wp[:, i % 3]
                pe.wait_ge(s["xp_lo"], 2 * (h + 1))
                pe.wait_ge(s["w_lo"], i + 1)
                if i >= 2:
                    pe.wait_ge(s["t_dve"], i - 1)
                for v, name in ((0, "hin_pe"), (1, "vin_pe")):
                    for k in range(2):
                        for pw, px in PAIRS:
                            last = mm(bank(2 * (i % 2) + v)[:, 0:W],
                                      w_[:, pw, (2 * v + k) * HID:(2 * v + k + 1) * HID], xp[h][:, px, k, :],
                                      start=k == 0 and pw == px, stop=k == 1 and pw == 1)
                    last.then_inc(s[name], 1)

            def down(i):
                h, e = divmod(i, NU)
                if e == 0:
                    if h:
                        pe.wait_ge(s["x2_dve"], HT * h)
                pe.wait_ge(s["ha_act"], i + 1)
                pe.wait_ge(s["hb_dve"], i + 1)
                for t in range(HT):
                    for ph, pw in PAIRS:
                        last = mm(bank(4 + t // 2)[0:T, (t % 2) * D:(t % 2 + 1) * D],
                                  hp[:, i % 2, ph, t * T:(t + 1) * T], wp[:, i % 3, pw, 4 * HID:6 * HID],
                                  start=e == 0 and t % 2 == 0 and ph == pw, stop=e == NU - 1 and ph == 1,
                                  skip_group_check=True)
                last.then_inc(s["out_pe"], 1)

            def sums_of_abs():
                take(6, s["ws_dve"], 1)
                pe.wait_ge(s["abs_act"], 2)
                mm(bank(6)[:, 0:2], ones[:, :], wabs[:, :], start=True, stop=True).then_inc(s["ws_pe"], 1)

            def ternary_t(k):
                pe.wait_ge(s["tq_dve"], 2 * (k + 1))
                take(6, s["w12_act"], k + 1)
                take(7, s["w12_dve"], k + 1)
                for c in range(2):
                    for i in range(8):
                        src = (tq1[:, i * D + c * 128:i * D + (c + 1) * 128] if k == 0 else
                               tq2[:, c * H4 + i * 128:c * H4 + (i + 1) * 128])
                        last = tr(bank(6 + c).bitcast(BF16)[:, i * 128:(i + 1) * 128], src, identb[:, :])
                    last.then_inc(s["w1t_pe"], 1)

            def patch_ends():
                take(6, s["eq_dve"], 1)
                pe.wait_ge(s["m_dve"], 1)
                for c in range(NCH):
                    for k in range(c + 1):
                        last = mm(bank(6)[0:CH, c * B:(c + 1) * B], (tri if k == c else ones)[0:CH, 0:CH],
                                  mskf[0:CH, k * B:(k + 1) * B], start=k == 0, stop=k == c)
                last.then_inc(s["cs_pe"], 1)

            def end_counts():
                pe.wait_ge(s["eq_dve"], 3)
                take(6, s["dd_dve"], 1)
                take(7, s["dd_dve"], 1)
                for h in range(HALF):
                    for c in range(NCH):
                        last = mm(bank(6 + h)[0:T, 0:W], onesb[0:CH, 0:T],
                                  eqm[0:CH, c * B * T + h * W:c * B * T + (h + 1) * W], start=c == 0, stop=c == NCH - 1)
                last.then_inc(s["cnt_pe"], 1)

            def xh_t(t):
                n = l_bank("xh", t)
                pe.wait_ge(s["l_xh"], t + 1)
                take(n, s["xht_act"], t + 1)
                for c in range(2):
                    last = tr(bank(n)[:, c * T:(c + 1) * T], xh[t % HT][0:T, c * 128:(c + 1) * 128], ident[0:T, 0:T])
                last.then_inc(s["xht_pe"], 1)

            def depool(t):
                n = l_bank("win", t)
                take(n, s["x3_dve"], t + 1)
                pe.wait_ge(s["u_dve"], B)
                pe.wait_ge(s["wdep_dve"], 1)
                mm(bank(n)[0:T, 0:D], wdep[0:T, t * T:(t + 1) * T], u[0:T, t, :], start=True, stop=False)

            def project_in(t):
                pe.wait_ge(s["xht_act"], t + 1)
                for c in range(2):
                    last = mm(bank(l_bank("win", t))[0:T, 0:D], xhT[t % HT][:, c * T:(c + 1) * T], winT[:, c, :],
                              start=False, stop=c == 1)
                last.then_inc(s["win_pe"], 1)

            def xq_t(t):
                n = l_bank("xq", t)
                pe.wait_ge(s["xq_dve"], t + 1)
                take(n, s["xqt_act"], t + 1)
                for c in range(2):
                    last = tr(bank(n).bitcast(BF16)[:, c * T:(c + 1) * T], xq[t % HT][0:T, c * 128:(c + 1) * 128],
                              identb[0:T, 0:T])
                last.then_inc(s["xqt_pe"], 1)

            def w1_up(t):
                n = l_bank("w1", t)
                pe.wait_ge(s["xqt_act"], t + 1)
                pe.wait_ge(s["w12_act"], 2)
                pe.wait_ge(s["w12_dve"], 2)
                for half_ in range(2):
                    take(n + half_, s["h1_dve"], t + 1)
                    for c in range(2):
                        last = mm(bank(n + half_)[0:T, :], xqT[t % HT][:, c * T:(c + 1) * T],
                                  w1T[:, c, half_ * 512:(half_ + 1) * 512], start=c == 0, stop=c == 1)
                last.then_inc(s["w1_pe"], 1)

            def hq_t(t):
                n = l_bank("hq", t)
                pe.wait_ge(s["hq_dve"], t + 1)
                take(n, s["hqt_act"], t + 1)
                for c in range(8):
                    last = tr(bank(n).bitcast(BF16)[:, c * T:(c + 1) * T], hq[t % HT][0:T, c * 128:(c + 1) * 128],
                              identb[0:T, 0:T])
                last.then_inc(s["hqt_pe"], 1)

            def w2_down(t):
                n = l_bank("w2", t)
                pe.wait_ge(s["hqt_act"], t + 1)
                take(n, s["y_dve"], t + 1)
                for c in range(8):
                    last = mm(bank(n)[0:T, 0:D], hqT[t % HT][:, c * T:(c + 1) * T], w2T[:, c, :],
                              start=c == 0, stop=c == 7)
                last.then_inc(s["w2_pe"], 1)

            def l_steps(e, *steps):
                for stage, step in steps:
                    t = l_slot(e, stage)
                    if t is not None:
                        step(t)

            for h in range(HALF):
                for e in range(NU):
                    i = h * NU + e
                    up(i)
                    if h == 1:
                        l_steps(e, ("w1", w1_up), ("win", depool), ("win", project_in))
                    if e >= 1:
                        down(i - 1)
                    if h == 1:
                        l_steps(e, ("xh", xh_t), ("hq", hq_t), ("xq", xq_t), ("w2", w2_down))
                    if h == 0:
                        if e == 2:
                            ln_t(3)
                        if e == 5:
                            gate_logits(1)
                        if e == 11:
                            combine_t(1)
                        if e == 9:
                            sums_of_abs()
                        if e in (13, 15):
                            ternary_t((e - 13) // 2)
                        if e == 1:
                            patch_ends()
                        if e == 4:
                            end_counts()
                down(h * NU + NU - 1)

            pe.wait_ge(s["t_dve"], HALF * NU)
            for t in range(HT, HT + 2):
                depool(t)
            for t in range(HT, HT + 2):
                xh_t(t)
            pe.wait_ge(s["x2_dve"], B)
            for t in range(HT + 2, B):
                depool(t)
            for t in range(HT, HT + 2):
                project_in(t)
            for t in range(HT + 2, B):
                xh_t(t)
            for t in range(HT + 2, B):
                project_in(t)
            for step, t in ((xq_t, 0), (xq_t, 1), (w1_up, 0), (w1_up, 1), (xq_t, 2), (xq_t, 3), (w1_up, 2), (w1_up, 3),
                            (hq_t, 0), (hq_t, 1), (w2_down, 0), (w2_down, 1), (hq_t, 2), (hq_t, 3), (w2_down, 2),
                            (w2_down, 3)):
                step(HT + t)

        @block.vector
        def _(dve):
            v = nc.vector
            steps = [0]

            def link(ins):
                steps[0] += 1
                ins.then_inc(s["step_dve"], 1)
                dve.wait_ge(s["step_dve"], steps[0])

            def ln_stats(k):
                h = k % 2
                for t in range(HT):
                    last = v.bn_stats(stats[0:T, h, t, :], xs[0:T, h * HT + t, :])
                link(last)
                for t in range(HT):
                    last = v.bn_aggr(mv[0:T, h, t, :], stats[0:T, h, t, :])
                last.then_inc(s["ln_stats"], 1)
                dve.wait_ge(s["ln_stats"], k + 1)

            def ln_x(k):
                h = k % 2
                dve.wait_ge(s["ln_rs"], k + 1)
                if k >= 1:
                    dve.wait_ge(s["xnt_pe"], 2 * k)
                for t in range(HT):
                    v.tensor_scalar(xn[0:T, t, :], xs[0:T, h * HT + t, :], mv[0:T, h, t, 0:1], rs[0:T, h, 1, t:t + 1],
                                    ALU.subtract, ALU.mult).then_inc(s["ln_x"], 1)

            def xnt(k):
                h = k % 2
                dve.wait_ge(s["xnt_pe"], 2 * k + 2)
                v.tensor_copy(xnT[:, 1, h * W:(h + 1) * W], bank(7)[:, 0:W]).then_inc(s["xnt_dve"], 1)

            def split_r1(n):
                kind, i = SPLITS[n]
                dve.wait_ge(s["sp_hi"], n + 1)
                if n >= 2:
                    dve.wait_ge(s["sp_lo"], n - 1)
                hi = comp[n % NCOMP][:, 0, :]
                if kind == "ctx":
                    v.tensor_tensor(r1[:, n % 2, :].rearrange("p (g t) -> p g t", g=2), PS[:, 6:8, 0:S],
                                    hi.rearrange("p (g t) -> p g t", g=2), ALU.subtract).then_inc(s["sp_r1"], 1)
                else:
                    v.scalar_tensor_tensor(out=r1[:, n % 2, 0:W], in0=bank(qk_bank(i))[:, 0:W],
                                           scalar=DH ** -0.5 if i % 4 < 2 else 1.0, in1=hi[:, 0:W],
                                           op0=ALU.mult, op1=ALU.subtract).then_inc(s["sp_r1"], 1)

            def patches(c):
                dve.wait_ge(s["rs_pool"], c + 1)
                v.scalar_tensor_tensor(out=u[0:T, c, :], in0=ctxs[0:T, c % 3, 0, 0:D], scalar=rsc[0:T, 1, c:c + 1],
                                       in1=gib[0:T, :], op0=ALU.mult, op1=ALU.mult).then_inc(s["u_dve"], 1)

            def row_max(b, h):
                n = NH * b + h
                dve.wait_ge(s["a_pe"], n + 1)
                if h == 0 and b >= 2:
                    dve.wait_ge(s["mt_pe"], b - 1)
                v.tensor_reduce(nm[0:T, b % 2, h:h + 1], bank(SCORE_ROWS[n % 3])[0:T, 0:KEYS], AX.X, ALU.max,
                                negate=True).then_inc(s["max_dve"], 1)

            def m_lo(b):
                dve.wait_ge(s["m_hi"], b + 1)
                v.tensor_tensor(mrow[0:NH, b % 2, 1, :], bank(7)[0:NH, 0:T], mrow[0:NH, b % 2, 0, :],
                                ALU.subtract).then_inc(s["m_lo"], 1)

            def normalise(b):
                dve.wait_ge(s["nt_pe"], b + 1)
                o = bank(6)[0:T, :].rearrange("p (h d) -> p h d", d=32)
                if b >= 1:
                    dve.wait_ge(s["as_dve"], b)
                link(v.reciprocal(rinv[0:T, :], o[:, :, DH]))
                if b >= 1:
                    dve.wait_ge(s["at_pe"], b)
                v.tensor_tensor(asb[0:T, :, :], o[:, :, 0:DH],
                                rinv[0:T, :].unsqueeze(2).broadcast_to([T, NH, DH]), ALU.mult)\
                    .then_inc(s["as_dve"], 1)

            def residual1(b):
                dve.wait_ge(s["pj_pe"], b + 1)
                dve.wait_ge(s["xb_pool"], 1)
                v.scalar_tensor_tensor(out=xs[0:T, b, :], in0=bank(6)[0:T, 0:D], scalar=tg[0:T, 0:1],
                                       in1=xs[0:T, b, :], op0=ALU.mult, op1=ALU.add).then_inc(s["x1_dve"], 1)

            def gate_weights(h, piece):
                g_ = gth[0:T, :, :]
                n = HT * NE * NE
                cmp, eq = ranks[0:T, 0:n], ranks[0:T, n:2 * n]
                if piece == 0:
                    dve.wait_ge(s["th_act"], h + 1)
                    if h:
                        dve.wait_ge(s["cT_pe"], h)
                    else:
                        for n in range(len(SPLITS) - NCOMP, len(SPLITS)):
                            dve.wait_ge(*parts_written(n))
                        dve.wait_ge(s["sp_lo"], len(SPLITS))
                    link(v.tensor_scalar(g_, g_, 0.5, 0.5, ALU.mult, ALU.add))
                if piece < 2:
                    for t in (2 * piece, 2 * piece + 1):
                        gj = g_[:, t, :].unsqueeze(1).broadcast_to([T, NE, NE])
                        ge = g_[:, t, :].unsqueeze(2).broadcast_to([T, NE, NE])
                        sl = slice(t * NE * NE, (t + 1) * NE * NE)
                        v.tensor_tensor(cmp[:, sl].rearrange("p (e j) -> p e j", e=NE), gj, ge, ALU.is_gt)
                        last = v.tensor_tensor(eq[:, sl].rearrange("p (e j) -> p e j", e=NE), gj, ge, ALU.is_equal)
                    link(last)
                if piece == 2:
                    link(v.tensor_tensor(eq.rearrange("p (t n) -> p t n", t=HT),
                                         eq.rearrange("p (t n) -> p t n", t=HT),
                                         before[0:T, :, :].rearrange("p e j -> p (e j)").unsqueeze(1)
                                         .broadcast_to([T, HT, NE * NE]), ALU.mult))
                if piece == 3:
                    link(v.tensor_tensor(cmp, cmp, eq, ALU.add))
                rk = ranks[0:T, 2 * n:2 * n + HT * NE]
                if piece == 4:
                    link(v.tensor_reduce(rk, cmp.rearrange("p (a j) -> p a j", j=NE), AX.X, ALU.add))
                    flat = gsg[0:T, :, :].rearrange("p t e -> p (t e)")
                    link(v.scalar_tensor_tensor(out=flat, in0=rk, scalar=float(TOPK),
                                                in1=g_.rearrange("p t e -> p (t e)"), op0=ALU.is_lt, op1=ALU.mult))
                    link(v.tensor_reduce(gsum[0:T, 0, :], gsg[0:T, :, :], AX.X, ALU.add))
                    link(v.reciprocal(gsum[0:T, 1, :], gsum[0:T, 0, :]))
                    v.tensor_tensor(gsg[0:T, :, :], gsg[0:T, :, :],
                                    gsum[0:T, 1, :].unsqueeze(2).broadcast_to([T, HT, NE]), ALU.mult)\
                        .then_inc(s["cmb_dve"], 1)
                    dve.wait_ge(s["cmb_dve"], h + 1)

            def w_out(half_):
                dve.wait_ge(s["wt_pe"], 2 * half_ + 2)
                v.tensor_copy(wT[:, 1, 512 * half_:512 * (half_ + 1)], bank(2 + half_)).then_inc(s["wt_dve"], 1)

            v.memset(magic[:, :], MAGIC)
            dve.wait_ge(in_x[0], 16)
            ln_stats(0)
            ln_x(0)
            w_out(0)
            xnt(0)
            w_out(1)
            for n in range(5):
                split_r1(n)
            split_r1(5)
            split_r1(6)
            dve.wait_ge(in_x[1], 16)
            ln_stats(1)
            dve.wait_ge(s["tanh_g"], 1)
            link(v.tensor_scalar(gbp[:, :], gbp[:, :], tg[:, 0:1], None, ALU.mult))
            v.tensor_scalar(gib[:, :], gib[:, :], BCOEF, None, ALU.mult)
            v.tensor_scalar(gbin[:, :], gbin[:, :], tg[:, 1:2], None, ALU.mult)
            v.tensor_scalar(gb2[:, :], gb2[:, :], tg[:, 3:4], None, ALU.mult).then_inc(s["gbp_s"], 1)
            dve.wait_ge(s["gbp_s"], 1)
            for c in range(3):
                patches(c)
            dve.wait_ge(s["wt_pe"], 6)
            v.tensor_copy(gateT[:, :, :], bank(7)[:, 0:2 * NE].rearrange("p (k e) -> p k e", k=2))\
                .then_inc(s["wt_dve"], 1)
            ln_x(1)
            for h in range(NH):
                row_max(0, h)
            m_lo(0)
            xnt(1)
            split_r1(7)
            split_r1(8)
            for b in range(B):
                if b == B - 1:
                    dve.wait_ge(in_mask, 16 * NCH)
                    v.tensor_copy(mskf[0:CH, :], msk[0:CH, :]).then_inc(s["m_dve"], 1)
                for h in range(NH):
                    if b + 1 < B:
                        row_max(b + 1, h)
                    if b == 0 and h == 11:
                        split_r1(9)
                        split_r1(10)
                    if h == 4 and 1 <= b <= B - 3:
                        split_r1(SP_AT[("ctx", b + 2)])
                    if h == 13 and b == 5:
                        dve.wait_ge(s["x1_dve"], HT)
                        ln_stats(2)
                    if h == 9 and b >= 1:
                        normalise(b - 1)
                    if h == 12 and 1 <= b and b + 2 < B:
                        patches(b + 2)
                if b >= 1:
                    residual1(b - 1)
                if b == 5:
                    ln_x(2)
                if b + 1 < B:
                    m_lo(b + 1)
                if b == 5:
                    xnt(2)
                if b == 6:
                    for piece in range(5):
                        gate_weights(0, piece)
            normalise(B - 1)
            residual1(B - 1)
            dve.wait_ge(s["x1_dve"], B)
            ln_stats(3)

            def ternary_scales():
                dve.wait_ge(s["ws_pe"], 1)
                v.tensor_scalar(wsc[:, 0, :], bank(6)[:, 0:2], 1.0 / (H4 * D), Q_EPS, ALU.mult, ALU.max)\
                    .then_inc(s["ws_dve"], 1)
                dve.wait_ge(s["ws_dve"], 1)
                v.tensor_scalar(wsc[:, 1, :], wsc[:, 0, :], 0.5, None, ALU.mult)
                v.tensor_scalar(wsc[:, 2, :], wsc[:, 0, :], -0.5, None, ALU.mult)
                link(v.tensor_scalar(wsc[:, 3, :], wsc[:, 0, :], -1.0 / QB, None, ALU.mult))
                v.tensor_scalar(wsc[:, 4, 0:1], wsc[:, 3, 0:1], 1.0, None, ALU.mult)
                link(v.tensor_scalar(wsc[:, 4, 1:2], wsc[:, 3, 1:2], tg[:, 3:4], None, ALU.mult))

            def ternary(piece):
                k, half_ = divmod(piece, 2)
                cols = slice(half_ * 1024, (half_ + 1) * 1024)
                w_, q_ = ((w1s, tq1), (w2s, tq2))[k]
                big = junk[:, k * 1024:(k + 1) * 1024].bitcast(BF16)
                link(v.tensor_scalar(big[:, cols], w_[:, cols], wsc[:, 1, k:k + 1], None, ALU.is_gt))
                v.scalar_tensor_tensor(out=q_[:, cols], in0=w_[:, cols], scalar=wsc[:, 2, k:k + 1], in1=big[:, cols],
                                       op0=ALU.is_lt, op1=ALU.subtract).then_inc(s["tq_dve"], 1)

            def ternary_out(k):
                dve.wait_ge(s["w1t_pe"], 2 * k + 2)
                src = bank(7).bitcast(BF16)
                if k == 0:
                    v.tensor_copy(w1T[:, 1, :], src).then_inc(s["w12_dve"], 1)
                else:
                    v.tensor_copy(w2T[:, :, 128:256], src.rearrange("p (k c) -> p k c", k=8)).then_inc(s["w12_dve"], 1)

            def ends_at():
                dve.wait_ge(s["cs_pe"], 1)
                i0, i1 = idx[0:CH, 0, :], idx[0:CH, 1, :]
                v.tensor_scalar(i0, bank(6)[0:CH, 0:NCH * B], 1.0, None, ALU.subtract).then_inc(s["eq_dve"], 1)
                dve.wait_ge(s["eq_dve"], 1)
                link(v.tensor_scalar(i1, i0, 0.0, float(T), ALU.is_lt, ALU.mult))
                link(v.tensor_tensor(i0, i0, i1, ALU.add))

            def ends_at_rows(piece):
                n = NCH * B // 2
                i0 = idx[0:CH, 0, piece * n:(piece + 1) * n]
                v.tensor_tensor(eqm[0:CH, piece * n * T:(piece + 1) * n * T].rearrange("p (n t) -> p n t", n=n),
                                iota_t[0:CH, :].unsqueeze(1).broadcast_to([CH, n, T]),
                                i0.unsqueeze(2).broadcast_to([CH, n, T]), ALU.is_equal).then_inc(s["eq_dve"], 1)

            def distance(piece):
                bm_, kp, wd = bm[0:T, :], keep[0:T, :], wdep[0:T, :]
                if piece == 0:
                    dve.wait_ge(s["cnt_pe"], 1)
                    dve.wait_ge(s["keep_pool"], 1)
                    v.tensor_scalar(bm_.rearrange("p (a t) -> p a t", a=2), PS[0:T, 6:8, 0:W], 1.0, None, ALU.min)\
                        .then_inc(s["dd_dve"], 1)
                    dve.wait_ge(s["dd_dve"], 1)
                    link(v.tensor_tensor_scan(wd, kp, bm_, 0.0, ALU.mult, ALU.add))
                    return
                link(v.tensor_scalar(wd, wd, -1.0, 0.0, ALU.add, ALU.max))
                link(v.tensor_scalar(wd, wd, pidx[0:T, :], None, ALU.subtract))
                v.tensor_scalar(kp, wd, 0.0, None, ALU.max).then_inc(s["dd_dve"], 1)

            def depool_weights():
                dve.wait_ge(s["e_act"], 1)
                v.scalar_tensor_tensor(out=wdep[0:T, :], in0=wdep[0:T, :], scalar=0.0, in1=bm[0:T, :],
                                       op0=ALU.is_ge, op1=ALU.mult).then_inc(s["wdep_dve"], 1)

            def hidden(i):
                h, e = divmod(i, NU)
                dve.wait_ge(s["vin_pe"], i + 1)
                dve.wait_ge(s["silu_act"], i + 1)
                shared = e < 2
                if i >= 2:
                    dve.wait_ge(s["hb_dve"], i - 1)
                dst = h_sb[i % 2] if shared else t_sb[i % 2]
                v.tensor_tensor(dst, bank(2 * (i % 2) + 1)[:, 0:W], silu_sb[i % 2], ALU.mult)\
                    .then_inc(s["t_dve"], 1)
                if not shared:
                    j = h * NE + e - 2
                    dve.wait_ge(s["t_dve"], i + 1)
                    dve.wait_ge(in_cb[j % 4], 16 * (j // 4 + 1))
                    v.tensor_tensor(h_sb[i % 2], t_sb[i % 2], cb[j % 4], ALU.mult).then_inc(s["h_dve"], 1)

            def h_low(i):
                dve.wait_ge(s["ha_act"], i + 1)
                dve.wait_ge(*h_done(i))
                v.tensor_tensor(hp[:, i % 2, 1, :], h_sb[i % 2], hp[:, i % 2, 0, :].bitcast(F32), ALU.subtract)\
                    .then_inc(s["hb_dve"], 1)

            def ln_last(k):
                first, n = ROOTS[k]
                h, at = divmod(first, HT)
                dve.wait_ge(s["x2_dve"], first + n)
                for t in range(at, at + n):
                    last = v.bn_stats(stats[0:T, h, t, :], xs[0:T, h * HT + t, :])
                link(last)
                for t in range(at, at + n):
                    last = v.bn_aggr(mv[0:T, h, t, :], stats[0:T, h, t, :])
                last.then_inc(s["l_st"], 1)
                dve.wait_ge(s["l_st"], k + 1)

            def residual2(t):
                h, k = divmod(t, HT)
                dve.wait_ge(s["out_pe"], NU * (h + 1))
                v.scalar_tensor_tensor(out=xs[0:T, t, :], in0=bank(4 + k // 2)[0:T, (k % 2) * D:(k % 2 + 1) * D],
                                       scalar=tg[0:T, 2:3], in1=xs[0:T, t, :], op0=ALU.mult, op1=ALU.add)\
                    .then_inc(s["x2_dve"], 1)

            def stage_a(t):
                h = t // HT
                dve.wait_ge(s["l_rs"], 1 + sum(t >= first for first, _ in ROOTS[1:]))
                v.tensor_scalar(xh[t % HT][0:T, :], xs[0:T, t, :], mv[0:T, h, t % HT, 0:1],
                                rs[0:T, h, 3, t % HT:t % HT + 1], ALU.subtract, ALU.mult).then_inc(s["l_xh"], 1)

            def stage_b(t):
                dve.wait_ge(s["win_pe"], t + 1)
                dve.wait_ge(s["l_xg"], t + 1)
                h, k = divmod(t, HT)
                v.scalar_tensor_tensor(out=xs[0:T, t, :], in0=bank(l_bank("win", t))[0:T, 0:D], scalar=tg[0:T, 1:2],
                                       in1=xs[0:T, t, :], op0=ALU.mult, op1=ALU.add).then_inc(s["x3_dve"], 1)
                dve.wait_ge(s["x3_dve"], t + 1)
                link(v.bn_stats(stats[0:T, h, k, :], xs[0:T, t, :]))
                v.bn_aggr(mv[0:T, h, k, :], stats[0:T, h, k, :]).then_inc(s["m_st"], 1)

            def stage_c(*ts):
                def c_(n):
                    return lc[0:T, n, ts[0] % HT:ts[-1] % HT + 1]

                f = [qf[t % HT][0:T, :] for t in ts]
                for t, f_ in zip(ts, f):
                    h, k = divmod(t, HT)
                    dve.wait_ge(s["m_rs"], t + 1)
                    last = v.tensor_scalar(f_, xs[0:T, t, :], mv[0:T, h, k, 0:1], lc[0:T, 1, k:k + 1],
                                           ALU.subtract, ALU.mult)
                link(last)
                for t, f_ in zip(ts, f):
                    last = v.tensor_reduce(lc[0:T, 2, t % HT:t % HT + 1], f_, AX.X, ALU.max, apply_absolute_value=True)
                link(last)
                link(v.tensor_scalar(c_(3), c_(2), Q_EPS, None, ALU.max))
                link(v.reciprocal(c_(4), c_(3)))
                v.tensor_scalar(c_(6), c_(3), wsc[0:T, 4, 0:1], None, ALU.mult)
                link(v.tensor_scalar(c_(5), c_(4), QB, None, ALU.mult))
                for i, (t, f_) in enumerate(zip(ts, f)):
                    last = v.tensor_scalar(f_, f_, lc[0:T, 5, t % HT:t % HT + 1], MAGIC, ALU.mult, ALU.add)
                    steps[0] += 1
                    last.then_inc(s["step_dve"], 1)
                for i, (t, f_) in enumerate(zip(ts, f)):
                    dve.wait_ge(s["step_dve"], steps[0] - len(ts) + 1 + i)
                    v.tensor_scalar(xq[t % HT][0:T, :], f_, MAGIC, QB, ALU.subtract, ALU.min).then_inc(s["xq_dve"], 1)

            def stage_d(t):
                n = l_bank("w1", t)
                dve.wait_ge(s["w1_pe"], t + 1)
                dve.wait_ge(s["xq_dve"], t + 1)
                v.scalar_tensor_tensor(out=h1[t % HT][0:T, :].rearrange("p (a n) -> p a n", a=2),
                                       in0=PS[0:T, n:n + 2, :], scalar=lc[0:T, 6, t % HT:t % HT + 1],
                                       in1=b1_b[0:T, :].rearrange("p (a n) -> p a n", a=2),
                                       op0=ALU.mult, op1=ALU.add).then_inc(s["h1_dve"], 1)

            def stage_e(*ts):
                def c_(n):
                    return lc[0:T, n, ts[0] % HT:ts[-1] % HT + 1]

                for t in ts:
                    dve.wait_ge(s["gelu_act"], t + 1)
                    last = v.tensor_reduce(lc[0:T, 7, t % HT:t % HT + 1], h1[t % HT][0:T, :], AX.X, ALU.max,
                                           apply_absolute_value=True)
                link(last)
                link(v.tensor_scalar(c_(8), c_(7), Q_EPS, None, ALU.max))
                v.tensor_scalar(c_(10), c_(8), wsc[0:T, 4, 1:2], None, ALU.mult)
                link(v.reciprocal(c_(11), c_(8)))
                v.tensor_scalar(c_(9), c_(11), QB, None, ALU.mult).then_inc(s["s2_dve"], len(ts))

            def stage_f(t):
                dve.wait_ge(s["s2_dve"], t + 1)
                dve.wait_ge(s["hr_act"], t + 1)
                v.tensor_scalar(hq[t % HT][0:T, :], h1[t % HT][0:T, :], MAGIC, QB, ALU.subtract, ALU.min)\
                    .then_inc(s["hq_dve"], 1)

            def stage_g(t):
                dve.wait_ge(s["w2_pe"], t + 1)
                dve.wait_ge(s["l_xg2"], t + 1)
                v.scalar_tensor_tensor(out=xs[0:T, t, :], in0=bank(l_bank("w2", t))[0:T, 0:D],
                                       scalar=lc[0:T, 10, t % HT:t % HT + 1], in1=xs[0:T, t, :],
                                       op0=ALU.mult, op1=ALU.add).then_inc(s["y_dve"], 1)

            def l_steps(e, *steps):
                for stage, step in steps:
                    t = l_slot(e, stage)
                    if t is not None:
                        step(t)

            for h in range(HALF):
                for e in range(NU):
                    hidden(h * NU + e)
                    if h == 0:
                        if e == 2:
                            xnt(3)
                        if 6 <= e < 11:
                            gate_weights(1, e - 6)
                        if e == 11:
                            ternary_scales()
                        if 11 <= e < 15:
                            ternary(e - 11)
                        if e == 1:
                            ln_x(3)
                            ends_at()
                        if e in (4, 5):
                            distance(e - 4)
                        if e == 16:
                            depool_weights()
                    else:
                        l_steps(e, ("y", stage_g), ("win", stage_b), ("w1", stage_d))
                    h_low(h * NU + e)
                    if h == 0:
                        if e in (13, 15):
                            ternary_out((e - 13) // 2)
                        if e in (1, 2):
                            ends_at_rows(e - 1)
                    else:
                        l_steps(e, ("win", stage_c), ("gelu", stage_e), ("pre", stage_a), ("scale", stage_f))
                if h == 0:
                    for t in range(HT):
                        residual2(t)
                    ln_last(0)
            stage_g(HT - 1)
            t0 = HT
            residual2(t0)
            residual2(t0 + 1)
            ln_last(1)
            residual2(t0 + 2)
            residual2(t0 + 3)
            stage_a(t0)
            stage_a(t0 + 1)
            ln_last(2)
            stage_a(t0 + 2)
            stage_a(t0 + 3)
            stage_b(t0)
            stage_b(t0 + 1)
            stage_c(t0, t0 + 1)
            stage_b(t0 + 2)
            stage_b(t0 + 3)
            stage_d(t0)
            stage_d(t0 + 1)
            stage_c(t0 + 2, t0 + 3)
            stage_e(t0, t0 + 1)
            stage_d(t0 + 2)
            stage_d(t0 + 3)
            for t in (t0, t0 + 1):
                stage_f(t)
            stage_e(t0 + 2, t0 + 3)
            for t in (t0 + 2, t0 + 3):
                stage_f(t)
            for t in range(t0, B):
                stage_g(t)


_INS = ['x', 'ctx_2048', 'mask_BxS2_if0', 'g_xattn', 'g_ffn', 'L0_xattn_w_qkv', 'L0_xattn_w_proj', 'L0_xattn_b_proj',
        'L0_ffn_gate_w', 'L0_ffn_ws_in', 'L0_ffn_vs_in', 'L0_ffn_ws_out', 'L0_ffn_e_win', 'L0_ffn_e_vin',
        'L0_ffn_e_wout', 'L1_xattn_W_in', 'L1_xattn_b_in', 'L1_xattn_g_res', 'L1_xattn_g_init', 'L1_ffn_W1',
        'L1_ffn_b1', 'L1_ffn_W2', 'L1_ffn_b2']


def kernel(**inputs):
    import numpy as _np
    import concourse.bacc as _bacc
    from concourse import mybir as _mybir
    from concourse.bass_utils import run_bass_kernel_spmd as _run

    nc = _bacc.Bacc("TRN2", target_bir_lowering=False, num_devices=1)
    arrays, args = {}, []
    for name in _INS:
        a = _np.ascontiguousarray(inputs[name])
        arrays[f"in_{name}_dram"] = a
        args.append(nc.dram_tensor(f"in_{name}_dram", a.shape, _mybir.dt.from_np(a.dtype), kind="ExternalInput").ap())
    args.append(nc.dram_tensor("out_0_dram", (B, T, D), F32, kind="ExternalOutput").ap())
    flamingo(nc, *args)
    r = _run(nc, [arrays], core_ids=[0])
    return r.results[0]["out_0_dram"]
```
